# Optimizing a Trainium2 kernel written in Bass

```python
import numpy as np
import jax
import jax.numpy as jnp

def _softmax(x, axis=-1):
    return jax.nn.softmax(x, axis=axis)

def _gelu(x):
    return jax.nn.gelu(x, approximate=True)

def _silu(x):
    return jax.nn.silu(x)

def _sigmoid(x):
    return jax.nn.sigmoid(x)

def _layernorm(x, axis=-1, eps=1e-05):
    m = jnp.mean(x, axis=axis, keepdims=True)
    v = jnp.var(x, axis=axis, keepdims=True)
    return (x - m) / jnp.sqrt(v + eps)

def _scatter_add(tgt, idx, src, axis=0):
    return tgt.at[idx].add(src)

def _segment_sum(src, seg, n):
    return jax.ops.segment_sum(src, seg, n)
kernel_name = 'mk_adj_preln_d4_adj_r2_106a88'

def setup_inputs(seed: int=0):
    np.random.seed(seed)
    _w = jnp.asarray

    def _rec_inputs():
        import jax
        import jax.numpy as jnp
        _gk = jax.random.key(seed)
        x = -0.0005207 + 1.001 * jax.random.normal(jax.random.fold_in(_gk, 1), (3327, 128), jnp.float32)
        _a = jax.random.bernoulli(jax.random.fold_in(_gk, 2), 0.00120228, (3327, 3327))
        _a = jnp.logical_or(_a, jnp.eye(3327, dtype=bool))
        _af = _a.astype(jnp.float32)
        _af = _af * jax.random.uniform(jax.random.fold_in(_gk, 3), (3327, 3327), jnp.float32, 0.05, 1)
        adj = _af
        return (x, adj)
    x, adj = _rec_inputs()

    def _L0_gnn_setup():
        import jax, jax.numpy as jnp
        import numpy as np
        N = 4096
        F_IN = 128
        F_OUT = 128
        key = jax.random.key(seed)
        k1, k2, k3, k4 = jax.random.split(key, 4)
        x = jax.random.normal(k1, (N, F_IN), dtype=jnp.float32)
        adj = jax.random.uniform(k2, (N, N), dtype=jnp.float32)
        bound = 1.0 / np.sqrt(F_IN)
        W = jax.random.uniform(k3, (F_OUT, F_IN), dtype=jnp.float32, minval=-bound, maxval=bound)
        b = jax.random.uniform(k4, (F_OUT,), dtype=jnp.float32, minval=-bound, maxval=bound)
        return {'x': x, 'adj': adj, 'W': W, 'b': b}
    _L0_gnn_all = _L0_gnn_setup()
    _L0_gnn_in = {k: v for k, v in _L0_gnn_all.items() if k in ('W', 'b')}
    del _L0_gnn_all

    def _L1_gnn_setup():
        import jax, jax.numpy as jnp
        import numpy as np
        N, IN_DIM, OUT_DIM, HEADS = (2048, 128, 128, 4)
        D_K = OUT_DIM // HEADS
        NEG_SLOPE = 0.2
        key = jax.random.key(seed)
        k1, k2, k3, k4, k5 = jax.random.split(key, 5)
        H = jax.random.normal(k1, (N, IN_DIM), dtype=jnp.float32)
        A = jax.random.randint(k2, (N, N), 0, 2).astype(jnp.float32)
        W = jax.random.normal(k3, (OUT_DIM, IN_DIM), dtype=jnp.float32) * (1.0 / np.sqrt(IN_DIM))
        a_l = jax.random.normal(k4, (HEADS, D_K), dtype=jnp.float32) * 0.1
        a_r = jax.random.normal(k5, (HEADS, D_K), dtype=jnp.float32) * 0.1
        return {'H': H, 'A': A, 'W': W, 'a_l': a_l, 'a_r': a_r}
    _L1_gnn_all = _L1_gnn_setup()
    _L1_gnn_in = {k: v for k, v in _L1_gnn_all.items() if k in ('W', 'a_l', 'a_r')}
    del _L1_gnn_all

    def _L2_gnn_setup():
        import jax, jax.numpy as jnp
        import numpy as np
        N, H, HEADS = (2048, 128, 3)
        ALPHA = 0.2
        NEG_INF = -9000000000000000.0

        def _sign_adj(key, n, density):
            k1, k2 = jax.random.split(key)
            mask = jax.random.uniform(k1, (n, n)) < density
            sign = jnp.where(jax.random.uniform(k2, (n, n)) < 0.5, -1.0, 1.0)
            adj = jnp.where(mask, sign, 0.0).astype(jnp.float32)
            idx = jnp.arange(n)
            return adj.at[idx, idx].set(1.0)

        def _gru_cell(x, hstate, Wih, Whh, bih, bhh):
            gi = x @ Wih.T + bih
            gh = hstate @ Whh.T + bhh
            ir, iz, inn = jnp.split(gi, 3, axis=1)
            hr, hz, hn = jnp.split(gh, 3, axis=1)
            r = jax.nn.sigmoid(ir + hr)
            z = jax.nn.sigmoid(iz + hz)
            n = jnp.tanh(inn + r * hn)
            return (1.0 - z) * n + z * hstate

        def _gat_head(h, node_adj, edge_adj, W, a):
            hW = h @ W
            hp = (node_adj > 0).astype(hW.dtype) @ hW
            hm = (node_adj < 0).astype(hW.dtype) @ hW
            e_plus = jax.nn.leaky_relu(jnp.concatenate([hp, hm], axis=1) @ a, ALPHA)[:, 0]
            e_minus = jax.nn.leaky_relu(jnp.concatenate([hm, hp], axis=1) @ a, ALPHA)[:, 0]
            att = jnp.where(edge_adj > 0, e_plus[None, :], NEG_INF)
            att = jnp.where(edge_adj < 0, e_minus[None, :], att)
            att = jax.nn.softmax(att, axis=1)
            return att * edge_adj @ hW
        key = jax.random.key(seed)
        ks = jax.random.split(key, 16)
        std = 0.01
        gain = 1.414
        return {'h': jax.random.normal(ks[0], (N, H), jnp.float32), 'node_adj': _sign_adj(ks[1], N, 0.005), 'edge_adj': _sign_adj(ks[2], N, 0.005), 'gat_W': jax.random.normal(ks[3], (HEADS, H, H), jnp.float32) * (gain / np.sqrt(H, dtype=np.float32)), 'gat_a': jax.random.normal(ks[4], (HEADS, 2 * H, 1), jnp.float32) * 0.1, 'edge_Wih': jax.random.normal(ks[5], (3 * H, H), jnp.float32) * std, 'edge_Whh': jax.random.normal(ks[6], (3 * H, H), jnp.float32) * std, 'edge_bih': jnp.zeros((3 * H,), jnp.float32), 'edge_bhh': jnp.zeros((3 * H,), jnp.float32), 'node_Wih': jax.random.normal(ks[7], (3 * H, H), jnp.float32) * std, 'node_Whh': jax.random.normal(ks[8], (3 * H, H), jnp.float32) * std, 'node_bih': jnp.zeros((3 * H,), jnp.float32), 'node_bhh': jnp.zeros((3 * H,), jnp.float32)}
    _L2_gnn_all = _L2_gnn_setup()
    _L2_gnn_in = {k: v for k, v in _L2_gnn_all.items() if k in ('gat_W', 'gat_a', 'edge_Wih', 'edge_Whh', 'edge_bih', 'edge_bhh', 'node_Wih', 'node_Whh', 'node_bih', 'node_bhh')}
    del _L2_gnn_all

    def _L3_gnn_setup():
        import jax, jax.numpy as jnp
        import numpy as np
        D_IN = 128
        D_ATTN = 64
        STEPS = 2
        TOP_P = 0.9
        TAU = 1.0
        LN_EPS = 1e-05
        N_NODES = 4096

        def _top_p_attention(X, W1, W2, W3):
            q = X @ W1.T @ W2.T
            k = X @ W3.T
            logits = q @ k.T / TAU
            probs = jax.nn.softmax(logits, axis=-1)
            idx = jnp.argsort(-probs, axis=-1)
            sp = jnp.take_along_axis(probs, idx, axis=-1)
            cs = jnp.cumsum(sp, axis=-1)
            keep_sorted = cs - sp < TOP_P
            rows = jnp.arange(probs.shape[0])[:, None]
            mask = jnp.zeros(probs.shape, dtype=bool).at[rows, idx].set(keep_sorted)
            A = probs * mask
            return A / jnp.maximum(A.sum(-1, keepdims=True), 1e-12)
        key = jax.random.key(seed)
        ks = jax.random.split(key, 8)
        N, d, da, steps = (N_NODES, D_IN, D_ATTN, STEPS)
        X = jax.random.normal(ks[0], (N, d), dtype=jnp.float32)
        S = jax.random.uniform(ks[1], (N, N), dtype=jnp.float32)
        W1 = jax.random.normal(ks[2], (da, d), dtype=jnp.float32) / np.sqrt(d)
        W2 = jax.random.normal(ks[3], (da, da), dtype=jnp.float32) / np.sqrt(da)
        W3 = jax.random.normal(ks[4], (da, d), dtype=jnp.float32) / np.sqrt(d)
        U1 = jax.random.normal(ks[5], (steps, d, d), dtype=jnp.float32) / np.sqrt(d)
        U2 = jax.random.normal(ks[6], (steps, d, d), dtype=jnp.float32) / np.sqrt(d)
        ln_g = jnp.ones((d,), dtype=jnp.float32)
        ln_b = jnp.zeros((d,), dtype=jnp.float32)
        return {'X': X, 'S': S, 'W1': W1, 'W2': W2, 'W3': W3, 'U1': U1, 'U2': U2, 'ln_g': ln_g, 'ln_b': ln_b}
    _L3_gnn_all = _L3_gnn_setup()
    _L3_gnn_in = {k: v for k, v in _L3_gnn_all.items() if k in ('W1', 'W2', 'W3', 'U1', 'U2', 'ln_g', 'ln_b')}
    del _L3_gnn_all
    return {'x': x, 'adj': adj, 'L0_gnn_W': _L0_gnn_in['W'], 'L0_gnn_b': _L0_gnn_in['b'], 'L1_gnn_W': _L1_gnn_in['W'], 'L1_gnn_a_l': _L1_gnn_in['a_l'], 'L1_gnn_a_r': _L1_gnn_in['a_r'], 'L2_gnn_gat_W': _L2_gnn_in['gat_W'], 'L2_gnn_gat_a': _L2_gnn_in['gat_a'], 'L2_gnn_edge_Wih': _L2_gnn_in['edge_Wih'], 'L2_gnn_edge_Whh': _L2_gnn_in['edge_Whh'], 'L2_gnn_edge_bih': _L2_gnn_in['edge_bih'], 'L2_gnn_edge_bhh': _L2_gnn_in['edge_bhh'], 'L2_gnn_node_Wih': _L2_gnn_in['node_Wih'], 'L2_gnn_node_Whh': _L2_gnn_in['node_Whh'], 'L2_gnn_node_bih': _L2_gnn_in['node_bih'], 'L2_gnn_node_bhh': _L2_gnn_in['node_bhh'], 'L3_gnn_W1': _L3_gnn_in['W1'], 'L3_gnn_W2': _L3_gnn_in['W2'], 'L3_gnn_W3': _L3_gnn_in['W3'], 'L3_gnn_U1': _L3_gnn_in['U1'], 'L3_gnn_U2': _L3_gnn_in['U2'], 'L3_gnn_ln_g': _L3_gnn_in['ln_g'], 'L3_gnn_ln_b': _L3_gnn_in['ln_b']}

def reference(x, adj, L0_gnn_W, L0_gnn_b, L1_gnn_W, L1_gnn_a_l, L1_gnn_a_r, L2_gnn_gat_W, L2_gnn_gat_a, L2_gnn_edge_Wih, L2_gnn_edge_Whh, L2_gnn_edge_bih, L2_gnn_edge_bhh, L2_gnn_node_Wih, L2_gnn_node_Whh, L2_gnn_node_bih, L2_gnn_node_bhh, L3_gnn_W1, L3_gnn_W2, L3_gnn_W3, L3_gnn_U1, L3_gnn_U2, L3_gnn_ln_g, L3_gnn_ln_b):
    import jax
    import jax.numpy as jnp

    def _L0_gnn_ref(x, adj, W, b):
        import jax, jax.numpy as jnp
        import numpy as np
        N = 4096
        F_IN = 128
        F_OUT = 128
        D = jnp.sum(adj, axis=1)
        d_inv_sqrt = jnp.power(D + 1e-09, -0.5)
        adj_norm = adj * d_inv_sqrt[:, None] * d_inv_sqrt[None, :]
        h = adj_norm @ x
        out = h @ W.T + b
        return jax.nn.relu(out)

    def _L1_gnn_ref(H, A, W, a_l, a_r):
        import jax, jax.numpy as jnp
        import numpy as np
        N, IN_DIM, OUT_DIM, HEADS = (2048, 128, 128, 4)
        D_K = OUT_DIM // HEADS
        NEG_SLOPE = 0.2
        n = H.shape[0]
        A_tilde = A + jnp.eye(n, dtype=A.dtype)
        mask = A_tilde > 0
        Wh = (H @ W.T).reshape(n, HEADS, D_K)
        score_l = jnp.einsum('nhd,hd->nh', Wh, a_l)
        score_r = jnp.einsum('nhd,hd->nh', Wh, a_r)
        e = score_l[:, :, None] + score_r.T[None, :, :]
        e = jnp.where(e >= 0, e, NEG_SLOPE * e)
        e = jnp.where(mask[:, None, :], e, -jnp.inf)
        alpha = jax.nn.softmax(e, axis=2)
        out = jnp.einsum('nhm,mhd->nhd', alpha, Wh).reshape(n, OUT_DIM)
        return jax.nn.elu(out)

    def _L2_gnn_ref(h, node_adj, edge_adj, gat_W, gat_a, edge_Wih, edge_Whh, edge_bih, edge_bhh, node_Wih, node_Whh, node_bih, node_bhh):
        import jax, jax.numpy as jnp
        import numpy as np
        N, H, HEADS = (2048, 128, 3)
        ALPHA = 0.2
        NEG_INF = -9000000000000000.0

        def _sign_adj(key, n, density):
            k1, k2 = jax.random.split(key)
            mask = jax.random.uniform(k1, (n, n)) < density
            sign = jnp.where(jax.random.uniform(k2, (n, n)) < 0.5, -1.0, 1.0)
            adj = jnp.where(mask, sign, 0.0).astype(jnp.float32)
            idx = jnp.arange(n)
            return adj.at[idx, idx].set(1.0)

        def _gru_cell(x, hstate, Wih, Whh, bih, bhh):
            gi = x @ Wih.T + bih
            gh = hstate @ Whh.T + bhh
            ir, iz, inn = jnp.split(gi, 3, axis=1)
            hr, hz, hn = jnp.split(gh, 3, axis=1)
            r = jax.nn.sigmoid(ir + hr)
            z = jax.nn.sigmoid(iz + hz)
            n = jnp.tanh(inn + r * hn)
            return (1.0 - z) * n + z * hstate

        def _gat_head(h, node_adj, edge_adj, W, a):
            hW = h @ W
            hp = (node_adj > 0).astype(hW.dtype) @ hW
            hm = (node_adj < 0).astype(hW.dtype) @ hW
            e_plus = jax.nn.leaky_relu(jnp.concatenate([hp, hm], axis=1) @ a, ALPHA)[:, 0]
            e_minus = jax.nn.leaky_relu(jnp.concatenate([hm, hp], axis=1) @ a, ALPHA)[:, 0]
            att = jnp.where(edge_adj > 0, e_plus[None, :], NEG_INF)
            att = jnp.where(edge_adj < 0, e_minus[None, :], att)
            att = jax.nn.softmax(att, axis=1)
            return att * edge_adj @ hW
        dn = jnp.diag(node_adj)
        de = jnp.diag(edge_adj)
        idx = jnp.arange(node_adj.shape[0])
        node_adj_norm = node_adj.at[idx, idx].add(-dn)
        edge_adj_norm = edge_adj.at[idx, idx].add(-de)
        node_support = node_adj_norm @ h
        edge_output = _gru_cell(node_support, h, edge_Wih, edge_Whh, edge_bih, edge_bhh)
        edge_support = _gat_head(h, node_adj_norm, edge_adj_norm, gat_W[0], gat_a[0])
        for i in range(1, HEADS):
            edge_support = edge_support + _gat_head(h, node_adj_norm, edge_adj_norm, gat_W[i], gat_a[i])
        edge_support = edge_support / HEADS
        node_output = _gru_cell(edge_support, h, node_Wih, node_Whh, node_bih, node_bhh)
        return de[:, None] * edge_output + dn[:, None] * node_output

    def _L3_gnn_ref(X, S, W1, W2, W3, U1, U2, ln_g, ln_b):
        import jax, jax.numpy as jnp
        import numpy as np
        D_IN = 128
        D_ATTN = 64
        STEPS = 2
        TOP_P = 0.9
        TAU = 1.0
        LN_EPS = 1e-05
        N_NODES = 4096

        def _top_p_attention(X, W1, W2, W3):
            q = X @ W1.T @ W2.T
            k = X @ W3.T
            logits = q @ k.T / TAU
            probs = jax.nn.softmax(logits, axis=-1)
            idx = jnp.argsort(-probs, axis=-1)
            sp = jnp.take_along_axis(probs, idx, axis=-1)
            cs = jnp.cumsum(sp, axis=-1)
            keep_sorted = cs - sp < TOP_P
            rows = jnp.arange(probs.shape[0])[:, None]
            mask = jnp.zeros(probs.shape, dtype=bool).at[rows, idx].set(keep_sorted)
            A = probs * mask
            return A / jnp.maximum(A.sum(-1, keepdims=True), 1e-12)
        N = X.shape[0]
        R = S + jnp.eye(N, dtype=X.dtype)
        R = R / R.sum(-1, keepdims=True)
        Z = jnp.zeros_like(X)
        Xf = X
        Xa = X
        for n in range(STEPS):
            A = _top_p_attention(Xa, W1, W2, W3)
            Xf = R @ Xf
            Xa = A @ Xa
            Z = Z + Xf @ U1[n].T + Xa @ U2[n].T
        h = X + Z
        mu = h.mean(-1, keepdims=True)
        var = jnp.mean((h - mu) ** 2, axis=-1, keepdims=True)
        return (h - mu) / jnp.sqrt(var + LN_EPS) * ln_g + ln_b
    h = jnp.maximum(_layernorm(x, axis=-1), 0.0)
    x = x + _L0_gnn_ref(h, adj, L0_gnn_W, L0_gnn_b)
    h = jnp.maximum(_layernorm(x, axis=-1), 0.0)
    x = x + _L1_gnn_ref(h, adj, L1_gnn_W, L1_gnn_a_l, L1_gnn_a_r)
    h = jnp.maximum(_layernorm(x, axis=-1), 0.0)
    x = x + _L2_gnn_ref(h, adj, adj, L2_gnn_gat_W, L2_gnn_gat_a, L2_gnn_edge_Wih, L2_gnn_edge_Whh, L2_gnn_edge_bih, L2_gnn_edge_bhh, L2_gnn_node_Wih, L2_gnn_node_Whh, L2_gnn_node_bih, L2_gnn_node_bhh)
    h = jnp.maximum(_layernorm(x, axis=-1), 0.0)
    x = x + _L3_gnn_ref(h, adj, L3_gnn_W1, L3_gnn_W2, L3_gnn_W3, L3_gnn_U1, L3_gnn_U2, L3_gnn_ln_g, L3_gnn_ln_b)
    return x

_drawn_inputs = setup_inputs


def setup_inputs(seed=0):
    import zlib

    import numpy as np

    out = dict(_drawn_inputs(seed))
    spreads = {'L2_gnn_edge_bih': (0.0, 0.374),
     'L2_gnn_edge_bhh': (0.0, 0.63),
     'L2_gnn_node_bih': (0.0, 0.4),
     'L2_gnn_node_bhh': (0.0, 0.547),
     'L3_gnn_ln_g': (1.0, 0.2),
     'L3_gnn_ln_b': (0.0, 0.1)}
    factors = {'L1_gnn_a_l': 2.961,
     'L2_gnn_gat_W': 8.0,
     'L2_gnn_gat_a': 8.0,
     'L2_gnn_edge_Whh': 5.71,
     'L2_gnn_node_Wih': 8.0,
     'L2_gnn_node_Whh': 6.054}
    for name, (base, spread) in spreads.items():
        noise = np.random.default_rng([zlib.crc32(name.encode()), seed]).standard_normal(out[name].shape)
        drawn = base * np.exp(spread * noise) if base else spread * noise
        out[name] = jnp.asarray(drawn.astype(out[name].dtype))
    for name, factor in factors.items():
        out[name] = (out[name] * factor).astype(out[name].dtype)
    return out
```

```python
import concourse.bass as bass
from concourse import mybir
from contextlib import ExitStack

F32 = mybir.dt.float32
BF16 = mybir.dt.bfloat16
ALU = mybir.AluOpType
ACT = mybir.ActivationFunctionType
X = mybir.AxisListType.X
ADD, SUB, MUL, MAX, MIN = ALU.add, ALU.subtract, ALU.mult, ALU.max, ALU.min
ds = bass.ds

P = 128
NODES = 3327
T = (NODES + P - 1) // P
NP = T * P
BANK = 512
NB = (NP + BANK - 1) // BANK
PER = BANK // P
BANKS = [(b, b * BANK, min(BANK, NP - b * BANK)) for b in range(NB)]
LN_EPS = 1e-5
L1_HEADS, L1_D = 4, 32
L1_SLOPE = 0.2
L2_HEADS = 3
L2_ALPHA = 0.2
CHUNKS = [(0, 6), (6, 6), (12, 6), (18, 8)]
WMAX = max(n for _, n in CHUNKS)
D_ATTN, STEPS, TOP_P = 64, 2, 0.9
SEARCH_SPAN = 10.42
SEARCH_ROUNDS = 21


class Chain:

    def __init__(self, engine, sem):
        self.engine, self.sem, self.base, self.k, self.i, self.per = engine, sem, 0, 0, None, 0

    def __call__(self, ins):
        self.k += 1
        ins.then_inc(self.sem, 1)
        at = self.base + self.k
        if self.i is not None:
            at = at + self.i * self.per
        self.engine.wait_ge(self.sem, at)
        return ins

    def enter(self, i, per):
        assert self.i is None
        self.base, self.k, self.i, self.per = self.base + self.k, 0, i, per

    def leave(self, rounds):
        assert self.k == self.per, (self.k, self.per)
        self.base, self.k, self.i = self.base + rounds * self.per, 0, None


def tiles(ap):
    return ap.rearrange("p (t c) -> p t c", t=T)


class Kernel:

    def __init__(self, nc, ctx, d, out):
        self.nc, self.ctx, self.d, self.out = nc, ctx, d, out
        self.names = {}
        self.counted = []
        sb = self.sb
        self.ps = ctx.enter_context(nc.psum_tensor("psum", [P, 8, BANK], F32))
        self.psf = self.ps[:, :, :].rearrange("p b c -> p (b c)")
        self.x = sb("x", [P, T, P])
        self.h = sb("h", [P, T, P])
        self.hT = sb("hT", [P, NP])
        self.ident = sb("ident", [P, P])
        self.deg = sb("deg", [P, T])
        self.diag = sb("diag", [P, T])
        self.s1 = sb("s1", [P, T])
        self.s2 = sb("s2", [P, T])
        self.s3 = sb("s3", [P, T])
        self.s4 = sb("s4", [P, T])

    def sb(self, name, shape, dt=F32, ctx=None):
        return (ctx or self.ctx).enter_context(self.nc.sbuf_tensor(name, shape, dt))

    def sem(self, name, ctx):
        n = self.names[name] = self.names.get(name, 0) + 1
        handle = ctx.enter_context(self.nc.semaphore(f"{name}_{n}"))
        self.counted.append(handle)
        return handle


def clear_semaphores(k):
    with k.nc.Block() as block:
        @block.gpsimd
        def _(pool):
            for handle in k.counted:
                pool.sem_clear(handle)
    k.counted = []


def bcast(ap, n):
    return ap.unsqueeze(2).to_broadcast([ap.shape[0], ap.shape[1], n])


def layer_norm(k, who, source=None, affine=None):
    nc, ctx = k.nc, ExitStack()
    source = k.x if source is None else source
    with ctx:
        xc = k.sb(f"ln_centred_{who}", [P, T, P], ctx=ctx)
        sq = k.sb(f"ln_squares_{who}", [P, T, P], ctx=ctx)
        centred, squared, var_ready, root_ready, h_ready = (
            k.sem(n, ctx) for n in ("ln_centred", "ln_squared", "ln_var", "ln_root", "ln_h"))
        turned, taken_dve, taken_act = (k.sem(n, ctx) for n in ("ln_turned", "ln_taken_dve", "ln_taken_act"))
        own, own_act = k.sem("ln_dve", ctx), k.sem("ln_act", ctx)
        block = ctx.enter_context(nc.Block())

        @block.vector
        def _(dve):
            link = Chain(dve, own)
            link(nc.vector.reduce_sum(k.s1[:, :], source[:, :, :], X))
            link(nc.vector.tensor_scalar(k.s1[:, :], k.s1[:, :], 1.0 / P, None, MUL))
            nc.vector.tensor_tensor(xc[:, :, :], source[:, :, :], bcast(k.s1[:, :], P), SUB).then_inc(centred, 1)
            dve.wait_ge(squared, 1)
            link(nc.vector.reduce_sum(k.s2[:, :], sq[:, :, :], X))
            nc.vector.tensor_scalar(k.s2[:, :], k.s2[:, :], 1.0 / P, LN_EPS, MUL, ADD).then_inc(var_ready, 1)
            dve.wait_ge(var_ready, 1)
            dve.wait_ge(root_ready, 1)
            link(nc.vector.reciprocal(k.s4[:, :], k.s3[:, :]))
            link(nc.vector.tensor_tensor(k.s4[:, :], k.s4[:, :], k.s2[:, :], MUL))
            link(nc.vector.tensor_tensor(k.s4[:, :], k.s4[:, :], k.s3[:, :], ADD))
            link(nc.vector.tensor_scalar(k.s4[:, :], k.s4[:, :], 0.5, None, MUL))
            link(nc.vector.reciprocal(k.s4[:, :], k.s4[:, :]))
            if affine:
                gain, shift = (v[:, :].unsqueeze(1).to_broadcast([P, T, P]) for v in affine)
                link(nc.vector.tensor_tensor(xc[:, :, :], xc[:, :, :], bcast(k.s4[:, :], P), MUL))
                link(nc.vector.tensor_tensor(xc[:, :, :], xc[:, :, :], gain, MUL))
                link(nc.vector.tensor_tensor(xc[:, :, :], xc[:, :, :], shift, ADD))
                link(nc.vector.tensor_tensor(k.x[:, :, :], k.x[:, :, :], xc[:, :, :], ADD))
                return
            nc.vector.scalar_tensor_tensor(k.h[:, :, :], xc[:, :, :], 0.0, bcast(k.s4[:, :], P),
                                           MAX, MUL).then_inc(h_ready, 1)
            for b, c, w in BANKS[0::2]:
                dve.wait_ge(turned, b + 1)
                last = nc.vector.tensor_copy(k.hT[:, c:c + w], k.psf[:, c:c + w])
            last.then_inc(taken_dve, 1)

        @block.scalar
        def _(act):
            act.wait_ge(centred, 1)
            nc.scalar.activation(sq[:, :, :], xc[:, :, :], ACT.Square).then_inc(squared, 1)
            act.wait_ge(var_ready, 1)
            nc.scalar.activation(k.s3[:, :], k.s2[:, :], ACT.Sqrt).then_inc(root_ready, 1)
            if affine:
                return
            for b, c, w in BANKS[1::2]:
                act.wait_ge(turned, b + 1)
                last = nc.scalar.copy(k.hT[:, c:c + w], k.psf[:, c:c + w])
            last.then_inc(taken_act, 1)

        @block.tensor
        def _(pe):
            if affine:
                return
            pe.wait_ge(h_ready, 1)
            for b, c, w in BANKS:
                for t in range(c // P, (c + w) // P):
                    last = nc.tensor.transpose(k.psf[:, t * P:(t + 1) * P], k.h[:, t, :], k.ident[:, :])
                last.then_inc(turned, 1)


def propagate(k, source, who, ring=3, self_loops=False):
    nc, ctx = k.nc, ExitStack()
    first = 2
    assert (T - first) % ring == 0
    rounds = (T - first) // ring
    with ctx:
        a = k.sb(f"pr_adj_{who}", [P, ring, NP], ctx=ctx)
        v = k.sb(f"pr_source_{who}", [P, ring, P], ctx=ctx)
        loaded = [k.sem(f"pr_loaded{u}", ctx) for u in range(ring)]
        picked, used = k.sem("pr_picked", ctx), k.sem("pr_used", ctx)
        block = ctx.enter_context(nc.Block())

        def steps(engine, body):
            for j in range(first):
                body(j, j % ring, 0)
            with engine.Fori(0, rounds) as r:
                for u in range(ring):
                    slot = (first + u) % ring
                    body(r * ring + (first + u), slot, r + (first + u) // ring)

        @block.sync
        def _(sp):
            def load(j, slot, before):
                if not isinstance(j, int) or j >= ring:
                    sp.wait_ge(used, j - (ring - 1))
                sp.dma_start(a[:, slot, :], k.d["adjT"][ds(j * P, P), :]).then_inc(loaded[slot], 16)
            for j in range(ring):
                load(j, j, 0)
            with sp.Fori(0, rounds - 1) as r:
                for u in range(ring):
                    load(r * ring + (ring + u), u, r + 1)
            for j in range(ring * rounds, T):
                load(j, j % ring, 0)

        @block.gpsimd
        def _(pool):
            def pick(j, slot, before):
                if not isinstance(j, int) or j >= ring:
                    pool.wait_ge(used, j - (ring - 1))
                nc.gpsimd.tensor_copy(v[:, slot, :], source[:, ds(j, 1), :].rearrange("p o c -> p (o c)")).then_inc(picked, 1)
            for j in range(ring):
                pick(j, j, 0)
            with pool.Fori(0, rounds - 1) as r:
                for u in range(ring):
                    pick(r * ring + (ring + u), u, r + 1)
            for j in range(ring * rounds, T):
                pick(j, j % ring, 0)

        @block.tensor
        def _(pe):
            def tile(j, slot, before):
                pe.wait_ge(loaded[slot], (before + 1) * 16)
                pe.wait_ge(picked, j + 1)
                for b, c, w in BANKS:
                    last = nc.tensor.matmul(k.psf[:, c:c + w], v[:, slot, :], a[:, slot, c:c + w],
                                            start=isinstance(j, int) and j == 0, stop=False,
                                            skip_group_check=True)
                if self_loops:
                    last = nc.tensor.matmul(k.psf[:, ds(j * P, P)], v[:, slot, :], k.ident[:, :],
                                            start=False, stop=False, skip_group_check=True)
                last.then_inc(used, 1)
            steps(pe, tile)


def load_constants(k, c):
    nc, ctx = k.nc, ExitStack()
    ring = 4
    with ctx:
        a = k.sb("degree_rows", [P, ring, NP], ctx=ctx)
        arrived = k.sem("constants_arrived", ctx)
        loaded = [k.sem(f"rows_loaded{u}", ctx) for u in range(ring)]
        zeroed, ident_ready, blocks_zero, summed, own = (
            k.sem(n, ctx) for n in ("ident_zeroed", "ident_ready", "blocks_zero", "summed", "deg_dve"))
        block = ctx.enter_context(nc.Block())
        d = k.d
        first, rest = T % ring, T // ring

        @block.scalar
        def _(act):
            pairs = [(k.x[:, :, :], d["x"]), (k.diag[:, :], d["diag"])]
            pairs += [(c[n][:], d[n]) for n in ("w0T", "w1", "w1T", "gat_w", "gat_wT", "gat_a", "ewihT", "ewhhT",
                                               "nwihT", "nwhhT", "l3w1T", "l3w2T", "l3w3T", "u1T", "u2T")]
            pairs += [(c[n][:], d[n].to_broadcast([P, d[n].shape[1]])) for n in
                      ("b0", "ebih", "ebhh", "nbih", "nbhh", "ln_g", "ln_b")]
            for dst, src in pairs:
                act.dma_start(dst, src).then_inc(arrived, 16)
            act.wait_ge(blocks_zero, 1)
            for s, name in enumerate(("a_l", "a_r")):
                for h in range(L1_HEADS):
                    at = slice(h * L1_D, (h + 1) * L1_D)
                    act.dma_start(c["a_blocks"][at, s * L1_HEADS + h:s * L1_HEADS + h + 1],
                                  d[name][at, :]).then_inc(arrived, 16)
            act.wait_ge(arrived, 16 * (len(pairs) + 2 * L1_HEADS))

        @block.gpsimd
        def _(pool):
            nc.gpsimd.memset(c["a_blocks"][:], 0.0).then_inc(blocks_zero, 1)
            nc.gpsimd.memset(k.ident[:], 0.0).then_inc(zeroed, 1)
            pool.wait_ge(zeroed, 1)
            nc.gpsimd.affine_select(out=k.ident[:], in_=k.ident[:], compare_op=ALU.not_equal, fill=1.0,
                                    base=0, pattern=[[-1, P]], channel_multiplier=1).then_inc(ident_ready, 1)
            pool.wait_ge(ident_ready, 1)

        @block.sync
        def _(sp):
            for u in range(ring):
                sp.dma_start(a[:, u, :], d["adj"][u * P:(u + 1) * P, :]).then_inc(loaded[u], 16)
            with sp.Fori(1, rest) as r:
                for u in range(ring):
                    sp.wait_ge(summed, r * ring + (u - ring + 1))
                    sp.dma_start(a[:, u, :], d["adj"][ds((r * ring + u) * P, P), :]).then_inc(loaded[u], 16)
            for t in range(rest * ring, T):
                sp.wait_ge(summed, t - ring + 1)
                sp.dma_start(a[:, t % ring, :], d["adj"][t * P:(t + 1) * P, :]).then_inc(loaded[t % ring], 16)

        @block.vector
        def _(dve):
            def add_up(t, u, turn):
                dve.wait_ge(loaded[u], (turn + 1) * 16)
                nc.vector.reduce_sum(k.deg[:, ds(t, 1)], a[:, u, :], X).then_inc(summed, 1)
            with dve.Fori(0, rest) as r:
                for u in range(ring):
                    add_up(r * ring + u, u, r)
            for t in range(rest * ring, T):
                add_up(t, t % ring, t // ring)


def layer0(k, c):
    nc, ctx = k.nc, ExitStack()
    with ctx:
        y = k.sb("l0_source", [P, T, P], ctx=ctx)
        dinv = k.sb("dinv", [P, T], ctx=ctx)
        with ExitStack() as inner:
            dp, root, own = (k.sem(n, inner) for n in ("l0_deg", "l0_root", "l0_own"))
            block = inner.enter_context(nc.Block())

            @block.vector
            def _(dve):
                link = Chain(dve, own)
                nc.vector.tensor_scalar(k.s1[:, :], k.deg[:, :], 1e-9, None, ADD).then_inc(dp, 1)
                dve.wait_ge(dp, 1)
                dve.wait_ge(root, 1)
                link(nc.vector.reciprocal(k.s3[:, :], k.s2[:, :]))
                link(nc.vector.tensor_tensor(k.s3[:, :], k.s3[:, :], k.s1[:, :], MUL))
                link(nc.vector.tensor_tensor(k.s3[:, :], k.s3[:, :], k.s2[:, :], ADD))
                link(nc.vector.tensor_scalar(k.s3[:, :], k.s3[:, :], 0.5, None, MUL))
                link(nc.vector.reciprocal(dinv[:, :], k.s3[:, :]))
                link(nc.vector.tensor_tensor(y[:, :, :], k.h[:, :, :], bcast(dinv[:, :], P), MUL))

            @block.scalar
            def _(act):
                act.wait_ge(dp, 1)
                nc.scalar.activation(k.s2[:, :], k.s1[:, :], ACT.Sqrt).then_inc(root, 1)
        propagate(k, y, "l0")
        agg = k.sb("l0_agg", [P, NP], ctx=ctx)
        z = k.sb("l0_z", [P, T, P], ctx=ctx)
        with ExitStack() as inner:
            taken_dve, taken_act, made, own = (k.sem(n, inner) for n in ("l0_td", "l0_ta", "l0_made", "l0_dve"))
            block = inner.enter_context(nc.Block())

            @block.scalar
            def _(act):
                for b, col, w in BANKS[1::2]:
                    nc.scalar.copy(agg[:, col:col + w], k.psf[:, col:col + w]).then_inc(taken_act, 1)

            @block.tensor
            def _(pe):
                pe.wait_ge(taken_dve, len(BANKS[0::2]))
                pe.wait_ge(taken_act, len(BANKS[1::2]))
                for b, col, w in BANKS:
                    for t in range(col // P, (col + w) // P):
                        last = nc.tensor.matmul(k.psf[:, t * P:(t + 1) * P], agg[:, t * P:(t + 1) * P],
                                                c["w0T"][:, :], start=True, stop=True)
                    last.then_inc(made, 1)

            @block.vector
            def _(dve):
                link = Chain(dve, own)
                for b, col, w in BANKS[0::2]:
                    nc.vector.tensor_copy(agg[:, col:col + w], k.psf[:, col:col + w]).then_inc(taken_dve, 1)
                for b, col, w in BANKS:
                    dve.wait_ge(made, b + 1)
                    for t in range(col // P, (col + w) // P):
                        ins = nc.vector.scalar_tensor_tensor(z[:, t, :], k.psf[:, t * P:(t + 1) * P],
                                                             dinv[:, t:t + 1], c["b0"][:, :], MUL, ADD)
                        if t == T - 1:
                            link(ins)
                link(nc.vector.scalar_tensor_tensor(k.x[:, :, :], z[:, :, :], 0.0, k.x[:, :, :], MAX, ADD))


def diagonal_block(engine, j, i0, n, spare):
    inside = (j >= i0) * (j < i0 + n) if i0 else (j < n)
    return engine.snap((inside * (j - i0) + (1 - inside) * spare) * P).with_bounds(min_val=0, max_val=spare * P)


def split_bf16(link, nc, parts, rest):
    for n, part in enumerate(parts):
        link(nc.vector.tensor_copy(part, rest))
        if n < 2:
            link(nc.vector.tensor_tensor(rest, rest, part, SUB))


def layer1(k, c):
    nc, ctx = k.nc, ExitStack()
    H, D = L1_HEADS, L1_D
    GC, MC = 2 * (D + 1), D + 1
    VC = H * (GC + MC)
    with ctx:
        v = k.sb("l1_v", [P, T, 3, VC], BF16, ctx=ctx)
        neg_r = k.sb("l1_neg_r", [P, T * H], ctx=ctx)
        a_n = k.sb("l1_a", [P, T, H], ctx=ctx)
        c_n = k.sb("l1_c", [P, T, H], ctx=ctx)
        ub = k.sb("l1_ub", [P, H, P], ctx=ctx)
        with ExitStack() as inner:
            vf = k.sb("l1_vf", [P, T, VC], ctx=inner)
            wh = k.sb("l1_wh", [P, T, P], ctx=inner)
            sc = k.sb("l1_scores", [P, T, 2 * H], ctx=inner)
            u8 = k.sb("l1_u8", [P, 2 * H], ctx=inner)
            rmax = k.sb("l1_rmax", [P, H], ctx=inner)
            rall = k.sb("l1_rall", [P, H], ctx=inner)
            rs = k.sb("l1_rs", [P, T, H], ctx=inner)
            bt = k.sb("l1_bt", [P, T, H], ctx=inner)
            dt = k.sb("l1_dt", [P, T, H], ctx=inner)
            names = ("u_made", "u_taken", "wh_made", "rmax_ready", "rall_ready", "shifted", "tabled",
                     "wh_act", "own")
            u_made, u_taken, wh_made, rmax_ready, rall_ready, shifted, tabled, wh_act, own = (
                k.sem("l1_" + n, inner) for n in names)
            block = inner.enter_context(nc.Block())

            @block.tensor
            def _(pe):
                nc.tensor.matmul(k.ps[:, 7, 0:2 * H], c["w1"][:, :], c["a_blocks"][:, :], start=True,
                                 stop=True).then_inc(u_made, 1)
                for b, col, w in BANKS:
                    for t in range(col // P, (col + w) // P):
                        last = nc.tensor.matmul(k.psf[:, t * P:(t + 1) * P], k.hT[:, t * P:(t + 1) * P],
                                                c["w1T"][:, :], start=True, stop=True)
                    last.then_inc(wh_made, 1)
                pe.wait_ge(u_taken, 1)
                for t in range(T):
                    last = nc.tensor.matmul(k.ps[:, 7, t * 2 * H:(t + 1) * 2 * H], k.hT[:, t * P:(t + 1) * P],
                                            u8[:, :], start=True, stop=True)
                last.then_inc(wh_made, 1)

            @block.scalar
            def _(act):
                for b, col, w in BANKS[1::2]:
                    act.wait_ge(wh_made, b + 1)
                    last = nc.scalar.copy(wh[:, :, :].rearrange("p t c -> p (t c)")[:, col:col + w],
                                          k.psf[:, col:col + w])
                last.then_inc(wh_act, 1)
                act.wait_ge(shifted, 1)
                nc.scalar.activation(bt[:, :, :], rs[:, :, :], ACT.Exp)
                nc.scalar.activation(dt[:, :, :], rs[:, :, :], ACT.Exp, scale=L1_SLOPE).then_inc(tabled, 1)
                act.wait_ge(shifted, 2)
                nc.scalar.activation(a_n[:, :, :], a_n[:, :, :], ACT.Exp)
                nc.scalar.activation(c_n[:, :, :], c_n[:, :, :], ACT.Exp).then_inc(tabled, 1)
                act.wait_ge(tabled, 2)

            @block.gpsimd
            def _(pool):
                pool.wait_ge(rmax_ready, 1)
                nc.gpsimd.partition_all_reduce(rall[:, :], rmax[:, :], P, bass.bass_isa.ReduceOp.max).then_inc(rall_ready, 1)
                pool.wait_ge(rall_ready, 1)

            @block.vector
            def _(dve):
                link = Chain(dve, own)
                dve.wait_ge(u_made, 1)
                nc.vector.tensor_copy(u8[:, :], k.ps[:, 7, 0:2 * H]).then_inc(u_taken, 1)
                dve.wait_ge(u_taken, 1)
                link(nc.vector.tensor_copy(ub[:, :, :], bcast(u8[:, 0:H], P)))
                for b, col, w in BANKS[0::2]:
                    dve.wait_ge(wh_made, b + 1)
                    nc.vector.tensor_copy(wh[:, :, :].rearrange("p t c -> p (t c)")[:, col:col + w],
                                          k.psf[:, col:col + w])
                dve.wait_ge(wh_made, NB + 1)
                link(nc.vector.tensor_copy(sc[:, :, :], k.ps[:, 7, 0:T * 2 * H].rearrange("p (t e) -> p t e", t=T)))
                nc.vector.reduce_max(rmax[:, :], sc[:, :, H:2 * H].rearrange("p t e -> p e t"), X).then_inc(rmax_ready, 1)
                link(nc.vector.tensor_scalar(neg_r[:, :].rearrange("p (t e) -> p t e", t=T), sc[:, :, H:2 * H],
                                             -1.0, None, MUL))
                dve.wait_ge(rall_ready, 1)
                top = rall[:, :].unsqueeze(1).to_broadcast([P, T, H])
                nc.vector.tensor_tensor(rs[:, :, :], sc[:, :, H:2 * H], top, SUB).then_inc(shifted, 1)
                link(nc.vector.tensor_tensor(sc[:, :, 0:H], sc[:, :, 0:H], top, ADD))
                link(nc.vector.tensor_scalar(a_n[:, :, :], sc[:, :, 0:H], 1 - L1_SLOPE, 0.0, MUL, MIN))
                nc.vector.tensor_scalar(c_n[:, :, :], sc[:, :, 0:H], L1_SLOPE - 1, 0.0, MUL, MIN).then_inc(shifted, 1)
                dve.wait_ge(tabled, 1)
                dve.wait_ge(wh_act, 1)
                wh4 = wh[:, :, :].rearrange("p t (h d) -> p t h d", h=H)
                vg = vf[:, :, 0:H * GC].rearrange("p t (h d) -> p t h d", h=H)
                vm = vf[:, :, H * GC:VC].rearrange("p t (h d) -> p t h d", h=H)
                wide = lambda ap, n: ap.unsqueeze(3).to_broadcast([P, T, H, n])
                nc.vector.tensor_tensor(vg[:, :, :, 0:D], wh4, wide(bt[:, :, :], D), MUL)
                nc.vector.tensor_copy(vg[:, :, :, D:D + 1], wide(bt[:, :, :], 1))
                nc.vector.tensor_tensor(vm[:, :, :, 0:D], wh4, wide(dt[:, :, :], D), MUL)
                link(nc.vector.tensor_copy(vm[:, :, :, D:MC], wide(dt[:, :, :], 1)))
                link(nc.vector.tensor_scalar(vg[:, :, :, D + 1:GC], vm, -1.0, None, MUL))
                split_bf16(link, nc, [v[:, :, n, :] for n in range(3)], vf[:, :, :])

        lb = k.sb("l1_lb", [P, H, NP], ctx=ctx)
        with ExitStack() as inner:
            made, taken = k.sem("l1_lb_made", inner), k.sem("l1_lb_taken", inner)
            taken_dve = k.sem("l1_lb_taken_dve", inner)
            block = inner.enter_context(nc.Block())

            @block.tensor
            def _(pe):
                for h in range(H):
                    for b, col, w in BANKS:
                        if h:
                            pe.wait_ge(*((taken_dve, (h - 1) * 4 + b // 2 + 1) if b % 2 == 0 else
                                         (taken, (h - 1) * 3 + b // 2 + 1)))
                        nc.tensor.matmul(k.psf[:, col:col + w], ub[:, h, :], k.hT[:, col:col + w], start=True,
                                         stop=True).then_inc(made, 1)

            @block.scalar
            def _(act):
                for h in range(H):
                    for b, col, w in BANKS[1::2]:
                        act.wait_ge(made, h * NB + b + 1)
                        nc.scalar.copy(lb[:, h, col:col + w], k.psf[:, col:col + w]).then_inc(taken, 1)

            @block.vector
            def _(dve):
                for h in range(H):
                    for b, col, w in BANKS[0::2]:
                        dve.wait_ge(made, h * NB + b + 1)
                        nc.vector.tensor_copy(lb[:, h, col:col + w], k.psf[:, col:col + w]).then_inc(taken_dve, 1)

        ring = 2
        assert T % ring == 0
        a = k.sb("l1_adj", [P, ring, (WMAX + 1) * P], ctx=ctx)
        mask = k.sb("l1_mask", [P, ring, WMAX * P], BF16, ctx=ctx)
        g = k.sb("l1_g", [P, ring, H, WMAX * P], BF16, ctx=ctx)
        zeros = k.sb("l1_zeros", [P, P], BF16, ctx=ctx)
        e = k.h[:, :, :].rearrange("p t c -> p (t c)")[:, 0:WMAX * VC].rearrange("p (i c) -> p i c", i=WMAX)
        t1, t2 = (k.hT[:, n * WMAX * H * MC:(n + 1) * WMAX * H * MC].rearrange("p (i h d) -> p i h d", i=WMAX, h=H)
                  for n in range(2))
        loaded = [k.sem(f"l1_loaded{u}", ctx) for u in range(ring)]
        freed, g_ready, g_free, taken, sums_used, mins, exps, own, init = (
            k.sem("l1_" + n, ctx) for n in ("freed", "g_ready", "g_free", "taken", "sums_used", "mins", "exps",
                                            "dve", "zeros"))
        block = ctx.enter_context(nc.Block())

        @block.sync
        def _(sp):
            for ic, (i0, n) in enumerate(CHUNKS):
                def load(j, u, g0):
                    if ic or not isinstance(j, int):
                        sp.wait_ge(freed, j + (ic * T - ring + 1))
                    sp.dma_start(a[:, u, 0:n * P], k.d["adjT"][ds(j * P, P), i0 * P:(i0 + n) * P]
                                 ).then_inc(loaded[u], 16)
                for u in range(ring):
                    load(u, u, 0)
                with sp.Fori(1, T // ring) as r:
                    for u in range(ring):
                        load(r * ring + u, u, 0)

        @block.vector
        def _(dve):
            link = Chain(dve, own)
            link(nc.vector.memset(a[:, :, WMAX * P:(WMAX + 1) * P], 0.0))
            nc.vector.memset(zeros[:, :], 0.0).then_inc(init, 1)
            for ic, (i0, n) in enumerate(CHUNKS):
                w = n * P
                with dve.Fori(0, T // ring) as r:
                    link.enter(r, ring)
                    for u in range(ring):
                        j = r * ring + u
                        dve.wait_ge(loaded[u], (r + (ic * (T // ring) + 1)) * 16)
                        own_block = a[:, u, ds(diagonal_block(dve, j, i0, n, WMAX), P)]
                        link(nc.vector.tensor_tensor(own_block, own_block, k.ident[:, :], ADD))
                        dve.wait_ge(g_free, j + (ic * T + 1))
                        nc.vector.tensor_scalar(mask[:, u, 0:w], a[:, u, 0:w], 0.0, None,
                                                ALU.is_gt).then_inc(freed, 1)
                        dve.wait_ge(freed, j + (ic * T + 1))
                        for h in range(H):
                            last = nc.vector.scalar_tensor_tensor(
                                g[:, u, h, 0:w], lb[:, h, i0 * P:i0 * P + w],
                                neg_r[:, ds(j * H + h, 1)], mask[:, u, 0:w], ALU.is_gt, MUL)
                        last.then_inc(g_ready, 1)
                link.leave(T // ring)
                dve.wait_ge(taken, ic + 1)
                eg = e[:, 0:n, 0:H * GC].rearrange("p i (h d) -> p i h d", h=H)
                em = e[:, 0:n, H * GC:VC].rearrange("p i (h d) -> p i h d", h=H)
                u1, u2 = t1[:, 0:n], t2[:, 0:n]
                wide = lambda ap, m: ap[:, i0:i0 + n, :].unsqueeze(3).to_broadcast([P, n, H, m])
                link(nc.vector.tensor_tensor(u1, eg[:, :, :, MC:GC], em, ADD))
                link(nc.vector.tensor_tensor(u1, u1, wide(c_n[:, :, :], MC), MUL))
                link(nc.vector.tensor_tensor(u2, eg[:, :, :, 0:MC], wide(a_n[:, :, :], MC), MUL))
                link(nc.vector.tensor_tensor(u1, u1, u2, ADD))
                link(nc.vector.reciprocal(u2[:, :, :, D:MC], u1[:, :, :, D:MC]))
                link(nc.vector.tensor_tensor(u1[:, :, :, 0:D], u1[:, :, :, 0:D],
                                             u2[:, :, :, D:MC].to_broadcast([P, n, H, D]), MUL))
                nc.vector.tensor_scalar(u2[:, :, :, 0:D], u1[:, :, :, 0:D], 0.0, None, MIN).then_inc(mins, 1)
                dve.wait_ge(exps, ic + 1)
                link(nc.vector.tensor_scalar(u1[:, :, :, 0:D], u1[:, :, :, 0:D], 0.0, -1.0, MAX, ADD))
                link(nc.vector.tensor_tensor(u1[:, :, :, 0:D], u1[:, :, :, 0:D], u2[:, :, :, 0:D], ADD))
                xs = k.x[:, i0:i0 + n, :].rearrange("p i (h d) -> p i h d", h=H)
                nc.vector.tensor_tensor(xs, xs, u1[:, :, :, 0:D], ADD).then_inc(sums_used, 1)

        @block.scalar
        def _(act):
            for ic, (i0, n) in enumerate(CHUNKS):
                act.wait_ge(g_free, (ic + 1) * T + ring)
                if ic:
                    act.wait_ge(sums_used, ic)
                for i in range(n):
                    last = nc.scalar.copy(e[:, i, :], k.ps[:, i, 0:VC])
                last.then_inc(taken, 1)
                act.wait_ge(mins, ic + 1)
                nc.scalar.activation(t2[:, 0:n, :, 0:D], t2[:, 0:n, :, 0:D], ACT.Exp).then_inc(exps, 1)

        @block.tensor
        def _(pe):
            pe.wait_ge(init, 1)
            for ic, (i0, n) in enumerate(CHUNKS):
                if ic:
                    pe.wait_ge(taken, ic)
                for i in range(n):
                    ins = nc.tensor.matmul(k.ps[:, i, 0:VC], zeros[:, :], v[:, 0, 0, :], start=True,
                                           stop=False, skip_group_check=True)
                    if ic == 0 and i < ring:
                        ins.then_inc(g_free, 1)
                with pe.Fori(0, T // ring) as r:
                    for u in range(ring):
                        j = r * ring + u
                        pe.wait_ge(g_ready, j + (ic * T + 1))
                        for i in range(n):
                            at = slice(i * P, (i + 1) * P)
                            for m in range(H + 1):
                                cols = slice(m * GC, (m + 1) * GC) if m < H else slice(H * GC, VC)
                                for s in range(3):
                                    last = nc.tensor.matmul(
                                        k.ps[:, i, cols], g[:, u, m, at] if m < H else mask[:, u, at],
                                        v[:, ds(j, 1), s, cols].rearrange("p o c -> p (o c)"),
                                        start=False, stop=False, skip_group_check=True)
                        last.then_inc(g_free, 1)


def halves(i0, n):
    w = n * P // 2
    return [(0, i0 * P, w), (w, i0 * P + w, w)]


def to_features(k, source, dest, who):
    nc = k.nc
    with ExitStack() as ctx:
        turned, taken_dve, taken_act = (k.sem(f"tf_{n}", ctx) for n in ("turned", "taken_dve", "taken_act"))
        block = ctx.enter_context(nc.Block())

        @block.tensor
        def _(pe):
            for b, c, w in BANKS:
                for t in range(c // P, (c + w) // P):
                    last = nc.tensor.transpose(k.psf[:, t * P:(t + 1) * P], source[:, t, :], k.ident[:, :])
                last.then_inc(turned, 1)

        @block.vector
        def _(dve):
            for b, c, w in BANKS[0::2]:
                dve.wait_ge(turned, b + 1)
                nc.vector.tensor_copy(dest[:, c:c + w], k.psf[:, c:c + w]).then_inc(taken_dve, 1)

        @block.scalar
        def _(act):
            for b, c, w in BANKS[1::2]:
                act.wait_ge(turned, b + 1)
                nc.scalar.copy(dest[:, c:c + w], k.psf[:, c:c + w]).then_inc(taken_act, 1)


def spread_rows(k, columns, dest, who):
    nc = k.nc
    heads = dest.shape[1]
    with ExitStack() as ctx:
        made, taken_dve, taken_act = (k.sem(f"sr_{n}", ctx) for n in ("made", "taken_dve", "taken_act"))
        block = ctx.enter_context(nc.Block())

        @block.tensor
        def _(pe):
            for h in range(heads):
                for b, c, w in BANKS:
                    if h and b % 2 == 0:
                        pe.wait_ge(taken_dve, (h - 1) * len(BANKS[0::2]) + b // 2 + 1)
                    elif h:
                        pe.wait_ge(taken_act, (h - 1) * len(BANKS[1::2]) + b // 2 + 1)
                    for t in range(c // P, (c + w) // P):
                        last = nc.tensor.matmul(k.psf[:, t * P:(t + 1) * P], columns(t, h).to_broadcast([P, P]),
                                                k.ident[:, :], start=True, stop=True)
                    last.then_inc(made, 1)

        @block.vector
        def _(dve):
            for h in range(heads):
                for b, c, w in BANKS[0::2]:
                    dve.wait_ge(made, h * NB + b + 1)
                    nc.vector.tensor_copy(dest[:, h, c:c + w], k.psf[:, c:c + w]).then_inc(taken_dve, 1)

        @block.scalar
        def _(act):
            for h in range(heads):
                for b, c, w in BANKS[1::2]:
                    act.wait_ge(made, h * NB + b + 1)
                    nc.scalar.copy(dest[:, h, c:c + w], k.psf[:, c:c + w]).then_inc(taken_act, 1)


def signed_sums(k, hs, not_ident, nsT, spT, smT):
    nc, ctx = k.nc, ExitStack()
    ring = 2
    with ctx:
        a = k.sb("ss_adj", [P, ring, (WMAX + 1) * P], ctx=ctx)
        pos = k.sb("ss_pos", [P, ring, WMAX * P], BF16, ctx=ctx)
        neg = k.sb("ss_neg", [P, ring, WMAX * P], BF16, ctx=ctx)
        hv = k.sb("ss_h", [P, ring, P], ctx=ctx)
        zeros = k.sb("ss_zeros", [P, BANK], BF16, ctx=ctx)
        loaded = [k.sem(f"ss_loaded{u}", ctx) for u in range(ring)]
        ready, free, picked, taken_act, taken_dve, init, own = (
            k.sem("ss_" + n, ctx) for n in ("ready", "free", "picked", "taken_act", "taken_dve", "zeros", "dve"))
        block = ctx.enter_context(nc.Block())
        R = T // ring

        @block.sync
        def _(sp):
            for ic, (i0, n) in enumerate(CHUNKS):
                with sp.Fori(0, R) as r:
                    for u in range(ring):
                        j = r * ring + u
                        sp.wait_ge(free, j + (ic * T + 1))
                        sp.dma_start(a[:, u, 0:n * P], k.d["adjT"][ds(j * P, P), i0 * P:(i0 + n) * P]
                                     ).then_inc(loaded[u], 16)

        @block.gpsimd
        def _(pool):
            for ic in range(len(CHUNKS)):
                with pool.Fori(0, R) as r:
                    for u in range(ring):
                        j = r * ring + u
                        pool.wait_ge(free, j + (ic * T + 1))
                        nc.gpsimd.tensor_copy(hv[:, u, :], k.h[:, ds(j, 1), :].rearrange("p o c -> p (o c)")
                                              ).then_inc(picked, 1)

        @block.vector
        def _(dve):
            link = Chain(dve, own)
            link(nc.vector.memset(a[:, :, WMAX * P:(WMAX + 1) * P], 0.0))
            nc.vector.memset(zeros[:, :], 0.0).then_inc(init, 1)
            for ic, (i0, n) in enumerate(CHUNKS):
                w = n * P
                with dve.Fori(0, R) as r:
                    link.enter(r, ring)
                    for u in range(ring):
                        j = r * ring + u
                        dve.wait_ge(loaded[u], (r + (ic * R + 1)) * 16)
                        own_block = a[:, u, ds(diagonal_block(dve, j, i0, n, WMAX), P)]
                        link(nc.vector.tensor_tensor(own_block, own_block, not_ident[:, :], MUL))
                        nc.vector.tensor_scalar(pos[:, u, 0:w], a[:, u, 0:w], 0.0, None, ALU.is_gt)
                        nc.vector.tensor_scalar(neg[:, u, 0:w], a[:, u, 0:w], 0.0, None,
                                                ALU.is_lt).then_inc(ready, 1)
                link.leave(R)
                dve.wait_ge(free, (ic + 1) * T + ring)
                for b, (c0, col, hw) in zip((0, 1), halves(i0, n)):
                    nc.vector.tensor_copy(nsT[:, col:col + hw], k.ps[:, b, 0:hw])
                for b, (c0, col, hw) in zip((2,), halves(i0, n)):
                    nc.vector.tensor_copy(spT[:, col:col + hw], k.ps[:, b, 0:hw]).then_inc(taken_dve, 1)

        @block.scalar
        def _(act):
            for ic, (i0, n) in enumerate(CHUNKS):
                act.wait_ge(free, (ic + 1) * T + ring)
                (_, col, hw) = halves(i0, n)[1]
                nc.scalar.copy(spT[:, col:col + hw], k.ps[:, 3, 0:hw])
                for b, (c0, col, hw) in zip((4, 5), halves(i0, n)):
                    last = nc.scalar.copy(smT[:, col:col + hw], k.ps[:, b, 0:hw])
                last.then_inc(taken_act, 1)

        @block.tensor
        def _(pe):
            pe.wait_ge(init, 1)
            for ic, (i0, n) in enumerate(CHUNKS):
                if ic:
                    pe.wait_ge(taken_dve, ic)
                    pe.wait_ge(taken_act, ic)
                for b in range(6):
                    ins = nc.tensor.matmul(k.ps[:, b, :], zeros[:, 0:P], zeros[:, :], start=True, stop=False,
                                           skip_group_check=True)
                    if ic == 0 and b < ring:
                        ins.then_inc(free, 1)
                acc = dict(stop=False, start=False, skip_group_check=True)
                with pe.Fori(0, R) as r:
                    for u in range(ring):
                        j = r * ring + u
                        pe.wait_ge(ready, j + (ic * T + 1))
                        pe.wait_ge(picked, j + (ic * T + 1))
                        for b, (c0, _, hw) in enumerate(halves(i0, n)):
                            nc.tensor.matmul(k.ps[:, b, 0:hw], hv[:, u, :], a[:, u, c0:c0 + hw], **acc)
                        for s in range(3):
                            part = hs[:, ds(j, 1), s, :].rearrange("p o c -> p (o c)")
                            for m, mat in enumerate((pos, neg)):
                                for b, (c0, _, hw) in enumerate(halves(i0, n)):
                                    last = nc.tensor.matmul(k.ps[:, 2 + 2 * m + b, 0:hw], part,
                                                            mat[:, u, c0:c0 + hw], **acc)
                        last.then_inc(free, 1)


LSE_HALF = 36.0


def attention_logits(k, c, spT, smT, et, tau, top, yt):
    nc, ctx = k.nc, ExitStack()
    H = L2_HEADS
    with ctx:
        r1 = k.sb("al_r1", [P, 2 * H], ctx=ctx)
        r2 = k.sb("al_r2", [P, 2 * H], ctx=ctx)
        ends = k.sb("al_ends", [P, 2], ctx=ctx)
        ends_all = k.sb("al_ends_all", [P, 2], ctx=ctx)
        rtau = k.sb("al_rtau", [P, 1], ctx=ctx)
        yf = k.sb("al_yf", [P, T, 2 * H], ctx=ctx)
        made, taken, logits, ends_ready, spread, scaled, exped, own = (
            k.sem("al_" + n, ctx) for n in ("made", "taken", "logits", "ends", "spread", "scaled", "exped", "dve"))
        block = ctx.enter_context(nc.Block())

        @block.tensor
        def _(pe):
            for h in range(H):
                last = nc.tensor.matmul(k.ps[:, 7, 2 * h:2 * h + 2], c["gat_wT"][:, h * P:(h + 1) * P],
                                        c["gat_a"][:, 2 * h:2 * h + 2], start=True, stop=True)
            last.then_inc(made, 1)
            pe.wait_ge(taken, 1)
            for t in range(T):
                at = slice(t * P, (t + 1) * P)
                out = k.ps[:, 6, t * 2 * H:(t + 1) * 2 * H]
                nc.tensor.matmul(out, spT[:, at], r1[:, :], start=True, stop=False)
                last = nc.tensor.matmul(out, smT[:, at], r2[:, :], start=False, stop=True)
            last.then_inc(logits, 1)

        @block.vector
        def _(dve):
            link = Chain(dve, own)
            dve.wait_ge(made, 1)
            uv = k.ps[:, 7, 0:2 * H].rearrange("p (h a) -> p a h", a=2)
            nc.vector.tensor_copy(r1[:, :].rearrange("p (a h) -> p a h", a=2), uv)
            nc.vector.tensor_copy(r2[:, 0:H], uv[:, 1, :])
            nc.vector.tensor_copy(r2[:, H:2 * H], uv[:, 0, :]).then_inc(taken, 1)
            dve.wait_ge(logits, 1)
            link(nc.vector.tensor_copy(et[:, :], k.ps[:, 6, 0:T * 2 * H]))
            link(nc.vector.scalar_tensor_tensor(et[:, :], et[:, :], L2_ALPHA, et[:, :], MUL, MAX))
            nc.vector.reduce_max(ends[:, 0:1], et[:, :], X)
            link(nc.vector.tensor_reduce(ends[:, 1:2], et[:, :], X, MIN))
            nc.vector.tensor_scalar(ends[:, 1:2], ends[:, 1:2], -1.0, None, MUL).then_inc(ends_ready, 1)
            dve.wait_ge(spread, 1)
            link(nc.vector.tensor_copy(top[:, :], ends_all[:, 0:1]))
            link(nc.vector.tensor_tensor(tau[:, :], ends_all[:, 0:1], ends_all[:, 1:2], ADD))
            link(nc.vector.tensor_scalar(tau[:, :], tau[:, :], 0.5 / LSE_HALF, 1e-20, MUL, ADD))
            link(nc.vector.reciprocal(rtau[:, :], tau[:, :]))
            link(nc.vector.tensor_scalar(yf[:, :, :].rearrange("p t c -> p (t c)"), et[:, :], top[:, 0:1],
                                         rtau[:, 0:1], SUB, MUL))
            nc.vector.tensor_scalar(yf[:, :, :], yf[:, :, :], LSE_HALF, None, ADD).then_inc(scaled, 1)
            link(nc.vector.tensor_scalar(et[:, :], et[:, :], -1.0, None, MUL))

        @block.gpsimd
        def _(pool):
            pool.wait_ge(ends_ready, 1)
            nc.gpsimd.partition_all_reduce(ends_all[:, :], ends[:, :], P, bass.bass_isa.ReduceOp.max
                                           ).then_inc(spread, 1)

        @block.scalar
        def _(act):
            act.wait_ge(scaled, 1)
            nc.scalar.activation(yt[:, :, :], yf[:, :, :], ACT.Exp).then_inc(exped, 1)


def row_guards(k, not_ident, yt, tau, top, guards):
    nc, ctx = k.nc, ExitStack()
    H, ring = L2_HEADS, 2
    R = T // ring
    with ctx:
        a = k.sb("rg_adj", [P, ring, NP], ctx=ctx)
        pos = k.sb("rg_pos", [P, ring, NP], BF16, ctx=ctx)
        neg = k.sb("rg_neg", [P, ring, NP], BF16, ctx=ctx)
        zeros = k.sb("rg_zeros", [P, P], BF16, ctx=ctx)
        sums = k.sb("rg_sums", [P, T * H], ctx=ctx)
        shift = k.sb("rg_shift", [P, 1], ctx=ctx)
        loaded = [k.sem(f"rg_loaded{u}", ctx) for u in range(ring)]
        ready, free, freed, clipped, logged, init, own = (
            k.sem("rg_" + n, ctx) for n in ("ready", "free", "freed", "clipped", "logged", "zeros", "dve"))
        block = ctx.enter_context(nc.Block())

        @block.sync
        def _(sp):
            for u in range(ring):
                sp.dma_start(a[:, u, :], k.d["adjT"][u * P:(u + 1) * P, :]).then_inc(loaded[u], 16)
            with sp.Fori(1, R) as r:
                for u in range(ring):
                    j = r * ring + u
                    sp.wait_ge(ready, j - (ring - 1))
                    sp.dma_start(a[:, u, :], k.d["adjT"][ds(j * P, P), :]).then_inc(loaded[u], 16)

        @block.vector
        def _(dve):
            link = Chain(dve, own)
            nc.vector.memset(zeros[:, :], 0.0).then_inc(init, 1)
            with dve.Fori(0, R) as r:
                link.enter(r, ring)
                for u in range(ring):
                    j = r * ring + u
                    dve.wait_ge(loaded[u], (r + 1) * 16)
                    own_block = a[:, u, ds(j * P, P)]
                    link(nc.vector.tensor_tensor(own_block, own_block, not_ident[:, :], MUL))
                    dve.wait_ge(free, j + 1)
                    nc.vector.tensor_scalar(pos[:, u, :], a[:, u, :], 0.0, None, ALU.is_gt)
                    nc.vector.tensor_scalar(neg[:, u, :], a[:, u, :], 0.0, None, ALU.is_lt).then_inc(ready, 1)
            link.leave(R)
            dve.wait_ge(free, T + ring)
            nc.vector.tensor_scalar(sums[:, :], k.ps[:, 0, 0:T * H], 1e-19, None, MAX).then_inc(clipped, 1)
            link(nc.vector.scalar_tensor_tensor(shift[:, :], tau[:, :], 0.01 - LSE_HALF, top[:, :], MUL, ADD))
            dve.wait_ge(logged, 1)
            link(nc.vector.tensor_scalar(guards[:, :], sums[:, :], tau[:, 0:1], shift[:, 0:1], MUL, ADD))

        @block.scalar
        def _(act):
            act.wait_ge(clipped, 1)
            nc.scalar.activation(sums[:, :], sums[:, :], ACT.Ln).then_inc(logged, 1)

        @block.tensor
        def _(pe):
            pe.wait_ge(init, 1)
            acc = dict(start=False, stop=False, skip_group_check=True)
            for u in range(ring):
                nc.tensor.matmul(k.ps[:, 0, 0:P], zeros[:, :], zeros[:, :], start=True, stop=False,
                                 skip_group_check=True).then_inc(free, 1)
            with pe.Fori(0, R) as r:
                for u in range(ring):
                    j = r * ring + u
                    pe.wait_ge(ready, j + 1)
                    for i in range(T):
                        at = slice(i * P, (i + 1) * P)
                        for m, mat in enumerate((pos, neg)):
                            last = nc.tensor.matmul(k.ps[:, 0, i * H:(i + 1) * H], mat[:, u, at],
                                                    yt[:, ds(j, 1), m * H:(m + 1) * H].rearrange("p o c -> p (o c)"),
                                                    **acc)
                    last.then_inc(free, 1)


def signed_attention(k, c, not_ident, neg_et, gb, es):
    nc, ctx = k.nc, ExitStack()
    H, ring = L2_HEADS, 2
    R = T // ring
    signs = ((0, ALU.is_gt, MAX), (1, ALU.is_lt, MIN))
    with ctx:
        a = k.sb("sa_adj", [P, ring, (WMAX + 1) * P], ctx=ctx)
        mask = k.sb("sa_mask", [P, ring, WMAX * P], BF16, ctx=ctx)
        q = k.sb("sa_q", [P, ring, H, WMAX * P], ctx=ctx)
        wa = k.sb("sa_wa", [P, ring, H, WMAX * P], ctx=ctx)
        hv = k.sb("sa_h", [P, ring, P], ctx=ctx)
        zeros = k.sb("sa_zeros", [P, BANK], BF16, ctx=ctx)
        ones = k.sb("sa_ones", [P, 1], ctx=ctx)
        rden = k.sb("sa_rden", [P, H * WMAX], ctx=ctx)
        numT = k.sb("sa_numT", [P, H, WMAX * P], ctx=ctx)
        loaded = [k.sem(f"sa_loaded{u}", ctx) for u in range(ring)]
        exped, ready, free, distanced, picked, taken_act, taken_dve, projected, summed, init, own, masked = (
            k.sem("sa_" + n, ctx) for n in ("exped", "ready", "free", "distanced", "picked", "taken_act", "taken_dve",
                                            "projected", "summed", "zeros", "dve", "masked"))
        block = ctx.enter_context(nc.Block())
        passes = [(ic, i0, n, s) for ic, (i0, n) in enumerate(CHUNKS) for s in (0, 1)]

        @block.sync
        def _(sp):
            for g, (ic, i0, n, s) in enumerate(passes):
                with sp.Fori(0, R) as r:
                    for u in range(ring):
                        j = r * ring + u
                        sp.wait_ge(free, j + (g * T + 1))
                        sp.dma_start(a[:, u, 0:n * P], k.d["adjT"][ds(j * P, P), i0 * P:(i0 + n) * P]
                                     ).then_inc(loaded[u], 16)

        @block.gpsimd
        def _(pool):
            for g in range(len(passes)):
                with pool.Fori(0, R) as r:
                    for u in range(ring):
                        j = r * ring + u
                        pool.wait_ge(free, j + (g * T + 1))
                        nc.gpsimd.tensor_copy(hv[:, u, :], k.h[:, ds(j, 1), :].rearrange("p o c -> p (o c)")
                                              ).then_inc(picked, 1)

        @block.scalar
        def _(act):
            for g, (ic, i0, n, s) in enumerate(passes):
                w = n * P
                with act.Fori(0, R) as r:
                    for u in range(ring):
                        j = r * ring + u
                        act.wait_ge(free, j + (g * T + 1))
                        for h in range(H):
                            last = nc.scalar.activation(q[:, u, h, 0:w], gb[:, h, i0 * P:i0 * P + w], ACT.Relu,
                                                        bias=neg_et[:, ds(j * (2 * H) + (s * H + h), 1)])
                        last.then_inc(distanced, 1)
                        act.wait_ge(distanced, j + (g * T + 1))
                        last = nc.scalar.activation(q[:, u, :, 0:w], q[:, u, :, 0:w], ACT.Exp, scale=-1.0)
                        last.then_inc(exped, 1)
                if s:
                    act.wait_ge(free, (g + 1) * T + ring)
                    if ic:
                        act.wait_ge(projected, ic)
                    for h in range(H):
                        for b, (c0, _, hw) in enumerate(halves(i0, n)):
                            last = nc.scalar.copy(numT[:, h, c0:c0 + hw], k.ps[:, 2 * h + b, 0:hw])
                    last.then_inc(taken_act, 1)

        @block.vector
        def _(dve):
            link = Chain(dve, own)
            link(nc.vector.memset(a[:, :, WMAX * P:(WMAX + 1) * P], 0.0))
            nc.vector.memset(ones[:, :], 1.0)
            nc.vector.memset(zeros[:, :], 0.0).then_inc(init, 1)
            for g, (ic, i0, n, s) in enumerate(passes):
                w = n * P
                _, compare, keep = signs[s]
                with dve.Fori(0, R) as r:
                    link.enter(r, 2 * ring)
                    for u in range(ring):
                        j = r * ring + u
                        dve.wait_ge(loaded[u], (r + (g * R + 1)) * 16)
                        own_block = a[:, u, ds(diagonal_block(dve, j, i0, n, WMAX), P)]
                        link(nc.vector.tensor_tensor(own_block, own_block, not_ident[:, :], MUL))
                        nc.vector.tensor_scalar(mask[:, u, 0:w], a[:, u, 0:w], 0.0, None, compare)
                        link(nc.vector.tensor_scalar(a[:, u, 0:w], a[:, u, 0:w], 0.0, None, keep))
                        dve.wait_ge(exped, j + (g * T + 1))
                        for h in range(H):
                            nc.vector.tensor_tensor(wa[:, u, h, 0:w], q[:, u, h, 0:w], a[:, u, 0:w], MUL)
                            last = nc.vector.tensor_tensor(q[:, u, h, 0:w], q[:, u, h, 0:w], mask[:, u, 0:w], MUL)
                        last.then_inc(ready, 1)
                link.leave(R)
                if s:
                    dve.wait_ge(free, (g + 1) * T + ring)
                    link(nc.vector.tensor_scalar(rden[:, :], k.ps[:, 6, 0:H * WMAX], 1e-37, float(H), MAX, MUL))
                    nc.vector.reciprocal(rden[:, :], rden[:, :]).then_inc(taken_dve, 1)
                    dve.wait_ge(taken_dve, ic + 1)
                    dve.wait_ge(projected, ic + 1)
                    for h in range(H):
                        for i in range(n):
                            out, term = es[:, i0 + i, :], k.ps[:, i, h * P:(h + 1) * P]
                            scale = rden[:, h * WMAX + i:h * WMAX + i + 1]
                            if h == 0:
                                last = nc.vector.tensor_scalar(out, term, scale, None, MUL)
                            else:
                                last = nc.vector.scalar_tensor_tensor(out, term, scale, out, MUL, ADD)
                        link(last)
                    nc.vector.memset(ones[:, :], 1.0).then_inc(summed, 1)

        @block.tensor
        def _(pe):
            pe.wait_ge(init, 1)
            acc = dict(start=False, stop=False, skip_group_check=True)
            for g, (ic, i0, n, s) in enumerate(passes):
                if s == 0:
                    if ic:
                        pe.wait_ge(summed, ic)
                    for b in range(7):
                        ins = nc.tensor.matmul(k.ps[:, b, :], zeros[:, 0:P], zeros[:, :], start=True, stop=False,
                                               skip_group_check=True)
                        if ic == 0 and b < ring:
                            ins.then_inc(free, 1)
                with pe.Fori(0, R) as r:
                    for u in range(ring):
                        j = r * ring + u
                        pe.wait_ge(ready, j + (g * T + 1))
                        pe.wait_ge(picked, j + (g * T + 1))
                        for h in range(H):
                            for b, (c0, _, hw) in enumerate(halves(i0, n)):
                                nc.tensor.matmul(k.ps[:, 2 * h + b, 0:hw], hv[:, u, :], wa[:, u, h, c0:c0 + hw], **acc)
                        for h in range(H):
                            for i in range(n):
                                last = nc.tensor.matmul(k.ps[:, 6, h * WMAX + i:h * WMAX + i + 1],
                                                        q[:, u, h, i * P:(i + 1) * P], ones[:, :], **acc)
                        last.then_inc(free, 1)
                if s:
                    pe.wait_ge(taken_act, ic + 1)
                    pe.wait_ge(taken_dve, ic + 1)
                    for i in range(n):
                        for h in range(H):
                            last = nc.tensor.matmul(k.ps[:, i, h * P:(h + 1) * P], numT[:, h, i * P:(i + 1) * P],
                                                    c["gat_w"][:, h * P:(h + 1) * P], start=True, stop=True)
                    last.then_inc(projected, 1)


def gru(k, inT, wih, whh, bih, bhh, who):
    nc, ctx = k.nc, ExitStack()
    groups = [(t, min(PER, T - t)) for t in range(0, T, PER)]
    RZ, IN, HN = slice(0, 2 * P), slice(2 * P, 3 * P), slice(3 * P, 4 * P)
    with ctx:
        bias = k.sb(f"gru_bias_{who}", [P, 4 * P], ctx=ctx)
        gate = k.sb(f"gru_gate_{who}", [P, PER, 4 * P], ctx=ctx)
        n_t = k.sb(f"gru_n_{who}", [P, PER, P], ctx=ctx)
        made, added, sig, mixed, tanh, own = (
            k.sem("gru_" + n, ctx) for n in ("made", "added", "sig", "mixed", "tanh", "dve"))
        block = ctx.enter_context(nc.Block())

        @block.tensor
        def _(pe):
            for g, (t0, n) in enumerate(groups):
                if g >= 2:
                    pe.wait_ge(added, g - 1)
                for i in range(n):
                    at, bank = slice((t0 + i) * P, (t0 + i + 1) * P), k.ps[:, (g % 2) * PER + i, :]
                    nc.tensor.matmul(bank[:, RZ], inT[:, at], wih[:, RZ], start=True, stop=False)
                    nc.tensor.matmul(bank[:, RZ], k.hT[:, at], whh[:, RZ], start=False, stop=True)
                    nc.tensor.matmul(bank[:, IN], inT[:, at], wih[:, IN], start=True, stop=True)
                    last = nc.tensor.matmul(bank[:, HN], k.hT[:, at], whh[:, IN], start=True, stop=True)
                last.then_inc(made, 1)

        @block.scalar
        def _(act):
            for g, (t0, n) in enumerate(groups):
                act.wait_ge(added, g + 1)
                nc.scalar.activation(gate[:, 0:n, RZ], gate[:, 0:n, RZ], ACT.Sigmoid).then_inc(sig, 1)
                act.wait_ge(mixed, g + 1)
                nc.scalar.activation(n_t[:, 0:n, :], n_t[:, 0:n, :], ACT.Tanh).then_inc(tanh, 1)

        @block.vector
        def _(dve):
            link = Chain(dve, own)
            nc.vector.tensor_tensor(bias[:, RZ], bih[:, RZ], bhh[:, RZ], ADD)
            nc.vector.tensor_copy(bias[:, IN], bih[:, IN])
            link(nc.vector.tensor_copy(bias[:, HN], bhh[:, IN]))
            for g, (t0, n) in enumerate(groups):
                dve.wait_ge(made, g + 1)
                b0 = (g % 2) * PER
                nc.vector.tensor_tensor(gate[:, 0:n, :], k.ps[:, b0:b0 + n, :],
                                        bias[:, :].unsqueeze(1).to_broadcast([P, n, 4 * P]), ADD).then_inc(added, 1)
                dve.wait_ge(added, g + 1)
                dve.wait_ge(sig, g + 1)
                link(nc.vector.tensor_tensor(n_t[:, 0:n, :], gate[:, 0:n, 0:P], gate[:, 0:n, HN], MUL))
                nc.vector.tensor_tensor(n_t[:, 0:n, :], n_t[:, 0:n, :], gate[:, 0:n, IN], ADD).then_inc(mixed, 1)
                dve.wait_ge(tanh, g + 1)
                link(nc.vector.tensor_tensor(gate[:, 0:n, IN], k.h[:, t0:t0 + n, :], n_t[:, 0:n, :], SUB))
                link(nc.vector.tensor_tensor(gate[:, 0:n, IN], gate[:, 0:n, IN], gate[:, 0:n, P:2 * P], MUL))
                link(nc.vector.tensor_tensor(gate[:, 0:n, IN], gate[:, 0:n, IN], n_t[:, 0:n, :], ADD))
                link(nc.vector.tensor_tensor(gate[:, 0:n, IN], gate[:, 0:n, IN], bcast(k.diag[:, t0:t0 + n], P), MUL))
                link(nc.vector.tensor_tensor(k.x[:, t0:t0 + n, :], k.x[:, t0:t0 + n, :], gate[:, 0:n, IN], ADD))


def layer2(k, c):
    nc = k.nc
    H = L2_HEADS
    with ExitStack() as ctx:
        not_ident = k.sb("not_ident", [P, P], ctx=ctx)
        nsT = k.sb("l2_nsT", [P, NP], ctx=ctx)
        et = k.sb("l2_et", [P, T * 2 * H], ctx=ctx)
        tau = k.sb("l2_tau", [P, 1], ctx=ctx)
        top = k.sb("l2_top", [P, 1], ctx=ctx)
        yt = k.sb("l2_yt", [P, T, 2 * H], BF16, ctx=ctx)
        guards = k.sb("l2_guards", [P, T * H], ctx=ctx)
        with ExitStack() as inner:
            spT = k.sb("l2_spT", [P, NP], ctx=inner)
            smT = k.sb("l2_smT", [P, NP], ctx=inner)
            hs = k.sb("l2_hs", [P, T, 3, P], BF16, ctx=inner)
            with ExitStack() as first:
                rest = k.sb("l2_rest", [P, T, P], ctx=first)
                own = k.sem("l2_dve", first)
                block = first.enter_context(nc.Block())

                @block.vector
                def _(dve):
                    link = Chain(dve, own)
                    link(nc.vector.tensor_scalar(not_ident[:, :], k.ident[:, :], -1.0, 1.0, MUL, ADD))
                    link(nc.vector.tensor_copy(rest[:, :, :], k.h[:, :, :]))
                    split_bf16(link, nc, [hs[:, :, n, :] for n in range(3)], rest[:, :, :])
            signed_sums(k, hs, not_ident, nsT, spT, smT)
            attention_logits(k, c, spT, smT, et, tau, top, yt)
        row_guards(k, not_ident, yt, tau, top, guards)
        es = k.sb("l2_es", [P, T, P], ctx=ctx)
        with ExitStack() as inner:
            gb = k.sb("l2_gb", [P, H, NP], ctx=inner)
            spread_rows(k, lambda t, h: guards[:, t * H + h:t * H + h + 1], gb, "l2")
            signed_attention(k, c, not_ident, et, gb, es)
        gru(k, nsT, c["ewihT"], c["ewhhT"], c["ebih"], c["ebhh"], "edge")
        to_features(k, es, nsT, "l2")
        gru(k, nsT, c["nwihT"], c["nwhhT"], c["nbih"], c["nbhh"], "node")


def random_walk(k, xf, rdeg, u1T, z, first):
    nc = k.nc
    with ExitStack() as ctx:
        agg = k.sb(f"rw_agg_{first}", [P, NP], ctx=ctx)
        taken_dve, taken_act, made, read = (
            k.sem("rw_" + n, ctx) for n in ("taken_dve", "taken_act", "made", "read"))
        block = ctx.enter_context(nc.Block())
        pairs = [(t, min(2, T - t)) for t in range(0, T, 2)]

        @block.scalar
        def _(act):
            for b, col, w in BANKS[1::2]:
                nc.scalar.copy(agg[:, col:col + w], k.psf[:, col:col + w]).then_inc(taken_act, 1)

        @block.tensor
        def _(pe):
            pe.wait_ge(taken_dve, len(BANKS[0::2]))
            pe.wait_ge(taken_act, len(BANKS[1::2]))
            for g, (t0, n) in enumerate(pairs):
                if g >= 8:
                    pe.wait_ge(read, g - 7)
                for i in range(n):
                    at = slice((t0 + i) * P, (t0 + i + 1) * P)
                    for m, mat in enumerate((u1T, k.ident[:, :])):
                        last = nc.tensor.matmul(k.ps[:, g % 8, (2 * i + m) * P:(2 * i + m + 1) * P], agg[:, at], mat,
                                                start=True, stop=True)
                last.then_inc(made, 1)

        @block.vector
        def _(dve):
            for b, col, w in BANKS[0::2]:
                nc.vector.tensor_copy(agg[:, col:col + w], k.psf[:, col:col + w]).then_inc(taken_dve, 1)
            for g, (t0, n) in enumerate(pairs):
                dve.wait_ge(made, g + 1)
                for i in range(n):
                    t = t0 + i
                    scale = rdeg[:, t:t + 1]
                    product = k.ps[:, g % 8, 2 * i * P:(2 * i + 1) * P]
                    if first:
                        nc.vector.tensor_scalar(z[:, t, :], product, scale, None, MUL)
                    else:
                        nc.vector.scalar_tensor_tensor(z[:, t, :], product, scale, z[:, t, :], MUL, ADD)
                    last = nc.vector.tensor_scalar(xf[:, t, :], k.ps[:, g % 8, (2 * i + 1) * P:(2 * i + 2) * P], scale,
                                                   None, MUL)
                last.then_inc(read, 1)


def queries_and_keys(k, c, xaT, q1T, qT, kT, who):
    nc = k.nc
    with ExitStack() as ctx:
        made, taken_dve, taken_act = (k.sem("qk_" + n, ctx) for n in ("made", "taken_dve", "taken_act"))
        block = ctx.enter_context(nc.Block())
        jobs = [(c["l3w1T"], xaT, q1T), (c["l3w3T"], xaT, kT), (c["l3w2T"], q1T, qT)]
        EVEN, ODD = len(BANKS[0::2]), len(BANKS[1::2])

        @block.tensor
        def _(pe):
            for n, (w, source, _) in enumerate(jobs):
                if n == 2:
                    pe.wait_ge(taken_dve, EVEN)
                    pe.wait_ge(taken_act, ODD)
                for b, col, wd in BANKS:
                    if n and b % 2 == 0:
                        pe.wait_ge(taken_dve, (n - 1) * EVEN + b // 2 + 1)
                    elif n:
                        pe.wait_ge(taken_act, (n - 1) * ODD + b // 2 + 1)
                    nc.tensor.matmul(k.psf[0:D_ATTN, col:col + wd], w[:], source[:, col:col + wd], start=True,
                                     stop=True).then_inc(made, 1)

        @block.vector
        def _(dve):
            for n, (_, _, dest) in enumerate(jobs):
                for b, col, wd in BANKS[0::2]:
                    dve.wait_ge(made, n * NB + b + 1)
                    nc.vector.tensor_copy(dest[:, col:col + wd], k.psf[0:D_ATTN, col:col + wd]).then_inc(taken_dve, 1)

        @block.scalar
        def _(act):
            for n, (_, _, dest) in enumerate(jobs):
                for b, col, wd in BANKS[1::2]:
                    act.wait_ge(made, n * NB + b + 1)
                    nc.scalar.copy(dest[:, col:col + wd], k.psf[0:D_ATTN, col:col + wd]).then_inc(taken_act, 1)


def top_p_attention(k, qT, kT, xa, out, who):
    nc, ctx = k.nc, ExitStack()
    from math import exp
    half_range = [SEARCH_SPAN / 2 ** (n + 1) for n in range(SEARCH_ROUNDS + 1)]
    groups = [(g, g * PER, min(PER, T - g * PER)) for g in range(NB)]
    LB, TB, OB = 0, 3, 5
    MIDWAY = SEARCH_ROUNDS // 2
    LINKS = 2 + 3 * SEARCH_ROUNDS + 5
    with ctx:
        p = k.sb(f"ta_p_{who}", [P, 2, NP], ctx=ctx)
        junk = k.sb(f"ta_junk_{who}", [P, NP], BF16, ctx=ctx)
        pT = k.sb(f"ta_pT_{who}", [P, T, P], ctx=ctx)
        qs = k.sb(f"ta_q_{who}", [D_ATTN, 2, P], ctx=ctx)
        top = k.sb(f"ta_top_{who}", [P, 2], ctx=ctx)
        total = k.sb(f"ta_total_{who}", [P, 2], ctx=ctx)
        goal = k.sb(f"ta_goal_{who}", [P, 1], ctx=ctx)
        reach = k.sb(f"ta_reach_{who}", [P, 1], ctx=ctx)
        step = k.sb(f"ta_step_{who}", [P, 1], ctx=ctx)
        thr = k.sb(f"ta_thr_{who}", [P, 1], ctx=ctx)
        least = k.sb(f"ta_least_{who}", [P, 1], ctx=ctx)
        rden = k.sb(f"ta_rden_{who}", [P, 2], ctx=ctx)
        names = ("padded", "q_ready", "logits", "copied", "topped", "exped", "masked", "turned", "taken", "multiplied",
                 "out_read", "own")
        padded, q_ready, logits, copied, topped, exped, masked, turned, taken, multiplied, out_read, own = (
            k.sem("ta_" + n, ctx) for n in names)
        block = ctx.enter_context(nc.Block())
        LOOPED = (T - 4) // 2
        assert T == 4 + 2 * LOOPED

        def rows(engine, body):
            body(0, 0)
            body(1, 1)
            with engine.Fori(0, LOOPED) as r:
                body(r * 2 + 2, 0)
                body(r * 2 + 3, 1)
            body(T - 2, 0)
            body(T - 1, 1)

        def ahead(i, by):
            return not isinstance(i, int) or i + by < T

        @block.gpsimd
        def _(pool):
            def pick(i, slot):
                if not isinstance(i, int) or i >= 2:
                    pool.wait_ge(logits, i * NB - NB)
                nc.gpsimd.tensor_copy(qs[:, slot, :], qT[:, ds(i * P, P)]).then_inc(q_ready, 1)
            rows(pool, pick)

        @block.tensor
        def _(pe):
            def make_logits(i, slot):
                pe.wait_ge(q_ready, i + 1)
                for b, col, w in BANKS:
                    if b >= 3:
                        pe.wait_ge(copied, i * NB + (b - 2))
                    elif b == 0 and not (isinstance(i, int) and i == 0):
                        pe.wait_ge(copied, i * NB)
                    nc.tensor.matmul(k.ps[:, LB + b % 3, 0:w], qs[:, slot, :], kT[:, col:col + w], start=True,
                                     stop=True).then_inc(logits, 1)

            def turn_and_multiply(i, slot):
                pe.wait_ge(masked, i + 1)
                for g, t0, n in groups:
                    if g > 1:
                        pe.wait_ge(taken, i * NB + (g - 1))
                    elif g == 0 and not (isinstance(i, int) and i == 0):
                        pe.wait_ge(taken, i * NB)
                    for t in range(n):
                        last = nc.tensor.transpose(k.ps[:, TB + g % 2, t * P:(t + 1) * P],
                                                   p[:, slot, (t0 + t) * P:(t0 + t + 1) * P], k.ident[:, :])
                    last.then_inc(turned, 1)
                if not isinstance(i, int) or i >= 2:
                    pe.wait_ge(out_read, i - 1)
                for g, t0, n in groups:
                    pe.wait_ge(taken, i * NB + (g + 1))
                    for j in range(t0, t0 + n):
                        last = nc.tensor.matmul(k.ps[:, OB + slot, 0:P], pT[:, j, :], xa[:, j, :], start=j == 0,
                                                stop=j == T - 1)
                last.then_inc(multiplied, 1)

            make_logits(0, 0)
            make_logits(1, 1)

            def row(i, slot):
                turn_and_multiply(i, slot)
                if ahead(i, 2):
                    make_logits(i + 2, slot)
            rows(pe, row)

        @block.scalar
        def _(act):
            def copy_logits(i, slot):
                for b, col, w in BANKS:
                    act.wait_ge(logits, i * NB + (b + 1))
                    if b == 0 and not (isinstance(i, int) and i < 2):
                        act.wait_ge(turned, i * NB - NB)
                    w = min(w, NODES - col)
                    nc.scalar.copy(p[:, slot, col:col + w], k.ps[:, LB + b % 3, 0:w]).then_inc(copied, 1)

            def exponentials(i, slot):
                act.wait_ge(topped, i + 1)
                nc.scalar.activation(p[:, slot, 0:NODES], p[:, slot, 0:NODES], ACT.Exp, bias=top[:, slot:slot + 1],
                                     accum_out=total[:, slot:slot + 1]).then_inc(exped, 1)

            act.wait_ge(padded, 1)
            copy_logits(0, 0)
            exponentials(0, 0)
            copy_logits(1, 1)

            def row(i, slot):
                if ahead(i, 1):
                    exponentials(i + 1, 1 - slot)
                for g, t0, n in groups:
                    act.wait_ge(turned, i * NB + (g + 1))
                    if g == 0 and not (isinstance(i, int) and i == 0):
                        act.wait_ge(multiplied, i)
                    nc.scalar.copy(pT[:, t0:t0 + n, :].rearrange("p t c -> p (t c)"), k.ps[:, TB + g % 2, 0:n * P]
                                   ).then_inc(taken, 1)
                if ahead(i, 2):
                    copy_logits(i + 2, slot)
            rows(act, row)

        @block.vector
        def _(dve):
            link = Chain(dve, own)
            nc.vector.memset(p[:, :, NODES:NP], 0.0).then_inc(padded, 1)

            def largest(i, slot):
                dve.wait_ge(copied, i * NB + NB)
                link(nc.vector.reduce_max(top[:, slot:slot + 1], p[:, slot, 0:NODES], X))
                nc.vector.tensor_scalar(top[:, slot:slot + 1], top[:, slot:slot + 1], -1.0, None, MUL
                                        ).then_inc(topped, 1)

            def search(slot, rounds):
                for n in rounds:
                    link(nc.vector.scalar_tensor_tensor(junk[:, 0:NODES], p[:, slot, 0:NODES], thr[:, 0:1],
                                                        p[:, slot, 0:NODES], ALU.is_ge, MUL, accum_out=reach[:, 0:1]))
                    up, down = exp(half_range[n + 1]), exp(-half_range[n + 1])
                    link(nc.vector.tensor_scalar(step[:, :], reach[:, :], goal[:, 0:1], up - down, ALU.is_ge, MUL))
                    link(nc.vector.scalar_tensor_tensor(thr[:, :], step[:, :], down, thr[:, :], ADD, MUL))

            def read_out(i, slot):
                dve.wait_ge(multiplied, i + 1)
                nc.vector.tensor_scalar(out[:, ds(i, 1), :].rearrange("p o c -> p (o c)"), k.ps[:, OB + slot, 0:P],
                                        rden[:, slot:slot + 1], None, MUL).then_inc(out_read, 1)

            def row(i, slot):
                dve.wait_ge(exped, i + 1)
                link(nc.vector.memset(thr[:, :], exp(-half_range[0])))
                link(nc.vector.tensor_scalar(goal[:, :], total[:, slot:slot + 1], TOP_P, None, MUL))
                search(slot, range(MIDWAY))
                if not (isinstance(i, int) and i == 0):
                    read_out(i - 1, 1 - slot)
                if ahead(i, 1):
                    largest(i + 1, 1 - slot)
                else:
                    link(nc.vector.memset(step[:, :], 0.0))
                search(slot, range(MIDWAY, SEARCH_ROUNDS))
                link(nc.vector.tensor_scalar(thr[:, :], thr[:, :], exp(-half_range[SEARCH_ROUNDS]), None, MUL))
                link(nc.vector.tensor_scalar(least[:, :], total[:, slot:slot + 1], 1e-12, None, MUL))
                nc.vector.scalar_tensor_tensor(p[:, slot, 0:NODES], p[:, slot, 0:NODES], thr[:, 0:1],
                                               p[:, slot, 0:NODES], ALU.is_ge, MUL,
                                               accum_out=rden[:, slot:slot + 1]).then_inc(masked, 1)
                dve.wait_ge(masked, i + 1)
                link(nc.vector.tensor_tensor(rden[:, slot:slot + 1], rden[:, slot:slot + 1], least[:, :], MAX))
                link(nc.vector.reciprocal(rden[:, slot:slot + 1], rden[:, slot:slot + 1]))

            largest(0, 0)
            row(0, 0)
            row(1, 1)
            with dve.Fori(0, LOOPED) as r:
                link.enter(r, 2 * LINKS)
                row(r * 2 + 2, 0)
                row(r * 2 + 3, 1)
            link.leave(LOOPED)
            row(T - 2, 0)
            row(T - 1, 1)
            read_out(T - 1, 1)


def add_product(k, sourceT, w, z, who):
    nc = k.nc
    with ExitStack() as ctx:
        made = k.sem("ap_made", ctx)
        block = ctx.enter_context(nc.Block())

        @block.tensor
        def _(pe):
            for b, col, wd in BANKS:
                for t in range(col // P, (col + wd) // P):
                    last = nc.tensor.matmul(k.psf[:, t * P:(t + 1) * P], sourceT[:, t * P:(t + 1) * P], w, start=True,
                                            stop=True)
                last.then_inc(made, 1)

        @block.vector
        def _(dve):
            for b, col, wd in BANKS:
                dve.wait_ge(made, b + 1)
                zs = z[:, col // P:(col + wd) // P, :]
                nc.vector.tensor_tensor(zs, zs, k.psf[:, col:col + wd].rearrange("p (t c) -> p t c", c=P), ADD)


def layer3(k, c):
    nc = k.nc
    with ExitStack() as ctx:
        z = k.sb("l3_z", [P, T, P], ctx=ctx)
        rdeg = k.sb("l3_rdeg", [P, T], ctx=ctx)
        xf = k.sb("l3_xf", [P, T, P], ctx=ctx)
        with ExitStack() as inner:
            own = k.sem("l3_own", inner)
            block = inner.enter_context(nc.Block())

            @block.vector
            def _(dve):
                link = Chain(dve, own)
                link(nc.vector.tensor_scalar(rdeg[:, :], k.deg[:, :], 1.0, None, ADD))
                link(nc.vector.reciprocal(rdeg[:, :], rdeg[:, :]))
        for n in range(STEPS):
            propagate(k, xf if n else k.h, f"walk{n}", self_loops=True)
            random_walk(k, xf, rdeg, c["u1T"][:, n * P:(n + 1) * P], z, n == 0)
        xa, new = k.h, xf
        for n in range(STEPS):
            with ExitStack() as inner:
                qT = k.sb(f"l3_qT{n}", [D_ATTN, NP], ctx=inner)
                kT = k.sb(f"l3_kT{n}", [D_ATTN, NP], ctx=inner)
                with ExitStack() as first:
                    q1T = k.sb(f"l3_q1T{n}", [D_ATTN, NP], ctx=first)
                    queries_and_keys(k, c, k.hT, q1T, qT, kT, n)
                if n == 0:
                    with ExitStack() as first:
                        block = first.enter_context(nc.Block())

                        @block.vector
                        def _(dve):
                            nc.vector.tensor_tensor(z[:, :, :], z[:, :, :], k.h[:, :, :], ADD)
                top_p_attention(k, qT, kT, xa, new, n)
            to_features(k, new, k.hT, f"l3{n}")
            add_product(k, k.hT, c["u2T"][:, n * P:(n + 1) * P], z, n)
            xa, new = new, xa
        layer_norm(k, "l3_out", source=z, affine=(c["ln_g"], c["ln_b"]))


def build(nc, d, out, upto=9):
    ctx = ExitStack()
    with ctx:
        k = Kernel(nc, ctx, d, out)
        c = {n: k.sb(n + "_sb", list(s)) for n, s in dict(
            w0T=(P, P), w1=(P, P), w1T=(P, P), gat_w=(P, L2_HEADS * P), gat_wT=(P, L2_HEADS * P),
            gat_a=(P, 2 * L2_HEADS), ewihT=(P, 3 * P), ewhhT=(P, 3 * P), nwihT=(P, 3 * P), nwhhT=(P, 3 * P),
            l3w1T=(P, D_ATTN), l3w2T=(D_ATTN, D_ATTN), l3w3T=(P, D_ATTN), u1T=(P, STEPS * P), u2T=(P, STEPS * P),
            b0=(P, P), ebih=(P, 3 * P), ebhh=(P, 3 * P), nbih=(P, 3 * P), nbhh=(P, 3 * P), ln_g=(P, P), ln_b=(P, P),
            a_blocks=(P, 2 * L1_HEADS)).items()}
        load_constants(k, c)
        layer_norm(k, "l0")
        if upto >= 1:
            layer0(k, c)
        if upto >= 2:
            layer_norm(k, "l1")
            layer1(k, c)
        clear_semaphores(k)
        if upto >= 3:
            layer_norm(k, "l2")
            layer2(k, c)
        clear_semaphores(k)
        if upto >= 4:
            layer_norm(k, "l3")
            layer3(k, c)
        store(k)


def store(k):
    nc = k.nc
    with ExitStack() as ctx:
        stored = k.sem("stored", ctx)
        block = ctx.enter_context(nc.Block())

        @block.sync
        def _(sp):
            sp.dma_start(k.out, k.x[:, :, :]).then_inc(stored, 16)
            sp.wait_ge(stored, 16)


def kernel(**inputs):
    import numpy as np
    import concourse.bacc as bacc
    from concourse.bass_utils import run_bass_kernel_spmd

    def packed(a):
        return np.ascontiguousarray(a.reshape(T, P, -1).transpose(1, 0, 2))

    g = {n: np.asarray(a) for n, a in inputs.items()}
    pad = NP - NODES
    adj = np.pad(g["adj"], ((0, pad), (0, pad)))
    row = lambda n: np.ascontiguousarray(g[n].reshape(1, -1))
    turn = lambda n: np.ascontiguousarray(g[n].T)
    side = lambda a: np.ascontiguousarray(np.concatenate(list(a), axis=1))
    arrays = dict(
        x=packed(np.pad(g["x"], ((0, pad), (0, 0)))), adj=adj, adjT=np.ascontiguousarray(adj.T),
        diag=packed(np.diagonal(adj)).reshape(P, T),
        w0T=turn("L0_gnn_W"), b0=row("L0_gnn_b"), w1=g["L1_gnn_W"], w1T=turn("L1_gnn_W"),
        a_l=g["L1_gnn_a_l"].reshape(-1, 1), a_r=g["L1_gnn_a_r"].reshape(-1, 1),
        gat_w=side(g["L2_gnn_gat_W"]), gat_wT=side(g["L2_gnn_gat_W"].transpose(0, 2, 1)),
        gat_a=np.ascontiguousarray(g["L2_gnn_gat_a"].reshape(L2_HEADS, 2, P).transpose(2, 0, 1).reshape(P, -1)),
        ewihT=turn("L2_gnn_edge_Wih"), ewhhT=turn("L2_gnn_edge_Whh"), nwihT=turn("L2_gnn_node_Wih"),
        nwhhT=turn("L2_gnn_node_Whh"), ebih=row("L2_gnn_edge_bih"), ebhh=row("L2_gnn_edge_bhh"),
        nbih=row("L2_gnn_node_bih"), nbhh=row("L2_gnn_node_bhh"), ln_g=row("L3_gnn_ln_g"), ln_b=row("L3_gnn_ln_b"),
        l3w1T=turn("L3_gnn_W1"), l3w2T=turn("L3_gnn_W2"), l3w3T=turn("L3_gnn_W3"),
        u1T=side(g["L3_gnn_U1"].transpose(0, 2, 1)), u2T=side(g["L3_gnn_U2"].transpose(0, 2, 1)))
    arrays = {n: np.ascontiguousarray(a) for n, a in arrays.items()}
    nc = bacc.Bacc("TRN2", target_bir_lowering=False, num_devices=1)
    d = {n: nc.dram_tensor(f"in_{n}", a.shape, mybir.dt.from_np(a.dtype), kind="ExternalInput").ap()
         for n, a in arrays.items()}
    out = nc.dram_tensor("out_x", (P, T, P), F32, kind="ExternalOutput").ap()
    build(nc, d, out)
    r = run_bass_kernel_spmd(nc, [{f"in_{n}": a for n, a in arrays.items()}], core_ids=[0])
    return np.ascontiguousarray(r.results[0]["out_x"].transpose(1, 0, 2).reshape(NP, P)[:NODES])
```

```python
import concourse.bass as bass
from concourse import mybir
from contextlib import ExitStack

F32 = mybir.dt.float32
BF16 = mybir.dt.bfloat16
ALU = mybir.AluOpType
ACT = mybir.ActivationFunctionType
X = mybir.AxisListType.X
ADD, SUB, MUL, MAX, MIN = ALU.add, ALU.subtract, ALU.mult, ALU.max, ALU.min
ds = bass.ds

P = 128
NODES = 3327
T = (NODES + P - 1) // P
NP = T * P
BANK = 512
NB = (NP + BANK - 1) // BANK
PER = BANK // P
BANKS = [(b, b * BANK, min(BANK, NP - b * BANK)) for b in range(NB)]
LN_EPS = 1e-5
L1_HEADS, L1_D = 4, 32
L1_SLOPE = 0.2
L2_HEADS = 3
L2_ALPHA = 0.2
CHUNKS = [(0, 6), (6, 6), (12, 6), (18, 8)]
WMAX = max(n for _, n in CHUNKS)
D_ATTN, STEPS, TOP_P = 64, 2, 0.9
SEARCH_SPAN = 10.42
SEARCH_ROUNDS = 13
ALL_ROUNDS = 22


class Chain:

    def __init__(self, engine, sem):
        self.engine, self.sem, self.base, self.k, self.i, self.per = engine, sem, 0, 0, None, 0

    def count(self, ins):
        self.k += 1
        ins.then_inc(self.sem, 1)

    def __call__(self, ins):
        self.count(ins)
        at = self.base + self.k
        if self.i is not None:
            at = at + self.i * self.per
        self.engine.wait_ge(self.sem, at)
        return ins

    def enter(self, i, per):
        assert self.i is None
        self.base, self.k, self.i, self.per = self.base + self.k, 0, i, per

    def leave(self, rounds):
        assert self.k == self.per, (self.k, self.per)
        self.base, self.k, self.i = self.base + rounds * self.per, 0, None


def tiles(ap):
    return ap.rearrange("p (t c) -> p t c", t=T)


class Kernel:

    def __init__(self, nc, ctx, d, out):
        self.nc, self.ctx, self.d, self.out = nc, ctx, d, out
        self.names = {}
        self.counted = []
        sb = self.sb
        self.ps = ctx.enter_context(nc.psum_tensor("psum", [P, 8, BANK], F32))
        self.psf = self.ps[:, :, :].rearrange("p b c -> p (b c)")
        self.x = sb("x", [P, T, P])
        self.h = sb("h", [P, T, P])
        self.hT = sb("hT", [P, NP])
        self.ident = sb("ident", [P, P])
        self.deg = sb("deg", [P, T])
        self.diag = sb("diag", [P, T])
        self.signed = sb("signed", [P, 1], mybir.dt.int32)
        self.s1 = sb("s1", [P, T])
        self.s2 = sb("s2", [P, T])
        self.s3 = sb("s3", [P, T])
        self.s4 = sb("s4", [P, T])

    def sb(self, name, shape, dt=F32, ctx=None):
        return (ctx or self.ctx).enter_context(self.nc.sbuf_tensor(name, shape, dt))

    def sem(self, name, ctx):
        n = self.names[name] = self.names.get(name, 0) + 1
        handle = ctx.enter_context(self.nc.semaphore(f"{name}_{n}"))
        self.counted.append(handle)
        return handle


def clear_semaphores(k):
    with k.nc.Block() as block:
        @block.gpsimd
        def _(pool):
            for handle in k.counted:
                pool.sem_clear(handle)
    k.counted = []


def bcast(ap, n):
    return ap.unsqueeze(2).to_broadcast([ap.shape[0], ap.shape[1], n])


def layer_norm(k, who, source=None, affine=None):
    nc, ctx = k.nc, ExitStack()
    source = k.x if source is None else source
    with ctx:
        xc = k.sb(f"ln_centred_{who}", [P, T, P], ctx=ctx)
        sq = k.sb(f"ln_squares_{who}", [P, T, P], ctx=ctx)
        centred, squared, var_ready, root_ready, h_ready = (
            k.sem(n, ctx) for n in ("ln_centred", "ln_squared", "ln_var", "ln_root", "ln_h"))
        turned, taken_dve, taken_act = (k.sem(n, ctx) for n in ("ln_turned", "ln_taken_dve", "ln_taken_act"))
        own, own_act = k.sem("ln_dve", ctx), k.sem("ln_act", ctx)
        block = ctx.enter_context(nc.Block())

        @block.vector
        def _(dve):
            link = Chain(dve, own)
            link(nc.vector.reduce_sum(k.s1[:, :], source[:, :, :], X))
            link(nc.vector.tensor_scalar(k.s1[:, :], k.s1[:, :], 1.0 / P, None, MUL))
            nc.vector.tensor_tensor(xc[:, :, :], source[:, :, :], bcast(k.s1[:, :], P), SUB).then_inc(centred, 1)
            dve.wait_ge(squared, 1)
            link(nc.vector.reduce_sum(k.s2[:, :], sq[:, :, :], X))
            nc.vector.tensor_scalar(k.s2[:, :], k.s2[:, :], 1.0 / P, LN_EPS, MUL, ADD).then_inc(var_ready, 1)
            dve.wait_ge(var_ready, 1)
            dve.wait_ge(root_ready, 1)
            link(nc.vector.reciprocal(k.s4[:, :], k.s3[:, :]))
            link(nc.vector.tensor_tensor(k.s4[:, :], k.s4[:, :], k.s2[:, :], MUL))
            link(nc.vector.tensor_tensor(k.s4[:, :], k.s4[:, :], k.s3[:, :], ADD))
            link(nc.vector.tensor_scalar(k.s4[:, :], k.s4[:, :], 0.5, None, MUL))
            link(nc.vector.reciprocal(k.s4[:, :], k.s4[:, :]))
            if affine:
                gain, shift = (v[:, :].unsqueeze(1).to_broadcast([P, T, P]) for v in affine)
                link(nc.vector.tensor_tensor(xc[:, :, :], xc[:, :, :], bcast(k.s4[:, :], P), MUL))
                link(nc.vector.tensor_tensor(xc[:, :, :], xc[:, :, :], gain, MUL))
                link(nc.vector.tensor_tensor(xc[:, :, :], xc[:, :, :], shift, ADD))
                link(nc.vector.tensor_tensor(k.x[:, :, :], k.x[:, :, :], xc[:, :, :], ADD))
                return
            nc.vector.scalar_tensor_tensor(k.h[:, :, :], xc[:, :, :], 0.0, bcast(k.s4[:, :], P),
                                           MAX, MUL).then_inc(h_ready, 1)
            for b, c, w in BANKS[0::2]:
                dve.wait_ge(turned, b + 1)
                last = nc.vector.tensor_copy(k.hT[:, c:c + w], k.psf[:, c:c + w])
            last.then_inc(taken_dve, 1)

        @block.scalar
        def _(act):
            act.wait_ge(centred, 1)
            nc.scalar.activation(sq[:, :, :], xc[:, :, :], ACT.Square).then_inc(squared, 1)
            act.wait_ge(var_ready, 1)
            nc.scalar.activation(k.s3[:, :], k.s2[:, :], ACT.Sqrt).then_inc(root_ready, 1)
            if affine:
                return
            for b, c, w in BANKS[1::2]:
                act.wait_ge(turned, b + 1)
                last = nc.scalar.copy(k.hT[:, c:c + w], k.psf[:, c:c + w])
            last.then_inc(taken_act, 1)

        @block.tensor
        def _(pe):
            if affine:
                return
            pe.wait_ge(h_ready, 1)
            for b, c, w in BANKS:
                for t in range(c // P, (c + w) // P):
                    last = nc.tensor.transpose(k.psf[:, t * P:(t + 1) * P], k.h[:, t, :], k.ident[:, :])
                last.then_inc(turned, 1)


def propagate(k, source, who, ring=3, self_loops=False):
    nc, ctx = k.nc, ExitStack()
    first = 2
    assert (T - first) % ring == 0
    rounds = (T - first) // ring
    with ctx:
        a = k.sb(f"pr_adj_{who}", [P, ring, NP], ctx=ctx)
        v = k.sb(f"pr_source_{who}", [P, ring, P], ctx=ctx)
        loaded = [k.sem(f"pr_loaded{u}", ctx) for u in range(ring)]
        picked, used = k.sem("pr_picked", ctx), k.sem("pr_used", ctx)
        block = ctx.enter_context(nc.Block())

        def steps(engine, body):
            for j in range(first):
                body(j, j % ring, 0)
            with engine.Fori(0, rounds) as r:
                for u in range(ring):
                    slot = (first + u) % ring
                    body(r * ring + (first + u), slot, r + (first + u) // ring)

        @block.sync
        def _(sp):
            def load(j, slot, before):
                if not isinstance(j, int) or j >= ring:
                    sp.wait_ge(used, j - (ring - 1))
                sp.dma_start(a[:, slot, :], k.d["adjT"][ds(j * P, P), :]).then_inc(loaded[slot], 16)
            for j in range(ring):
                load(j, j, 0)
            with sp.Fori(0, rounds - 1) as r:
                for u in range(ring):
                    load(r * ring + (ring + u), u, r + 1)
            for j in range(ring * rounds, T):
                load(j, j % ring, 0)

        @block.gpsimd
        def _(pool):
            def pick(j, slot, before):
                if not isinstance(j, int) or j >= ring:
                    pool.wait_ge(used, j - (ring - 1))
                nc.gpsimd.tensor_copy(v[:, slot, :], source[:, ds(j, 1), :].rearrange("p o c -> p (o c)")).then_inc(picked, 1)
            for j in range(ring):
                pick(j, j, 0)
            with pool.Fori(0, rounds - 1) as r:
                for u in range(ring):
                    pick(r * ring + (ring + u), u, r + 1)
            for j in range(ring * rounds, T):
                pick(j, j % ring, 0)

        @block.tensor
        def _(pe):
            def tile(j, slot, before):
                pe.wait_ge(loaded[slot], (before + 1) * 16)
                pe.wait_ge(picked, j + 1)
                for b, c, w in BANKS:
                    last = nc.tensor.matmul(k.psf[:, c:c + w], v[:, slot, :], a[:, slot, c:c + w],
                                            start=isinstance(j, int) and j == 0, stop=False,
                                            skip_group_check=True)
                if self_loops:
                    last = nc.tensor.matmul(k.psf[:, ds(j * P, P)], v[:, slot, :], k.ident[:, :],
                                            start=False, stop=False, skip_group_check=True)
                last.then_inc(used, 1)
            steps(pe, tile)


def load_constants(k, c):
    nc, ctx = k.nc, ExitStack()
    ring = 4
    with ctx:
        a = k.sb("degree_rows", [P, ring, NP], ctx=ctx)
        below = k.sb("degree_below", [P, T], ctx=ctx)
        below_junk = k.sb("degree_below_junk", [P, ring, NP], BF16, ctx=ctx)
        most = k.sb("degree_most", [P, 1], ctx=ctx)
        most_all = k.sb("degree_most_all", [P, 1], ctx=ctx)
        negatives, most_ready, most_spread = (k.sem(n, ctx) for n in ("negatives", "most_ready", "most_spread"))
        arrived = k.sem("constants_arrived", ctx)
        loaded = [k.sem(f"rows_loaded{u}", ctx) for u in range(ring)]
        zeroed, ident_ready, blocks_zero, summed, own = (
            k.sem(n, ctx) for n in ("ident_zeroed", "ident_ready", "blocks_zero", "summed", "deg_dve"))
        block = ctx.enter_context(nc.Block())
        d = k.d
        first, rest = T % ring, T // ring

        @block.scalar
        def _(act):
            pairs = [(k.x[:, :, :], d["x"]), (k.diag[:, :], d["diag"])]
            pairs += [(c[n][:], d[n]) for n in ("w0T", "w1", "w1T", "gat_w", "gat_wT", "gat_a", "ewihT", "ewhhT",
                                               "nwihT", "nwhhT", "l3w1T", "l3w2T", "l3w3T", "u1T", "u2T")]
            pairs += [(c[n][:], d[n].to_broadcast([P, d[n].shape[1]])) for n in
                      ("b0", "ebih", "ebhh", "nbih", "nbhh", "ln_g", "ln_b")]
            for dst, src in pairs:
                act.dma_start(dst, src).then_inc(arrived, 16)
            act.wait_ge(blocks_zero, 1)
            for s, name in enumerate(("a_l", "a_r")):
                for h in range(L1_HEADS):
                    at = slice(h * L1_D, (h + 1) * L1_D)
                    act.dma_start(c["a_blocks"][at, s * L1_HEADS + h:s * L1_HEADS + h + 1],
                                  d[name][at, :]).then_inc(arrived, 16)
            def find_negatives(t, u, turn):
                act.wait_ge(loaded[u], (turn + 1) * 16)
                nc.scalar.activation(below_junk[:, u, :], a[:, u, :], ACT.Relu, scale=-1.0,
                                     accum_out=below[:, ds(t, 1)]).then_inc(negatives, 1)
            with act.Fori(0, rest) as r:
                for u in range(ring):
                    find_negatives(r * ring + u, u, r)
            for t in range(rest * ring, T):
                find_negatives(t, t % ring, t // ring)
            act.wait_ge(arrived, 16 * (len(pairs) + 2 * L1_HEADS))

        @block.gpsimd
        def _(pool):
            nc.gpsimd.memset(c["a_blocks"][:], 0.0).then_inc(blocks_zero, 1)
            nc.gpsimd.memset(k.ident[:], 0.0).then_inc(zeroed, 1)
            pool.wait_ge(zeroed, 1)
            nc.gpsimd.affine_select(out=k.ident[:], in_=k.ident[:], compare_op=ALU.not_equal, fill=1.0,
                                    base=0, pattern=[[-1, P]], channel_multiplier=1).then_inc(ident_ready, 1)
            pool.wait_ge(ident_ready, 1)
            pool.wait_ge(most_ready, 1)
            nc.gpsimd.partition_all_reduce(most_all[:, :], most[:, :], P, bass.bass_isa.ReduceOp.max
                                           ).then_inc(most_spread, 1)

        @block.sync
        def _(sp):
            for u in range(ring):
                sp.dma_start(a[:, u, :], d["adj"][u * P:(u + 1) * P, :]).then_inc(loaded[u], 16)
            with sp.Fori(1, rest) as r:
                for u in range(ring):
                    sp.wait_ge(summed, r * ring + (u - ring + 1))
                    sp.wait_ge(negatives, r * ring + (u - ring + 1))
                    sp.dma_start(a[:, u, :], d["adj"][ds((r * ring + u) * P, P), :]).then_inc(loaded[u], 16)
            for t in range(rest * ring, T):
                sp.wait_ge(summed, t - ring + 1)
                sp.wait_ge(negatives, t - ring + 1)
                sp.dma_start(a[:, t % ring, :], d["adj"][t * P:(t + 1) * P, :]).then_inc(loaded[t % ring], 16)

        @block.vector
        def _(dve):
            def add_up(t, u, turn):
                dve.wait_ge(loaded[u], (turn + 1) * 16)
                nc.vector.reduce_sum(k.deg[:, ds(t, 1)], a[:, u, :], X).then_inc(summed, 1)
            with dve.Fori(0, rest) as r:
                for u in range(ring):
                    add_up(r * ring + u, u, r)
            for t in range(rest * ring, T):
                add_up(t, t % ring, t // ring)
            dve.wait_ge(negatives, T)
            nc.vector.reduce_max(most[:, :], below[:, :], X).then_inc(most_ready, 1)
            dve.wait_ge(most_spread, 1)
            nc.vector.tensor_scalar(k.signed[:, :], most_all[:, :], 0.0, None, ALU.is_gt)


def layer0(k, c):
    nc, ctx = k.nc, ExitStack()
    with ctx:
        y = k.sb("l0_source", [P, T, P], ctx=ctx)
        dinv = k.sb("dinv", [P, T], ctx=ctx)
        with ExitStack() as inner:
            dp, root, own = (k.sem(n, inner) for n in ("l0_deg", "l0_root", "l0_own"))
            block = inner.enter_context(nc.Block())

            @block.vector
            def _(dve):
                link = Chain(dve, own)
                nc.vector.tensor_scalar(k.s1[:, :], k.deg[:, :], 1e-9, None, ADD).then_inc(dp, 1)
                dve.wait_ge(dp, 1)
                dve.wait_ge(root, 1)
                link(nc.vector.reciprocal(k.s3[:, :], k.s2[:, :]))
                link(nc.vector.tensor_tensor(k.s3[:, :], k.s3[:, :], k.s1[:, :], MUL))
                link(nc.vector.tensor_tensor(k.s3[:, :], k.s3[:, :], k.s2[:, :], ADD))
                link(nc.vector.tensor_scalar(k.s3[:, :], k.s3[:, :], 0.5, None, MUL))
                link(nc.vector.reciprocal(dinv[:, :], k.s3[:, :]))
                link(nc.vector.tensor_tensor(y[:, :, :], k.h[:, :, :], bcast(dinv[:, :], P), MUL))

            @block.scalar
            def _(act):
                act.wait_ge(dp, 1)
                nc.scalar.activation(k.s2[:, :], k.s1[:, :], ACT.Sqrt).then_inc(root, 1)
        propagate(k, y, "l0")
        agg = k.sb("l0_agg", [P, NP], ctx=ctx)
        z = k.sb("l0_z", [P, T, P], ctx=ctx)
        with ExitStack() as inner:
            taken_dve, taken_act, made, own = (k.sem(n, inner) for n in ("l0_td", "l0_ta", "l0_made", "l0_dve"))
            block = inner.enter_context(nc.Block())

            @block.scalar
            def _(act):
                for b, col, w in BANKS[1::2]:
                    nc.scalar.copy(agg[:, col:col + w], k.psf[:, col:col + w]).then_inc(taken_act, 1)

            @block.tensor
            def _(pe):
                pe.wait_ge(taken_dve, len(BANKS[0::2]))
                pe.wait_ge(taken_act, len(BANKS[1::2]))
                for b, col, w in BANKS:
                    for t in range(col // P, (col + w) // P):
                        last = nc.tensor.matmul(k.psf[:, t * P:(t + 1) * P], agg[:, t * P:(t + 1) * P],
                                                c["w0T"][:, :], start=True, stop=True)
                    last.then_inc(made, 1)

            @block.vector
            def _(dve):
                link = Chain(dve, own)
                for b, col, w in BANKS[0::2]:
                    nc.vector.tensor_copy(agg[:, col:col + w], k.psf[:, col:col + w]).then_inc(taken_dve, 1)
                for b, col, w in BANKS:
                    dve.wait_ge(made, b + 1)
                    for t in range(col // P, (col + w) // P):
                        ins = nc.vector.scalar_tensor_tensor(z[:, t, :], k.psf[:, t * P:(t + 1) * P],
                                                             dinv[:, t:t + 1], c["b0"][:, :], MUL, ADD)
                        if t == T - 1:
                            link(ins)
                link(nc.vector.scalar_tensor_tensor(k.x[:, :, :], z[:, :, :], 0.0, k.x[:, :, :], MAX, ADD))


def diagonal_block(engine, j, i0, n, spare):
    inside = (j >= i0) * (j < i0 + n) if i0 else (j < n)
    return engine.snap((inside * (j - i0) + (1 - inside) * spare) * P).with_bounds(min_val=0, max_val=spare * P)


def split_bf16(link, nc, parts, rest):
    for n, part in enumerate(parts):
        link(nc.vector.tensor_copy(part, rest))
        if n < 2:
            link(nc.vector.tensor_tensor(rest, rest, part, SUB))


def layer1(k, c):
    nc, ctx = k.nc, ExitStack()
    H, D = L1_HEADS, L1_D
    GC, MC = 2 * (D + 1), D + 1
    VC = H * (GC + MC)
    with ctx:
        v = k.sb("l1_v", [P, T, 3, VC], BF16, ctx=ctx)
        neg_r = k.sb("l1_neg_r", [P, T * H], ctx=ctx)
        a_n = k.sb("l1_a", [P, T, H], ctx=ctx)
        c_n = k.sb("l1_c", [P, T, H], ctx=ctx)
        ub = k.sb("l1_ub", [P, H, P], ctx=ctx)
        with ExitStack() as inner:
            vf = k.sb("l1_vf", [P, T, VC], ctx=inner)
            wh = k.sb("l1_wh", [P, T, P], ctx=inner)
            sc = k.sb("l1_scores", [P, T, 2 * H], ctx=inner)
            u8 = k.sb("l1_u8", [P, 2 * H], ctx=inner)
            rmax = k.sb("l1_rmax", [P, H], ctx=inner)
            rall = k.sb("l1_rall", [P, H], ctx=inner)
            rs = k.sb("l1_rs", [P, T, H], ctx=inner)
            bt = k.sb("l1_bt", [P, T, H], ctx=inner)
            dt = k.sb("l1_dt", [P, T, H], ctx=inner)
            names = ("u_made", "u_taken", "wh_made", "rmax_ready", "rall_ready", "shifted", "tabled",
                     "wh_act", "own")
            u_made, u_taken, wh_made, rmax_ready, rall_ready, shifted, tabled, wh_act, own = (
                k.sem("l1_" + n, inner) for n in names)
            block = inner.enter_context(nc.Block())

            @block.tensor
            def _(pe):
                nc.tensor.matmul(k.ps[:, 7, 0:2 * H], c["w1"][:, :], c["a_blocks"][:, :], start=True,
                                 stop=True).then_inc(u_made, 1)
                for b, col, w in BANKS:
                    for t in range(col // P, (col + w) // P):
                        last = nc.tensor.matmul(k.psf[:, t * P:(t + 1) * P], k.hT[:, t * P:(t + 1) * P],
                                                c["w1T"][:, :], start=True, stop=True)
                    last.then_inc(wh_made, 1)
                pe.wait_ge(u_taken, 1)
                for t in range(T):
                    last = nc.tensor.matmul(k.ps[:, 7, t * 2 * H:(t + 1) * 2 * H], k.hT[:, t * P:(t + 1) * P],
                                            u8[:, :], start=True, stop=True)
                last.then_inc(wh_made, 1)

            @block.scalar
            def _(act):
                for b, col, w in BANKS[1::2]:
                    act.wait_ge(wh_made, b + 1)
                    last = nc.scalar.copy(wh[:, :, :].rearrange("p t c -> p (t c)")[:, col:col + w],
                                          k.psf[:, col:col + w])
                last.then_inc(wh_act, 1)
                act.wait_ge(shifted, 1)
                nc.scalar.activation(bt[:, :, :], rs[:, :, :], ACT.Exp)
                nc.scalar.activation(dt[:, :, :], rs[:, :, :], ACT.Exp, scale=L1_SLOPE).then_inc(tabled, 1)
                act.wait_ge(shifted, 2)
                nc.scalar.activation(a_n[:, :, :], a_n[:, :, :], ACT.Exp)
                nc.scalar.activation(c_n[:, :, :], c_n[:, :, :], ACT.Exp).then_inc(tabled, 1)
                act.wait_ge(tabled, 2)

            @block.gpsimd
            def _(pool):
                pool.wait_ge(rmax_ready, 1)
                nc.gpsimd.partition_all_reduce(rall[:, :], rmax[:, :], P, bass.bass_isa.ReduceOp.max).then_inc(rall_ready, 1)
                pool.wait_ge(rall_ready, 1)

            @block.vector
            def _(dve):
                link = Chain(dve, own)
                dve.wait_ge(u_made, 1)
                nc.vector.tensor_copy(u8[:, :], k.ps[:, 7, 0:2 * H]).then_inc(u_taken, 1)
                dve.wait_ge(u_taken, 1)
                link(nc.vector.tensor_copy(ub[:, :, :], bcast(u8[:, 0:H], P)))
                for b, col, w in BANKS[0::2]:
                    dve.wait_ge(wh_made, b + 1)
                    nc.vector.tensor_copy(wh[:, :, :].rearrange("p t c -> p (t c)")[:, col:col + w],
                                          k.psf[:, col:col + w])
                dve.wait_ge(wh_made, NB + 1)
                link(nc.vector.tensor_copy(sc[:, :, :], k.ps[:, 7, 0:T * 2 * H].rearrange("p (t e) -> p t e", t=T)))
                nc.vector.reduce_max(rmax[:, :], sc[:, :, H:2 * H].rearrange("p t e -> p e t"), X).then_inc(rmax_ready, 1)
                link(nc.vector.tensor_scalar(neg_r[:, :].rearrange("p (t e) -> p t e", t=T), sc[:, :, H:2 * H],
                                             -1.0, None, MUL))
                dve.wait_ge(rall_ready, 1)
                top = rall[:, :].unsqueeze(1).to_broadcast([P, T, H])
                nc.vector.tensor_tensor(rs[:, :, :], sc[:, :, H:2 * H], top, SUB).then_inc(shifted, 1)
                link(nc.vector.tensor_tensor(sc[:, :, 0:H], sc[:, :, 0:H], top, ADD))
                link(nc.vector.tensor_scalar(a_n[:, :, :], sc[:, :, 0:H], 1 - L1_SLOPE, 0.0, MUL, MIN))
                nc.vector.tensor_scalar(c_n[:, :, :], sc[:, :, 0:H], L1_SLOPE - 1, 0.0, MUL, MIN).then_inc(shifted, 1)
                dve.wait_ge(tabled, 1)
                dve.wait_ge(wh_act, 1)
                wh4 = wh[:, :, :].rearrange("p t (h d) -> p t h d", h=H)
                vg = vf[:, :, 0:H * GC].rearrange("p t (h d) -> p t h d", h=H)
                vm = vf[:, :, H * GC:VC].rearrange("p t (h d) -> p t h d", h=H)
                wide = lambda ap, n: ap.unsqueeze(3).to_broadcast([P, T, H, n])
                nc.vector.tensor_tensor(vg[:, :, :, 0:D], wh4, wide(bt[:, :, :], D), MUL)
                nc.vector.tensor_copy(vg[:, :, :, D:D + 1], wide(bt[:, :, :], 1))
                nc.vector.tensor_tensor(vm[:, :, :, 0:D], wh4, wide(dt[:, :, :], D), MUL)
                link(nc.vector.tensor_copy(vm[:, :, :, D:MC], wide(dt[:, :, :], 1)))
                link(nc.vector.tensor_scalar(vg[:, :, :, D + 1:GC], vm, -1.0, None, MUL))
                split_bf16(link, nc, [v[:, :, n, :] for n in range(3)], vf[:, :, :])

        lb = k.sb("l1_lb", [P, H, NP], ctx=ctx)
        with ExitStack() as inner:
            made, taken = k.sem("l1_lb_made", inner), k.sem("l1_lb_taken", inner)
            taken_dve = k.sem("l1_lb_taken_dve", inner)
            block = inner.enter_context(nc.Block())

            @block.tensor
            def _(pe):
                for h in range(H):
                    for b, col, w in BANKS:
                        if h:
                            pe.wait_ge(*((taken_dve, (h - 1) * 4 + b // 2 + 1) if b % 2 == 0 else
                                         (taken, (h - 1) * 3 + b // 2 + 1)))
                        nc.tensor.matmul(k.psf[:, col:col + w], ub[:, h, :], k.hT[:, col:col + w], start=True,
                                         stop=True).then_inc(made, 1)

            @block.scalar
            def _(act):
                for h in range(H):
                    for b, col, w in BANKS[1::2]:
                        act.wait_ge(made, h * NB + b + 1)
                        nc.scalar.copy(lb[:, h, col:col + w], k.psf[:, col:col + w]).then_inc(taken, 1)

            @block.vector
            def _(dve):
                for h in range(H):
                    for b, col, w in BANKS[0::2]:
                        dve.wait_ge(made, h * NB + b + 1)
                        nc.vector.tensor_copy(lb[:, h, col:col + w], k.psf[:, col:col + w]).then_inc(taken_dve, 1)

        ring = 2
        assert T % ring == 0
        a = k.sb("l1_adj", [P, ring, (WMAX + 1) * P], ctx=ctx)
        mask = k.sb("l1_mask", [P, ring, WMAX * P], BF16, ctx=ctx)
        g = k.sb("l1_g", [P, ring, H, WMAX * P], BF16, ctx=ctx)
        zeros = k.sb("l1_zeros", [P, P], BF16, ctx=ctx)
        e = k.h[:, :, :].rearrange("p t c -> p (t c)")[:, 0:WMAX * VC].rearrange("p (i c) -> p i c", i=WMAX)
        t1, t2 = (k.hT[:, n * WMAX * H * MC:(n + 1) * WMAX * H * MC].rearrange("p (i h d) -> p i h d", i=WMAX, h=H)
                  for n in range(2))
        loaded = [k.sem(f"l1_loaded{u}", ctx) for u in range(ring)]
        freed, g_ready, g_free, taken, sums_used, mins, exps, own, init = (
            k.sem("l1_" + n, ctx) for n in ("freed", "g_ready", "g_free", "taken", "sums_used", "mins", "exps",
                                            "dve", "zeros"))
        block = ctx.enter_context(nc.Block())

        @block.sync
        def _(sp):
            for ic, (i0, n) in enumerate(CHUNKS):
                def load(j, u, g0):
                    if ic or not isinstance(j, int):
                        sp.wait_ge(freed, j + (ic * T - ring + 1))
                    sp.dma_start(a[:, u, 0:n * P], k.d["adjT"][ds(j * P, P), i0 * P:(i0 + n) * P]
                                 ).then_inc(loaded[u], 16)
                for u in range(ring):
                    load(u, u, 0)
                with sp.Fori(1, T // ring) as r:
                    for u in range(ring):
                        load(r * ring + u, u, 0)

        @block.vector
        def _(dve):
            link = Chain(dve, own)
            link(nc.vector.memset(a[:, :, WMAX * P:(WMAX + 1) * P], 0.0))
            nc.vector.memset(zeros[:, :], 0.0).then_inc(init, 1)
            for ic, (i0, n) in enumerate(CHUNKS):
                w = n * P
                with dve.Fori(0, T // ring) as r:
                    link.enter(r, ring)
                    for u in range(ring):
                        j = r * ring + u
                        dve.wait_ge(loaded[u], (r + (ic * (T // ring) + 1)) * 16)
                        own_block = a[:, u, ds(diagonal_block(dve, j, i0, n, WMAX), P)]
                        link(nc.vector.tensor_tensor(own_block, own_block, k.ident[:, :], ADD))
                        dve.wait_ge(g_free, j + (ic * T + 1))
                        nc.vector.tensor_scalar(mask[:, u, 0:w], a[:, u, 0:w], 0.0, None,
                                                ALU.is_gt).then_inc(freed, 1)
                        dve.wait_ge(freed, j + (ic * T + 1))
                        for h in range(H):
                            last = nc.vector.scalar_tensor_tensor(
                                g[:, u, h, 0:w], lb[:, h, i0 * P:i0 * P + w],
                                neg_r[:, ds(j * H + h, 1)], mask[:, u, 0:w], ALU.is_gt, MUL)
                        last.then_inc(g_ready, 1)
                link.leave(T // ring)
                dve.wait_ge(taken, ic + 1)
                eg = e[:, 0:n, 0:H * GC].rearrange("p i (h d) -> p i h d", h=H)
                em = e[:, 0:n, H * GC:VC].rearrange("p i (h d) -> p i h d", h=H)
                u1, u2 = t1[:, 0:n], t2[:, 0:n]
                wide = lambda ap, m: ap[:, i0:i0 + n, :].unsqueeze(3).to_broadcast([P, n, H, m])
                link(nc.vector.tensor_tensor(u1, eg[:, :, :, MC:GC], em, ADD))
                link(nc.vector.tensor_tensor(u1, u1, wide(c_n[:, :, :], MC), MUL))
                link(nc.vector.tensor_tensor(u2, eg[:, :, :, 0:MC], wide(a_n[:, :, :], MC), MUL))
                link(nc.vector.tensor_tensor(u1, u1, u2, ADD))
                link(nc.vector.reciprocal(u2[:, :, :, D:MC], u1[:, :, :, D:MC]))
                link(nc.vector.tensor_tensor(u1[:, :, :, 0:D], u1[:, :, :, 0:D],
                                             u2[:, :, :, D:MC].to_broadcast([P, n, H, D]), MUL))
                nc.vector.tensor_scalar(u2[:, :, :, 0:D], u1[:, :, :, 0:D], 0.0, None, MIN).then_inc(mins, 1)
                dve.wait_ge(exps, ic + 1)
                link(nc.vector.tensor_scalar(u1[:, :, :, 0:D], u1[:, :, :, 0:D], 0.0, -1.0, MAX, ADD))
                link(nc.vector.tensor_tensor(u1[:, :, :, 0:D], u1[:, :, :, 0:D], u2[:, :, :, 0:D], ADD))
                xs = k.x[:, i0:i0 + n, :].rearrange("p i (h d) -> p i h d", h=H)
                nc.vector.tensor_tensor(xs, xs, u1[:, :, :, 0:D], ADD).then_inc(sums_used, 1)

        @block.scalar
        def _(act):
            for ic, (i0, n) in enumerate(CHUNKS):
                act.wait_ge(g_free, (ic + 1) * T + ring)
                if ic:
                    act.wait_ge(sums_used, ic)
                for i in range(n):
                    last = nc.scalar.copy(e[:, i, :], k.ps[:, i, 0:VC])
                last.then_inc(taken, 1)
                act.wait_ge(mins, ic + 1)
                nc.scalar.activation(t2[:, 0:n, :, 0:D], t2[:, 0:n, :, 0:D], ACT.Exp).then_inc(exps, 1)

        @block.tensor
        def _(pe):
            pe.wait_ge(init, 1)
            for ic, (i0, n) in enumerate(CHUNKS):
                if ic:
                    pe.wait_ge(taken, ic)
                for i in range(n):
                    ins = nc.tensor.matmul(k.ps[:, i, 0:VC], zeros[:, :], v[:, 0, 0, :], start=True,
                                           stop=False, skip_group_check=True)
                    if ic == 0 and i < ring:
                        ins.then_inc(g_free, 1)
                with pe.Fori(0, T // ring) as r:
                    for u in range(ring):
                        j = r * ring + u
                        pe.wait_ge(g_ready, j + (ic * T + 1))
                        for i in range(n):
                            at = slice(i * P, (i + 1) * P)
                            for m in range(H + 1):
                                cols = slice(m * GC, (m + 1) * GC) if m < H else slice(H * GC, VC)
                                for s in range(3):
                                    last = nc.tensor.matmul(
                                        k.ps[:, i, cols], g[:, u, m, at] if m < H else mask[:, u, at],
                                        v[:, ds(j, 1), s, cols].rearrange("p o c -> p (o c)"),
                                        start=False, stop=False, skip_group_check=True)
                        last.then_inc(g_free, 1)


def halves(i0, n):
    w = n * P // 2
    return [(0, i0 * P, w), (w, i0 * P + w, w)]


def to_features(k, source, dest, who):
    nc = k.nc
    with ExitStack() as ctx:
        turned, taken_dve, taken_act = (k.sem(f"tf_{n}", ctx) for n in ("turned", "taken_dve", "taken_act"))
        block = ctx.enter_context(nc.Block())

        @block.tensor
        def _(pe):
            for b, c, w in BANKS:
                for t in range(c // P, (c + w) // P):
                    last = nc.tensor.transpose(k.psf[:, t * P:(t + 1) * P], source[:, t, :], k.ident[:, :])
                last.then_inc(turned, 1)

        @block.vector
        def _(dve):
            for b, c, w in BANKS[0::2]:
                dve.wait_ge(turned, b + 1)
                nc.vector.tensor_copy(dest[:, c:c + w], k.psf[:, c:c + w]).then_inc(taken_dve, 1)

        @block.scalar
        def _(act):
            for b, c, w in BANKS[1::2]:
                act.wait_ge(turned, b + 1)
                nc.scalar.copy(dest[:, c:c + w], k.psf[:, c:c + w]).then_inc(taken_act, 1)


def spread_rows(k, columns, dest, who):
    nc = k.nc
    heads = dest.shape[1]
    with ExitStack() as ctx:
        made, taken_dve, taken_act = (k.sem(f"sr_{n}", ctx) for n in ("made", "taken_dve", "taken_act"))
        block = ctx.enter_context(nc.Block())

        @block.tensor
        def _(pe):
            for h in range(heads):
                for b, c, w in BANKS:
                    if h and b % 2 == 0:
                        pe.wait_ge(taken_dve, (h - 1) * len(BANKS[0::2]) + b // 2 + 1)
                    elif h:
                        pe.wait_ge(taken_act, (h - 1) * len(BANKS[1::2]) + b // 2 + 1)
                    for t in range(c // P, (c + w) // P):
                        last = nc.tensor.matmul(k.psf[:, t * P:(t + 1) * P], columns(t, h).to_broadcast([P, P]),
                                                k.ident[:, :], start=True, stop=True)
                    last.then_inc(made, 1)

        @block.vector
        def _(dve):
            for h in range(heads):
                for b, c, w in BANKS[0::2]:
                    dve.wait_ge(made, h * NB + b + 1)
                    nc.vector.tensor_copy(dest[:, h, c:c + w], k.psf[:, c:c + w]).then_inc(taken_dve, 1)

        @block.scalar
        def _(act):
            for h in range(heads):
                for b, c, w in BANKS[1::2]:
                    act.wait_ge(made, h * NB + b + 1)
                    nc.scalar.copy(dest[:, h, c:c + w], k.psf[:, c:c + w]).then_inc(taken_act, 1)


def signed_sums(k, hs, not_ident, nsT, spT, smT):
    nc, ctx = k.nc, ExitStack()
    ring = 2
    with ctx:
        a = k.sb("ss_adj", [P, ring, (WMAX + 1) * P], ctx=ctx)
        pos = k.sb("ss_pos", [P, ring, WMAX * P], BF16, ctx=ctx)
        neg = k.sb("ss_neg", [P, ring, WMAX * P], BF16, ctx=ctx)
        hv = k.sb("ss_h", [P, ring, P], ctx=ctx)
        zeros = k.sb("ss_zeros", [P, BANK], BF16, ctx=ctx)
        loaded = [k.sem(f"ss_loaded{u}", ctx) for u in range(ring)]
        ready, free, picked, taken_act, taken_dve, init, own = (
            k.sem("ss_" + n, ctx) for n in ("ready", "free", "picked", "taken_act", "taken_dve", "zeros", "dve"))
        block = ctx.enter_context(nc.Block())
        R = T // ring

        @block.sync
        def _(sp):
            for ic, (i0, n) in enumerate(CHUNKS):
                with sp.Fori(0, R) as r:
                    for u in range(ring):
                        j = r * ring + u
                        sp.wait_ge(free, j + (ic * T + 1))
                        sp.dma_start(a[:, u, 0:n * P], k.d["adjT"][ds(j * P, P), i0 * P:(i0 + n) * P]
                                     ).then_inc(loaded[u], 16)

        @block.gpsimd
        def _(pool):
            for ic in range(len(CHUNKS)):
                with pool.Fori(0, R) as r:
                    for u in range(ring):
                        j = r * ring + u
                        pool.wait_ge(free, j + (ic * T + 1))
                        nc.gpsimd.tensor_copy(hv[:, u, :], k.h[:, ds(j, 1), :].rearrange("p o c -> p (o c)")
                                              ).then_inc(picked, 1)

        @block.vector
        def _(dve):
            link = Chain(dve, own)
            link(nc.vector.memset(a[:, :, WMAX * P:(WMAX + 1) * P], 0.0))
            nc.vector.memset(zeros[:, :], 0.0).then_inc(init, 1)
            for ic, (i0, n) in enumerate(CHUNKS):
                w = n * P
                with dve.Fori(0, R) as r:
                    link.enter(r, ring)
                    for u in range(ring):
                        j = r * ring + u
                        dve.wait_ge(loaded[u], (r + (ic * R + 1)) * 16)
                        own_block = a[:, u, ds(diagonal_block(dve, j, i0, n, WMAX), P)]
                        link(nc.vector.tensor_tensor(own_block, own_block, not_ident[:, :], MUL))
                        nc.vector.tensor_scalar(pos[:, u, 0:w], a[:, u, 0:w], 0.0, None, ALU.is_gt)
                        nc.vector.tensor_scalar(neg[:, u, 0:w], a[:, u, 0:w], 0.0, None,
                                                ALU.is_lt).then_inc(ready, 1)
                link.leave(R)
                dve.wait_ge(free, (ic + 1) * T + ring)
                for b, (c0, col, hw) in zip((0, 1), halves(i0, n)):
                    nc.vector.tensor_copy(nsT[:, col:col + hw], k.ps[:, b, 0:hw])
                for b, (c0, col, hw) in zip((2,), halves(i0, n)):
                    nc.vector.tensor_copy(spT[:, col:col + hw], k.ps[:, b, 0:hw]).then_inc(taken_dve, 1)

        @block.scalar
        def _(act):
            for ic, (i0, n) in enumerate(CHUNKS):
                act.wait_ge(free, (ic + 1) * T + ring)
                (_, col, hw) = halves(i0, n)[1]
                nc.scalar.copy(spT[:, col:col + hw], k.ps[:, 3, 0:hw])
                for b, (c0, col, hw) in zip((4, 5), halves(i0, n)):
                    last = nc.scalar.copy(smT[:, col:col + hw], k.ps[:, b, 0:hw])
                last.then_inc(taken_act, 1)

        @block.tensor
        def _(pe):
            pe.wait_ge(init, 1)
            for ic, (i0, n) in enumerate(CHUNKS):
                if ic:
                    pe.wait_ge(taken_dve, ic)
                    pe.wait_ge(taken_act, ic)
                for b in range(6):
                    ins = nc.tensor.matmul(k.ps[:, b, :], zeros[:, 0:P], zeros[:, :], start=True, stop=False,
                                           skip_group_check=True)
                    if ic == 0 and b < ring:
                        ins.then_inc(free, 1)
                acc = dict(stop=False, start=False, skip_group_check=True)
                with pe.Fori(0, R) as r:
                    for u in range(ring):
                        j = r * ring + u
                        pe.wait_ge(ready, j + (ic * T + 1))
                        pe.wait_ge(picked, j + (ic * T + 1))
                        for b, (c0, _, hw) in enumerate(halves(i0, n)):
                            nc.tensor.matmul(k.ps[:, b, 0:hw], hv[:, u, :], a[:, u, c0:c0 + hw], **acc)
                        for s in range(3):
                            part = hs[:, ds(j, 1), s, :].rearrange("p o c -> p (o c)")
                            for m, mat in enumerate((pos, neg)):
                                for b, (c0, _, hw) in enumerate(halves(i0, n)):
                                    last = nc.tensor.matmul(k.ps[:, 2 + 2 * m + b, 0:hw], part,
                                                            mat[:, u, c0:c0 + hw], **acc)
                        last.then_inc(free, 1)


LSE_HALF = 36.0


def attention_logits(k, c, spT, smT, et, tau, top, yt):
    nc, ctx = k.nc, ExitStack()
    H = L2_HEADS
    with ctx:
        r1 = k.sb("al_r1", [P, 2 * H], ctx=ctx)
        r2 = k.sb("al_r2", [P, 2 * H], ctx=ctx)
        ends = k.sb("al_ends", [P, 2], ctx=ctx)
        ends_all = k.sb("al_ends_all", [P, 2], ctx=ctx)
        rtau = k.sb("al_rtau", [P, 1], ctx=ctx)
        yf = k.sb("al_yf", [P, T, 2 * H], ctx=ctx)
        made, taken, logits, ends_ready, spread, scaled, exped, own = (
            k.sem("al_" + n, ctx) for n in ("made", "taken", "logits", "ends", "spread", "scaled", "exped", "dve"))
        block = ctx.enter_context(nc.Block())

        @block.tensor
        def _(pe):
            for h in range(H):
                last = nc.tensor.matmul(k.ps[:, 7, 2 * h:2 * h + 2], c["gat_wT"][:, h * P:(h + 1) * P],
                                        c["gat_a"][:, 2 * h:2 * h + 2], start=True, stop=True)
            last.then_inc(made, 1)
            pe.wait_ge(taken, 1)
            for t in range(T):
                at = slice(t * P, (t + 1) * P)
                out = k.ps[:, 6, t * 2 * H:(t + 1) * 2 * H]
                nc.tensor.matmul(out, spT[:, at], r1[:, :], start=True, stop=False)
                last = nc.tensor.matmul(out, smT[:, at], r2[:, :], start=False, stop=True)
            last.then_inc(logits, 1)

        @block.vector
        def _(dve):
            link = Chain(dve, own)
            dve.wait_ge(made, 1)
            uv = k.ps[:, 7, 0:2 * H].rearrange("p (h a) -> p a h", a=2)
            nc.vector.tensor_copy(r1[:, :].rearrange("p (a h) -> p a h", a=2), uv)
            nc.vector.tensor_copy(r2[:, 0:H], uv[:, 1, :])
            nc.vector.tensor_copy(r2[:, H:2 * H], uv[:, 0, :]).then_inc(taken, 1)
            dve.wait_ge(logits, 1)
            link(nc.vector.tensor_copy(et[:, :], k.ps[:, 6, 0:T * 2 * H]))
            link(nc.vector.scalar_tensor_tensor(et[:, :], et[:, :], L2_ALPHA, et[:, :], MUL, MAX))
            nc.vector.reduce_max(ends[:, 0:1], et[:, :], X)
            link(nc.vector.tensor_reduce(ends[:, 1:2], et[:, :], X, MIN))
            nc.vector.tensor_scalar(ends[:, 1:2], ends[:, 1:2], -1.0, None, MUL).then_inc(ends_ready, 1)
            dve.wait_ge(spread, 1)
            link(nc.vector.tensor_copy(top[:, :], ends_all[:, 0:1]))
            link(nc.vector.tensor_tensor(tau[:, :], ends_all[:, 0:1], ends_all[:, 1:2], ADD))
            link(nc.vector.tensor_scalar(tau[:, :], tau[:, :], 0.5 / LSE_HALF, 1e-20, MUL, ADD))
            link(nc.vector.reciprocal(rtau[:, :], tau[:, :]))
            link(nc.vector.tensor_scalar(yf[:, :, :].rearrange("p t c -> p (t c)"), et[:, :], top[:, 0:1],
                                         rtau[:, 0:1], SUB, MUL))
            nc.vector.tensor_scalar(yf[:, :, :], yf[:, :, :], LSE_HALF, None, ADD).then_inc(scaled, 1)
            link(nc.vector.tensor_scalar(et[:, :], et[:, :], -1.0, None, MUL))

        @block.gpsimd
        def _(pool):
            pool.wait_ge(ends_ready, 1)
            nc.gpsimd.partition_all_reduce(ends_all[:, :], ends[:, :], P, bass.bass_isa.ReduceOp.max
                                           ).then_inc(spread, 1)

        @block.scalar
        def _(act):
            act.wait_ge(scaled, 1)
            nc.scalar.activation(yt[:, :, :], yf[:, :, :], ACT.Exp).then_inc(exped, 1)


def row_guards(k, not_ident, yt, tau, top, guards):
    nc, ctx = k.nc, ExitStack()
    H, ring = L2_HEADS, 2
    R = T // ring
    with ctx:
        a = k.sb("rg_adj", [P, ring, NP], ctx=ctx)
        pos = k.sb("rg_pos", [P, ring, NP], BF16, ctx=ctx)
        neg = k.sb("rg_neg", [P, ring, NP], BF16, ctx=ctx)
        zeros = k.sb("rg_zeros", [P, P], BF16, ctx=ctx)
        sums = k.sb("rg_sums", [P, T * H], ctx=ctx)
        shift = k.sb("rg_shift", [P, 1], ctx=ctx)
        loaded = [k.sem(f"rg_loaded{u}", ctx) for u in range(ring)]
        ready, free, freed, clipped, logged, init, own = (
            k.sem("rg_" + n, ctx) for n in ("ready", "free", "freed", "clipped", "logged", "zeros", "dve"))
        block = ctx.enter_context(nc.Block())

        @block.sync
        def _(sp):
            for u in range(ring):
                sp.dma_start(a[:, u, :], k.d["adjT"][u * P:(u + 1) * P, :]).then_inc(loaded[u], 16)
            with sp.Fori(1, R) as r:
                for u in range(ring):
                    j = r * ring + u
                    sp.wait_ge(ready, j - (ring - 1))
                    sp.dma_start(a[:, u, :], k.d["adjT"][ds(j * P, P), :]).then_inc(loaded[u], 16)

        @block.vector
        def _(dve):
            link = Chain(dve, own)
            nc.vector.memset(zeros[:, :], 0.0).then_inc(init, 1)
            with dve.Fori(0, R) as r:
                link.enter(r, ring)
                for u in range(ring):
                    j = r * ring + u
                    dve.wait_ge(loaded[u], (r + 1) * 16)
                    own_block = a[:, u, ds(j * P, P)]
                    link(nc.vector.tensor_tensor(own_block, own_block, not_ident[:, :], MUL))
                    dve.wait_ge(free, j + 1)
                    nc.vector.tensor_scalar(pos[:, u, :], a[:, u, :], 0.0, None, ALU.is_gt)
                    nc.vector.tensor_scalar(neg[:, u, :], a[:, u, :], 0.0, None, ALU.is_lt).then_inc(ready, 1)
            link.leave(R)
            dve.wait_ge(free, T + ring)
            nc.vector.tensor_scalar(sums[:, :], k.ps[:, 0, 0:T * H], 1e-19, None, MAX).then_inc(clipped, 1)
            link(nc.vector.scalar_tensor_tensor(shift[:, :], tau[:, :], 0.01 - LSE_HALF, top[:, :], MUL, ADD))
            dve.wait_ge(logged, 1)
            link(nc.vector.tensor_scalar(guards[:, :], sums[:, :], tau[:, 0:1], shift[:, 0:1], MUL, ADD))

        @block.scalar
        def _(act):
            act.wait_ge(clipped, 1)
            nc.scalar.activation(sums[:, :], sums[:, :], ACT.Ln).then_inc(logged, 1)

        @block.tensor
        def _(pe):
            pe.wait_ge(init, 1)
            acc = dict(start=False, stop=False, skip_group_check=True)
            for u in range(ring):
                nc.tensor.matmul(k.ps[:, 0, 0:P], zeros[:, :], zeros[:, :], start=True, stop=False,
                                 skip_group_check=True).then_inc(free, 1)
            with pe.Fori(0, R) as r:
                for u in range(ring):
                    j = r * ring + u
                    pe.wait_ge(ready, j + 1)
                    for i in range(T):
                        at = slice(i * P, (i + 1) * P)
                        for m, mat in enumerate((pos, neg)):
                            last = nc.tensor.matmul(k.ps[:, 0, i * H:(i + 1) * H], mat[:, u, at],
                                                    yt[:, ds(j, 1), m * H:(m + 1) * H].rearrange("p o c -> p (o c)"),
                                                    **acc)
                    last.then_inc(free, 1)


def where_signed(k, engine):
    flag = engine.value_load(k.signed[0:1, 0:1], min_val=0, max_val=1)
    return engine.If(flag > 0)


def signed_attention(k, c, not_ident, neg_et, gb, es):
    nc, ctx = k.nc, ExitStack()
    H, ring = L2_HEADS, 2
    R = T // ring
    signs = ((ALU.is_gt, MAX), (ALU.is_lt, MIN))
    with ctx:
        a = k.sb("sa_adj", [P, ring, (WMAX + 1) * P], ctx=ctx)
        mask = k.sb("sa_mask", [P, ring, WMAX * P], BF16, ctx=ctx)
        q = k.sb("sa_q", [P, ring, H, WMAX * P], ctx=ctx)
        wa = k.sb("sa_wa", [P, ring, H, WMAX * P], ctx=ctx)
        hv = k.sb("sa_h", [P, ring, P], ctx=ctx)
        zeros = k.sb("sa_zeros", [P, BANK], BF16, ctx=ctx)
        ones = k.sb("sa_ones", [P, 1], ctx=ctx)
        rden = k.sb("sa_rden", [P, H * WMAX], ctx=ctx)
        numT = k.sb("sa_numT", [P, H, WMAX * P], ctx=ctx)

        class Sems:
            def __init__(self, sign):
                self.loaded = [k.sem(f"sa_loaded{u}_{sign}", ctx) for u in range(ring)]
                self.exped, self.ready, self.free, self.distanced, self.picked, self.own = (
                    k.sem(f"sa_{n}_{sign}", ctx) for n in ("exped", "ready", "free", "distanced", "picked", "dve"))
        sems = [Sems("positive"), Sems("negative")]
        taken_act, taken_dve, projected, summed, init = (
            k.sem("sa_" + n, ctx) for n in ("taken_act", "taken_dve", "projected", "summed", "zeros"))
        block = ctx.enter_context(nc.Block())

        def chunk_passes(engine, ic, one_pass):
            one_pass(0, sems[0])
            with where_signed(k, engine):
                engine.wait_ge(sems[0].free, (ic + 1) * T + ring)
                one_pass(1, sems[1])
                engine.wait_ge(sems[1].free, (ic + 1) * T + ring)

        @block.sync
        def _(sp):
            for ic, (i0, n) in enumerate(CHUNKS):
                def load(s, m):
                    with sp.Fori(0, R) as r:
                        for u in range(ring):
                            j = r * ring + u
                            sp.wait_ge(m.free, j + (ic * T + 1))
                            sp.dma_start(a[:, u, 0:n * P], k.d["adjT"][ds(j * P, P), i0 * P:(i0 + n) * P]
                                         ).then_inc(m.loaded[u], 16)
                chunk_passes(sp, ic, load)

        @block.gpsimd
        def _(pool):
            for ic in range(len(CHUNKS)):
                def pick(s, m):
                    with pool.Fori(0, R) as r:
                        for u in range(ring):
                            j = r * ring + u
                            pool.wait_ge(m.free, j + (ic * T + 1))
                            nc.gpsimd.tensor_copy(hv[:, u, :], k.h[:, ds(j, 1), :].rearrange("p o c -> p (o c)")
                                                  ).then_inc(m.picked, 1)
                chunk_passes(pool, ic, pick)

        @block.scalar
        def _(act):
            for ic, (i0, n) in enumerate(CHUNKS):
                w = n * P

                def exponentials(s, m):
                    with act.Fori(0, R) as r:
                        for u in range(ring):
                            j = r * ring + u
                            act.wait_ge(m.free, j + (ic * T + 1))
                            for h in range(H):
                                last = nc.scalar.activation(q[:, u, h, 0:w], gb[:, h, i0 * P:i0 * P + w], ACT.Relu,
                                                            bias=neg_et[:, ds(j * (2 * H) + (s * H + h), 1)])
                            last.then_inc(m.distanced, 1)
                            act.wait_ge(m.distanced, j + (ic * T + 1))
                            nc.scalar.activation(q[:, u, :, 0:w], q[:, u, :, 0:w], ACT.Exp, scale=-1.0
                                                 ).then_inc(m.exped, 1)
                chunk_passes(act, ic, exponentials)
                act.wait_ge(sems[0].free, (ic + 1) * T + ring)
                if ic:
                    act.wait_ge(projected, ic)
                for h in range(H):
                    for b, (c0, _, hw) in enumerate(halves(i0, n)):
                        last = nc.scalar.copy(numT[:, h, c0:c0 + hw], k.ps[:, 2 * h + b, 0:hw])
                last.then_inc(taken_act, 1)

        @block.vector
        def _(dve):
            nc.vector.memset(ones[:, :], 1.0)
            nc.vector.memset(zeros[:, :], 0.0).then_inc(init, 1)
            nc.vector.memset(a[:, :, WMAX * P:(WMAX + 1) * P], 0.0).then_inc(init, 1)
            dve.wait_ge(init, 2)
            chains = [Chain(dve, m.own) for m in sems]
            epilogue = Chain(dve, k.sem("sa_epilogue", ctx))
            for ic, (i0, n) in enumerate(CHUNKS):
                w = n * P

                def weigh(s, m):
                    compare, keep = signs[s]
                    link = chains[s]
                    with dve.Fori(0, R) as r:
                        link.enter(r, 2 * ring)
                        for u in range(ring):
                            j = r * ring + u
                            dve.wait_ge(m.loaded[u], (r + (ic * R + 1)) * 16)
                            own_block = a[:, u, ds(diagonal_block(dve, j, i0, n, WMAX), P)]
                            link(nc.vector.tensor_tensor(own_block, own_block, not_ident[:, :], MUL))
                            nc.vector.tensor_scalar(mask[:, u, 0:w], a[:, u, 0:w], 0.0, None, compare)
                            link(nc.vector.tensor_scalar(a[:, u, 0:w], a[:, u, 0:w], 0.0, None, keep))
                            dve.wait_ge(m.exped, j + (ic * T + 1))
                            for h in range(H):
                                nc.vector.tensor_tensor(wa[:, u, h, 0:w], q[:, u, h, 0:w], a[:, u, 0:w], MUL)
                                last = nc.vector.tensor_tensor(q[:, u, h, 0:w], q[:, u, h, 0:w], mask[:, u, 0:w], MUL)
                            last.then_inc(m.ready, 1)
                    link.leave(R)
                chunk_passes(dve, ic, weigh)
                dve.wait_ge(sems[0].free, (ic + 1) * T + ring)
                epilogue(nc.vector.tensor_scalar(rden[:, :], k.ps[:, 6, 0:H * WMAX], 1e-37, float(H), MAX, MUL))
                nc.vector.reciprocal(rden[:, :], rden[:, :]).then_inc(taken_dve, 1)
                dve.wait_ge(taken_dve, ic + 1)
                dve.wait_ge(projected, ic + 1)
                for h in range(H):
                    for i in range(n):
                        out, term = es[:, i0 + i, :], k.ps[:, i, h * P:(h + 1) * P]
                        scale = rden[:, h * WMAX + i:h * WMAX + i + 1]
                        if h == 0:
                            last = nc.vector.tensor_scalar(out, term, scale, None, MUL)
                        else:
                            last = nc.vector.scalar_tensor_tensor(out, term, scale, out, MUL, ADD)
                    if h < H - 1:
                        epilogue(last)
                last.then_inc(summed, 1)

        @block.tensor
        def _(pe):
            pe.wait_ge(init, 1)
            acc = dict(start=False, stop=False, skip_group_check=True)
            for ic, (i0, n) in enumerate(CHUNKS):
                if ic:
                    pe.wait_ge(summed, ic)
                for b in range(7):
                    ins = nc.tensor.matmul(k.ps[:, b, :], zeros[:, 0:P], zeros[:, :], start=True, stop=False,
                                           skip_group_check=True)
                    if ic == 0 and b < 2 * ring:
                        ins.then_inc(sems[b // ring].free, 1)

                def add_up(s, m):
                    with pe.Fori(0, R) as r:
                        for u in range(ring):
                            j = r * ring + u
                            pe.wait_ge(m.ready, j + (ic * T + 1))
                            pe.wait_ge(m.picked, j + (ic * T + 1))
                            for h in range(H):
                                for b, (c0, _, hw) in enumerate(halves(i0, n)):
                                    nc.tensor.matmul(k.ps[:, 2 * h + b, 0:hw], hv[:, u, :], wa[:, u, h, c0:c0 + hw],
                                                     **acc)
                            for h in range(H):
                                for i in range(n):
                                    last = nc.tensor.matmul(k.ps[:, 6, h * WMAX + i:h * WMAX + i + 1],
                                                            q[:, u, h, i * P:(i + 1) * P], ones[:, :], **acc)
                            last.then_inc(m.free, 1)
                chunk_passes(pe, ic, add_up)
                pe.wait_ge(taken_act, ic + 1)
                pe.wait_ge(taken_dve, ic + 1)
                for i in range(n):
                    for h in range(H):
                        last = nc.tensor.matmul(k.ps[:, i, h * P:(h + 1) * P], numT[:, h, i * P:(i + 1) * P],
                                                c["gat_w"][:, h * P:(h + 1) * P], start=True, stop=True)
                last.then_inc(projected, 1)


def gru(k, inT, wih, whh, bih, bhh, who):
    nc, ctx = k.nc, ExitStack()
    groups = [(t, min(PER, T - t)) for t in range(0, T, PER)]
    RZ, IN, HN = slice(0, 2 * P), slice(2 * P, 3 * P), slice(3 * P, 4 * P)
    with ctx:
        bias = k.sb(f"gru_bias_{who}", [P, 4 * P], ctx=ctx)
        gate = k.sb(f"gru_gate_{who}", [P, PER, 4 * P], ctx=ctx)
        n_t = k.sb(f"gru_n_{who}", [P, PER, P], ctx=ctx)
        made, added, sig, mixed, tanh, own = (
            k.sem("gru_" + n, ctx) for n in ("made", "added", "sig", "mixed", "tanh", "dve"))
        block = ctx.enter_context(nc.Block())

        @block.tensor
        def _(pe):
            for g, (t0, n) in enumerate(groups):
                if g >= 2:
                    pe.wait_ge(added, g - 1)
                for i in range(n):
                    at, bank = slice((t0 + i) * P, (t0 + i + 1) * P), k.ps[:, (g % 2) * PER + i, :]
                    nc.tensor.matmul(bank[:, RZ], inT[:, at], wih[:, RZ], start=True, stop=False)
                    nc.tensor.matmul(bank[:, RZ], k.hT[:, at], whh[:, RZ], start=False, stop=True)
                    nc.tensor.matmul(bank[:, IN], inT[:, at], wih[:, IN], start=True, stop=True)
                    last = nc.tensor.matmul(bank[:, HN], k.hT[:, at], whh[:, IN], start=True, stop=True)
                last.then_inc(made, 1)

        @block.scalar
        def _(act):
            for g, (t0, n) in enumerate(groups):
                act.wait_ge(added, g + 1)
                nc.scalar.activation(gate[:, 0:n, RZ], gate[:, 0:n, RZ], ACT.Sigmoid).then_inc(sig, 1)
                act.wait_ge(mixed, g + 1)
                nc.scalar.activation(n_t[:, 0:n, :], n_t[:, 0:n, :], ACT.Tanh).then_inc(tanh, 1)

        @block.vector
        def _(dve):
            link = Chain(dve, own)
            nc.vector.tensor_tensor(bias[:, RZ], bih[:, RZ], bhh[:, RZ], ADD)
            nc.vector.tensor_copy(bias[:, IN], bih[:, IN])
            link(nc.vector.tensor_copy(bias[:, HN], bhh[:, IN]))
            for g, (t0, n) in enumerate(groups):
                dve.wait_ge(made, g + 1)
                b0 = (g % 2) * PER
                nc.vector.tensor_tensor(gate[:, 0:n, :], k.ps[:, b0:b0 + n, :],
                                        bias[:, :].unsqueeze(1).to_broadcast([P, n, 4 * P]), ADD).then_inc(added, 1)
                dve.wait_ge(added, g + 1)
                dve.wait_ge(sig, g + 1)
                link(nc.vector.tensor_tensor(n_t[:, 0:n, :], gate[:, 0:n, 0:P], gate[:, 0:n, HN], MUL))
                nc.vector.tensor_tensor(n_t[:, 0:n, :], n_t[:, 0:n, :], gate[:, 0:n, IN], ADD).then_inc(mixed, 1)
                dve.wait_ge(tanh, g + 1)
                link(nc.vector.tensor_tensor(gate[:, 0:n, IN], k.h[:, t0:t0 + n, :], n_t[:, 0:n, :], SUB))
                link(nc.vector.tensor_tensor(gate[:, 0:n, IN], gate[:, 0:n, IN], gate[:, 0:n, P:2 * P], MUL))
                link(nc.vector.tensor_tensor(gate[:, 0:n, IN], gate[:, 0:n, IN], n_t[:, 0:n, :], ADD))
                link(nc.vector.tensor_tensor(gate[:, 0:n, IN], gate[:, 0:n, IN], bcast(k.diag[:, t0:t0 + n], P), MUL))
                link(nc.vector.tensor_tensor(k.x[:, t0:t0 + n, :], k.x[:, t0:t0 + n, :], gate[:, 0:n, IN], ADD))


def layer2(k, c):
    nc = k.nc
    H = L2_HEADS
    with ExitStack() as ctx:
        not_ident = k.sb("not_ident", [P, P], ctx=ctx)
        nsT = k.sb("l2_nsT", [P, NP], ctx=ctx)
        et = k.sb("l2_et", [P, T * 2 * H], ctx=ctx)
        tau = k.sb("l2_tau", [P, 1], ctx=ctx)
        top = k.sb("l2_top", [P, 1], ctx=ctx)
        yt = k.sb("l2_yt", [P, T, 2 * H], BF16, ctx=ctx)
        guards = k.sb("l2_guards", [P, T * H], ctx=ctx)
        with ExitStack() as inner:
            spT = k.sb("l2_spT", [P, NP], ctx=inner)
            smT = k.sb("l2_smT", [P, NP], ctx=inner)
            hs = k.sb("l2_hs", [P, T, 3, P], BF16, ctx=inner)
            with ExitStack() as first:
                rest = k.sb("l2_rest", [P, T, P], ctx=first)
                own = k.sem("l2_dve", first)
                block = first.enter_context(nc.Block())

                @block.vector
                def _(dve):
                    link = Chain(dve, own)
                    link(nc.vector.tensor_scalar(not_ident[:, :], k.ident[:, :], -1.0, 1.0, MUL, ADD))
                    link(nc.vector.tensor_copy(rest[:, :, :], k.h[:, :, :]))
                    split_bf16(link, nc, [hs[:, :, n, :] for n in range(3)], rest[:, :, :])
            signed_sums(k, hs, not_ident, nsT, spT, smT)
            attention_logits(k, c, spT, smT, et, tau, top, yt)
        row_guards(k, not_ident, yt, tau, top, guards)
        es = k.sb("l2_es", [P, T, P], ctx=ctx)
        with ExitStack() as inner:
            gb = k.sb("l2_gb", [P, H, NP], ctx=inner)
            spread_rows(k, lambda t, h: guards[:, t * H + h:t * H + h + 1], gb, "l2")
            signed_attention(k, c, not_ident, et, gb, es)
        gru(k, nsT, c["ewihT"], c["ewhhT"], c["ebih"], c["ebhh"], "edge")
        to_features(k, es, nsT, "l2")
        gru(k, nsT, c["nwihT"], c["nwhhT"], c["nbih"], c["nbhh"], "node")


def random_walk(k, xf, rdeg, u1T, z, first):
    nc = k.nc
    with ExitStack() as ctx:
        agg = k.sb(f"rw_agg_{first}", [P, NP], ctx=ctx)
        taken_dve, taken_act, made, read = (
            k.sem("rw_" + n, ctx) for n in ("taken_dve", "taken_act", "made", "read"))
        block = ctx.enter_context(nc.Block())
        pairs = [(t, min(2, T - t)) for t in range(0, T, 2)]

        @block.scalar
        def _(act):
            for b, col, w in BANKS[1::2]:
                nc.scalar.copy(agg[:, col:col + w], k.psf[:, col:col + w]).then_inc(taken_act, 1)

        @block.tensor
        def _(pe):
            pe.wait_ge(taken_dve, len(BANKS[0::2]))
            pe.wait_ge(taken_act, len(BANKS[1::2]))
            for g, (t0, n) in enumerate(pairs):
                if g >= 8:
                    pe.wait_ge(read, g - 7)
                for i in range(n):
                    at = slice((t0 + i) * P, (t0 + i + 1) * P)
                    for m, mat in enumerate((u1T, k.ident[:, :])):
                        last = nc.tensor.matmul(k.ps[:, g % 8, (2 * i + m) * P:(2 * i + m + 1) * P], agg[:, at], mat,
                                                start=True, stop=True)
                last.then_inc(made, 1)

        @block.vector
        def _(dve):
            for b, col, w in BANKS[0::2]:
                nc.vector.tensor_copy(agg[:, col:col + w], k.psf[:, col:col + w]).then_inc(taken_dve, 1)
            for g, (t0, n) in enumerate(pairs):
                dve.wait_ge(made, g + 1)
                for i in range(n):
                    t = t0 + i
                    scale = rdeg[:, t:t + 1]
                    product = k.ps[:, g % 8, 2 * i * P:(2 * i + 1) * P]
                    if first:
                        nc.vector.tensor_scalar(z[:, t, :], product, scale, None, MUL)
                    else:
                        nc.vector.scalar_tensor_tensor(z[:, t, :], product, scale, z[:, t, :], MUL, ADD)
                    last = nc.vector.tensor_scalar(xf[:, t, :], k.ps[:, g % 8, (2 * i + 1) * P:(2 * i + 2) * P], scale,
                                                   None, MUL)
                last.then_inc(read, 1)


def queries_and_keys(k, c, xaT, q1T, qT, kT, who):
    nc = k.nc
    with ExitStack() as ctx:
        made, taken_dve, taken_act = (k.sem("qk_" + n, ctx) for n in ("made", "taken_dve", "taken_act"))
        block = ctx.enter_context(nc.Block())
        jobs = [(c["l3w1T"], xaT, q1T), (c["l3w3T"], xaT, kT), (c["l3w2T"], q1T, qT)]
        EVEN, ODD = len(BANKS[0::2]), len(BANKS[1::2])

        @block.tensor
        def _(pe):
            for n, (w, source, _) in enumerate(jobs):
                if n == 2:
                    pe.wait_ge(taken_dve, EVEN)
                    pe.wait_ge(taken_act, ODD)
                for b, col, wd in BANKS:
                    if n and b % 2 == 0:
                        pe.wait_ge(taken_dve, (n - 1) * EVEN + b // 2 + 1)
                    elif n:
                        pe.wait_ge(taken_act, (n - 1) * ODD + b // 2 + 1)
                    nc.tensor.matmul(k.psf[0:D_ATTN, col:col + wd], w[:], source[:, col:col + wd], start=True,
                                     stop=True).then_inc(made, 1)

        @block.vector
        def _(dve):
            for n, (_, _, dest) in enumerate(jobs):
                for b, col, wd in BANKS[0::2]:
                    dve.wait_ge(made, n * NB + b + 1)
                    nc.vector.tensor_copy(dest[:, col:col + wd], k.psf[0:D_ATTN, col:col + wd]).then_inc(taken_dve, 1)

        @block.scalar
        def _(act):
            for n, (_, _, dest) in enumerate(jobs):
                for b, col, wd in BANKS[1::2]:
                    act.wait_ge(made, n * NB + b + 1)
                    nc.scalar.copy(dest[:, col:col + wd], k.psf[0:D_ATTN, col:col + wd]).then_inc(taken_act, 1)


def top_p_attention(k, qT, kT, xa, out, who):
    nc, ctx = k.nc, ExitStack()
    from math import exp
    half_range = [SEARCH_SPAN / 2 ** (n + 1) for n in range(ALL_ROUNDS + 1)]
    groups = [(g, g * PER, min(PER, T - g * PER)) for g in range(NB)]
    LB, TB, OB = 0, 4, 6
    SLOTS, PAIRS = 4, T // 2
    SHARED, FILL = 11, 1
    MIDWAY = SEARCH_ROUNDS // 2
    TURNED_B, LOGITS_B, TURNED_A, LOGITS_A = 0, 6, 10, 16
    with ctx:
        p = k.sb(f"ta_p_{who}", [P, SLOTS, NP], ctx=ctx)
        chosen = k.sb(f"ta_chosen_{who}", [P, NODES], ctx=ctx)
        junk = k.sb(f"ta_junk_{who}", [P, NODES], BF16, ctx=ctx)
        pT = k.sb(f"ta_pT_{who}", [P, T, P], ctx=ctx)
        qs = k.sb(f"ta_q_{who}", [D_ATTN, 2, P], ctx=ctx)
        small = lambda name, n, dt=F32: k.sb(f"ta_{name}_{who}", [P, n], dt, ctx=ctx)
        top, total, goal, thr, rden = (small(n, SLOTS) for n in ("top", "total", "goal", "thr", "rden"))
        reach, step, least, high, below, need, cut, flag = (
            small(n, 1) for n in ("reach", "step", "least", "high", "below", "need", "cut", "flag"))
        best, sums, sums2 = (small(n, 12) for n in ("best", "sums", "sums2"))
        hits = small("hits", 8)
        flag_row, open_rows = small("flag_row", P), small("open_rows", 1, mybir.dt.int32)
        neg_thr, neg_goal = small("neg_thr", SLOTS), small("neg_goal", SLOTS)
        signs, excess, count, product, neg_reach, pstep, neg_share, halves = (small(n, 1) for n in (
            "signs", "excess", "count", "product", "neg_reach", "pstep", "neg_share", "halves"))
        names = ("padded", "q_ready", "logits", "copied", "topped", "exped", "masked", "turned", "taken", "multiplied",
                 "out_read", "own", "own_pool", "passed", "decided", "flagged", "flag_moved", "further")
        (padded, q_ready, logits, copied, topped, exped, masked, turned, taken, multiplied, out_read, own, own_pool,
         passed, decided, flagged, flag_moved, further) = (k.sem("ta_" + n, ctx) for n in names)
        block = ctx.enter_context(nc.Block())
        LOOPED = (PAIRS - 3) // 2
        assert PAIRS == 3 + 2 * LOOPED

        def pairs(engine, body, chain=None, links=0):
            body(0, 0, 0)
            with engine.Fori(0, LOOPED) as n:
                if chain:
                    chain.enter(n, links)
                body(n * 2 + 1, n * 4 + 2, 2)
                body(n * 2 + 2, n * 4 + 4, 0)
            if chain:
                chain.leave(LOOPED)
            body(PAIRS - 2, T - 4, (T - 4) % SLOTS)
            body(PAIRS - 1, T - 2, (T - 2) % SLOTS)

        def has(i):
            return not isinstance(i, int) or 0 <= i < T

        def late(i, first):
            return not isinstance(i, int) or i >= first

        @block.sync
        def _(sp):
            def move_flags(i):
                sp.wait_ge(flagged, i + 1)
                sp.dma_start(flag_row[0:1, :], flag[:, 0:1]).then_inc(flag_moved, 16)
            with sp.Fori(0, T) as i:
                move_flags(i)

        @block.gpsimd
        def _(pool):
            def pick(i, slot):
                if late(i, 2):
                    pool.wait_ge(logits, i * NB - NB)
                nc.gpsimd.tensor_copy(qs[:, slot % 2, :], qT[:, ds(i * P, P)]).then_inc(q_ready, 1)

            def decide(r, i, s):
                at = slice(s, s + 1)
                pool.sem_clear(own_pool)
                link = Chain(pool, own_pool)
                pool.wait_ge(exped, i + 1)
                link(nc.gpsimd.tensor_tensor(neg_goal[:, at], total[:, at], neg_share[:, :], MUL))
                nc.gpsimd.memset(neg_thr[:, at], -exp(-half_range[0])).then_inc(decided, 1)
                for n in range(SHARED):
                    before = r * (2 * SHARED) - 2 * SHARED + 2 * n
                    pool.wait_ge(passed, before + 1)
                    link(nc.gpsimd.tensor_tensor(count[:, :], signs[:, :], halves[:, :], MUL))
                    link(nc.gpsimd.tensor_scalar(product[:, :], count[:, :], NODES / 2, neg_thr[:, at], ADD, MUL))
                    pool.wait_ge(passed, before + 2)
                    link(nc.gpsimd.tensor_tensor(neg_reach[:, :], product[:, :], excess[:, :], SUB))
                    up, down = exp(half_range[n + 1]), exp(-half_range[n + 1])
                    link(nc.gpsimd.tensor_scalar(pstep[:, :], neg_reach[:, :], neg_goal[:, at], up - down, ALU.is_le,
                                                 MUL))
                    nc.gpsimd.tensor_scalar(neg_thr[:, at], pstep[:, :], down, neg_thr[:, at], ADD, MUL
                                            ).then_inc(decided, 1)

            link = Chain(pool, own_pool)
            link(nc.gpsimd.memset(neg_share[:, :], -TOP_P))
            link(nc.gpsimd.memset(halves[:, :], 0.5))
            for i in range(3):
                pick(i, i)

            def pair(r, a, s):
                for o in (3, 4):
                    if has(a + o):
                        pick(a + o, s + o)
                if has(a + 2):
                    decide(r + 1, a + 2, (s + 2) % SLOTS)
            pairs(pool, pair)

        @block.tensor
        def _(pe):
            def make_logits(i, slot):
                pe.wait_ge(q_ready, i + 1)
                for b, col, w in BANKS:
                    if late(i, 1) or b >= 4:
                        pe.wait_ge(copied, i * NB + (b - 3))
                    nc.tensor.matmul(k.ps[:, LB + (slot * NB + b) % 4, 0:w], qs[:, slot % 2, :], kT[:, col:col + w],
                                     start=True, stop=True).then_inc(logits, 1)

            def turn_and_multiply(i, slot):
                pe.wait_ge(masked, i + 1)
                for g, t0, n in groups:
                    if late(i, 1) or g >= 2:
                        pe.wait_ge(taken, i * NB + (g - 1))
                    for t in range(n):
                        last = nc.tensor.transpose(k.ps[:, TB + (slot * NB + g) % 2, t * P:(t + 1) * P],
                                                   p[:, slot, (t0 + t) * P:(t0 + t + 1) * P], k.ident[:, :])
                    last.then_inc(turned, 1)
                if late(i, 2):
                    pe.wait_ge(out_read, i - 1)
                for g, t0, n in groups:
                    pe.wait_ge(taken, i * NB + (g + 1))
                    for j in range(t0, t0 + n):
                        last = nc.tensor.matmul(k.ps[:, OB + slot % 2, 0:P], pT[:, j, :], xa[:, j, :], start=j == 0,
                                                stop=j == T - 1)
                last.then_inc(multiplied, 1)

            for i in range(3):
                make_logits(i, i)

            def pair(r, a, s):
                if late(a, 1):
                    turn_and_multiply(a - 1, (s - 1) % SLOTS)
                if has(a + 3):
                    make_logits(a + 3, (s + 3) % SLOTS)
                turn_and_multiply(a, s)
                if has(a + 4):
                    make_logits(a + 4, s)
            pairs(pe, pair)
            turn_and_multiply(T - 1, (T - 1) % SLOTS)

        @block.scalar
        def _(act):
            def copy_logits(i, slot, banks=BANKS):
                for b, col, w in banks:
                    act.wait_ge(logits, i * NB + (b + 1))
                    if b == 0 and late(i, SLOTS):
                        act.wait_ge(turned, i * NB - (SLOTS - 1) * NB)
                    w = min(w, NODES - col)
                    nc.scalar.copy(p[:, slot, col:col + w], k.ps[:, LB + (slot * NB + b) % 4, 0:w]).then_inc(copied, 1)

            def copy_turned(i, slot, some=groups):
                for g, t0, n in some:
                    act.wait_ge(turned, i * NB + (g + 1))
                    if g == 0 and late(i, 1):
                        act.wait_ge(multiplied, i)
                    nc.scalar.copy(pT[:, t0:t0 + n, :].rearrange("p t c -> p (t c)"),
                                   k.ps[:, TB + (slot * NB + g) % 2, 0:n * P]).then_inc(taken, 1)

            def exponentials(i, slot):
                act.wait_ge(topped, i + 1)
                nc.scalar.activation(p[:, slot, 0:NODES], p[:, slot, 0:NODES], ACT.Exp, bias=top[:, slot:slot + 1],
                                     accum_out=total[:, slot:slot + 1]).then_inc(exped, 1)

            act.wait_ge(padded, 1)
            for i in range(3):
                copy_logits(i, i)
            exponentials(0, 0)

            def pair(r, a, s):
                def take_over(step):
                    if 0 <= step - TURNED_B < 4 and late(a, 1):
                        n = 2 * (step - TURNED_B)
                        copy_turned(a - 1, (s - 1) % SLOTS, groups[n:n + 2])
                    if 0 <= step - LOGITS_B < 3 and has(a + 3):
                        n = 2 * (step - LOGITS_B) + 1
                        copy_logits(a + 3, (s + 3) % SLOTS, BANKS[n if n > 1 else 0:n + 2])
                    if 0 <= step - TURNED_A < 4:
                        n = 2 * (step - TURNED_A)
                        copy_turned(a, s, groups[n:n + 2])
                    if 0 <= step - LOGITS_A < 3 and has(a + 4):
                        n = 2 * (step - LOGITS_A) + 1
                        copy_logits(a + 4, s, BANKS[n if n > 1 else 0:n + 2])

                exponentials(a + 1, (s + 1) % SLOTS)
                if has(a + 2):
                    exponentials(a + 2, (s + 2) % SLOTS)
                slot = (s + 2) % SLOTS
                at = slice(slot, slot + 1)
                for n in range(SHARED):
                    if has(a + 2):
                        act.wait_ge(exped, a + 3)
                        if late(r, 1) or n > 0:
                            act.wait_ge(passed, r * (2 * SHARED) + 2 * n)
                        act.wait_ge(decided, r * (SHARED + 1) + (n + 1))
                        nc.scalar.activation(junk[:, :], p[:, slot, 0:NODES], ACT.Sign, bias=neg_thr[:, at],
                                             accum_out=signs[:, 0:1]).then_inc(passed, 1)
                    take_over(2 * n)
                    if has(a + 2):
                        act.wait_ge(passed, r * (2 * SHARED) + (2 * n + 1))
                        nc.scalar.activation(junk[:, :], p[:, slot, 0:NODES], ACT.Relu, bias=neg_thr[:, at],
                                             accum_out=excess[:, 0:1]).then_inc(passed, 1)
                    take_over(2 * n + 1)
            pairs(act, pair)
            copy_turned(T - 1, (T - 1) % SLOTS)

        @block.vector
        def _(dve):
            link = Chain(dve, own)
            nc.vector.memset(p[:, :, NODES:NP], 0.0).then_inc(padded, 1)
            for buffer in (best, sums, sums2):
                link(nc.vector.memset(buffer[:, 0:4], 0.0))

            def largest(i, slot):
                dve.wait_ge(copied, i * NB + NB)
                link(nc.vector.reduce_max(top[:, slot:slot + 1], p[:, slot, 0:NODES], X))
                nc.vector.tensor_scalar(top[:, slot:slot + 1], top[:, slot:slot + 1], -1.0, None, MUL
                                        ).then_inc(topped, 1)

            def search(link, slot, rounds):
                at = slice(slot, slot + 1)
                for n in rounds:
                    link(nc.vector.scalar_tensor_tensor(chosen[:, :], p[:, slot, 0:NODES], thr[:, at],
                                                        p[:, slot, 0:NODES], ALU.is_ge, MUL, accum_out=reach[:, 0:1]))
                    up, down = exp(half_range[n + 1]), exp(-half_range[n + 1])
                    link(nc.vector.tensor_scalar(step[:, :], reach[:, :], goal[:, at], up - down, ALU.is_ge, MUL))
                    link(nc.vector.scalar_tensor_tensor(thr[:, at], step[:, :], down, thr[:, at], ADD, MUL))

            def begin(slot):
                at = slice(slot, slot + 1)
                link(nc.vector.tensor_scalar(goal[:, at], total[:, at], TOP_P, None, MUL))

            def pick_cut(i, slot):
                at = slice(slot, slot + 1)
                link(nc.vector.tensor_scalar(high[:, :], thr[:, at], exp(half_range[SEARCH_ROUNDS]) * (1 + 1e-5), None,
                                             MUL))
                link(nc.vector.scalar_tensor_tensor(chosen[:, :], p[:, slot, 0:NODES], high[:, 0:1],
                                                    p[:, slot, 0:NODES], ALU.is_lt, MUL, accum_out=below[:, 0:1]))
                link.count(nc.vector.scalar_tensor_tensor(need[:, :], below[:, :], total[:, at], goal[:, at], SUB, ADD))
                link(nc.vector.max(out=best[:, 4:12], in_=chosen[:, :]))
                link(nc.vector.tensor_tensor(sums[:, 4:12], best[:, 4:12], best[:, 3:11], ADD))
                link(nc.vector.tensor_tensor(sums2[:, 4:12], sums[:, 4:12], sums[:, 2:10], ADD))
                link(nc.vector.tensor_tensor(sums[:, 4:12], sums2[:, 4:12], sums2[:, 0:8], ADD))
                link(nc.vector.scalar_tensor_tensor(hits[:, :], sums[:, 4:12], need[:, 0:1], best[:, 4:12],
                                                    ALU.is_ge, MUL))
                link(nc.vector.reduce_max(cut[:, :], hits[:, :], X))
                link(nc.vector.tensor_tensor(need[:, :], need[:, :], cut[:, :], MIN))
                nc.vector.tensor_scalar(flag[:, :], need[:, :], 0.0, None, ALU.is_le).then_inc(flagged, 1)

            def go_further(i, slot):
                at = slice(slot, slot + 1)
                dve.wait_ge(flag_moved, i * 16 + 16)
                link(nc.vector.reduce_max(open_rows[0:1, :], flag_row[0:1, :], X))
                nc.vector.tensor_scalar(least[:, :], total[:, at], 1e-12, None, MUL)
                some = dve.value_load(open_rows[0:1, 0:1], min_val=0, max_val=1)
                with dve.If(some > 0):
                    dve.sem_clear(further)
                    chain = Chain(dve, further)
                    search(chain, slot, range(SEARCH_ROUNDS, ALL_ROUNDS))
                    chain(nc.vector.tensor_scalar(cut[:, :], thr[:, at], exp(-half_range[ALL_ROUNDS]), None, MUL))

            def mask(i, slot):
                at = slice(slot, slot + 1)
                nc.vector.scalar_tensor_tensor(p[:, slot, 0:NODES], p[:, slot, 0:NODES], cut[:, 0:1],
                                               p[:, slot, 0:NODES], ALU.is_ge, MUL, accum_out=rden[:, at]
                                               ).then_inc(masked, 1)
                dve.wait_ge(masked, i + 1)
                link(nc.vector.tensor_tensor(rden[:, at], rden[:, at], least[:, :], MAX))
                link(nc.vector.reciprocal(rden[:, at], rden[:, at]))

            def read_out(i, slot):
                dve.wait_ge(multiplied, i + 1)
                nc.vector.tensor_scalar(out[:, ds(i, 1), :].rearrange("p o c -> p (o c)"), k.ps[:, OB + slot % 2, 0:P],
                                        rden[:, slot:slot + 1], None, MUL).then_inc(out_read, 1)

            for i in range(3):
                largest(i, i)

            def pair(r, a, s):
                b, sb = a + 1, (s + 1) % SLOTS
                if late(a, 1):
                    dve.wait_ge(decided, r * (SHARED + 1))
                    begin(s)
                    link(nc.vector.tensor_scalar(thr[:, s:s + 1], neg_thr[:, s:s + 1], -1.0, None, MUL))
                    search(link, s, range(SHARED, SEARCH_ROUNDS))
                else:
                    dve.wait_ge(exped, 1)
                    begin(s)
                    link(nc.vector.memset(thr[:, s:s + 1], exp(-half_range[0])))
                    search(link, s, range(SEARCH_ROUNDS))
                pick_cut(a, s)
                dve.wait_ge(exped, b + 1)
                begin(sb)
                link(nc.vector.memset(thr[:, sb:sb + 1], exp(-half_range[0])))
                search(link, sb, range(FILL))
                go_further(a, s)
                mask(a, s)
                if late(a, 1):
                    read_out(a - 1, (s - 1) % SLOTS)
                search(link, sb, range(FILL, MIDWAY))
                if has(a + 3):
                    largest(a + 3, (s + 3) % SLOTS)
                search(link, sb, range(MIDWAY, SEARCH_ROUNDS))
                pick_cut(b, sb)
                read_out(a, s)
                if has(a + 4):
                    largest(a + 4, s)
                go_further(b, sb)
                mask(b, sb)
            A_LINKS = 2 + 3 * (SEARCH_ROUNDS - SHARED)
            BOTH = 10 + 1 + 2
            B_LINKS = 2 + 3 * SEARCH_ROUNDS + 2
            pairs(dve, pair, link, 2 * (A_LINKS + B_LINKS + 2 * BOTH))
            read_out(T - 1, (T - 1) % SLOTS)


def add_product(k, sourceT, w, z, who):
    nc = k.nc
    with ExitStack() as ctx:
        made = k.sem("ap_made", ctx)
        block = ctx.enter_context(nc.Block())

        @block.tensor
        def _(pe):
            for b, col, wd in BANKS:
                for t in range(col // P, (col + wd) // P):
                    last = nc.tensor.matmul(k.psf[:, t * P:(t + 1) * P], sourceT[:, t * P:(t + 1) * P], w, start=True,
                                            stop=True)
                last.then_inc(made, 1)

        @block.vector
        def _(dve):
            for b, col, wd in BANKS:
                dve.wait_ge(made, b + 1)
                zs = z[:, col // P:(col + wd) // P, :]
                nc.vector.tensor_tensor(zs, zs, k.psf[:, col:col + wd].rearrange("p (t c) -> p t c", c=P), ADD)


def layer3(k, c):
    nc = k.nc
    with ExitStack() as ctx:
        z = k.sb("l3_z", [P, T, P], ctx=ctx)
        rdeg = k.sb("l3_rdeg", [P, T], ctx=ctx)
        xf = k.sb("l3_xf", [P, T, P], ctx=ctx)
        with ExitStack() as inner:
            own = k.sem("l3_own", inner)
            block = inner.enter_context(nc.Block())

            @block.vector
            def _(dve):
                link = Chain(dve, own)
                link(nc.vector.tensor_scalar(rdeg[:, :], k.deg[:, :], 1.0, None, ADD))
                link(nc.vector.reciprocal(rdeg[:, :], rdeg[:, :]))
        for n in range(STEPS):
            propagate(k, xf if n else k.h, f"walk{n}", self_loops=True)
            random_walk(k, xf, rdeg, c["u1T"][:, n * P:(n + 1) * P], z, n == 0)
        xa, new = k.h, xf
        for n in range(STEPS):
            with ExitStack() as inner:
                qT = k.sb(f"l3_qT{n}", [D_ATTN, NP], ctx=inner)
                kT = k.sb(f"l3_kT{n}", [D_ATTN, NP], ctx=inner)
                with ExitStack() as first:
                    q1T = k.sb(f"l3_q1T{n}", [D_ATTN, NP], ctx=first)
                    queries_and_keys(k, c, k.hT, q1T, qT, kT, n)
                if n == 0:
                    with ExitStack() as first:
                        block = first.enter_context(nc.Block())

                        @block.vector
                        def _(dve):
                            nc.vector.tensor_tensor(z[:, :, :], z[:, :, :], k.h[:, :, :], ADD)
                top_p_attention(k, qT, kT, xa, new, n)
            to_features(k, new, k.hT, f"l3{n}")
            add_product(k, k.hT, c["u2T"][:, n * P:(n + 1) * P], z, n)
            xa, new = new, xa
        layer_norm(k, "l3_out", source=z, affine=(c["ln_g"], c["ln_b"]))


def build(nc, d, out, upto=9):
    ctx = ExitStack()
    with ctx:
        k = Kernel(nc, ctx, d, out)
        c = {n: k.sb(n + "_sb", list(s)) for n, s in dict(
            w0T=(P, P), w1=(P, P), w1T=(P, P), gat_w=(P, L2_HEADS * P), gat_wT=(P, L2_HEADS * P),
            gat_a=(P, 2 * L2_HEADS), ewihT=(P, 3 * P), ewhhT=(P, 3 * P), nwihT=(P, 3 * P), nwhhT=(P, 3 * P),
            l3w1T=(P, D_ATTN), l3w2T=(D_ATTN, D_ATTN), l3w3T=(P, D_ATTN), u1T=(P, STEPS * P), u2T=(P, STEPS * P),
            b0=(P, P), ebih=(P, 3 * P), ebhh=(P, 3 * P), nbih=(P, 3 * P), nbhh=(P, 3 * P), ln_g=(P, P), ln_b=(P, P),
            a_blocks=(P, 2 * L1_HEADS)).items()}
        load_constants(k, c)
        layer_norm(k, "l0")
        if upto >= 1:
            layer0(k, c)
        if upto >= 2:
            layer_norm(k, "l1")
            layer1(k, c)
        clear_semaphores(k)
        if upto >= 3:
            layer_norm(k, "l2")
            layer2(k, c)
        clear_semaphores(k)
        if upto >= 4:
            layer_norm(k, "l3")
            layer3(k, c)
        store(k)


def store(k):
    nc = k.nc
    with ExitStack() as ctx:
        stored = k.sem("stored", ctx)
        block = ctx.enter_context(nc.Block())

        @block.sync
        def _(sp):
            sp.dma_start(k.out, k.x[:, :, :]).then_inc(stored, 16)
            sp.wait_ge(stored, 16)


def kernel(**inputs):
    import numpy as np
    import concourse.bacc as bacc
    from concourse.bass_utils import run_bass_kernel_spmd

    def packed(a):
        return np.ascontiguousarray(a.reshape(T, P, -1).transpose(1, 0, 2))

    g = {n: np.asarray(a) for n, a in inputs.items()}
    pad = NP - NODES
    adj = np.pad(g["adj"], ((0, pad), (0, pad)))
    row = lambda n: np.ascontiguousarray(g[n].reshape(1, -1))
    turn = lambda n: np.ascontiguousarray(g[n].T)
    side = lambda a: np.ascontiguousarray(np.concatenate(list(a), axis=1))
    arrays = dict(
        x=packed(np.pad(g["x"], ((0, pad), (0, 0)))), adj=adj, adjT=np.ascontiguousarray(adj.T),
        diag=packed(np.diagonal(adj)).reshape(P, T),
        w0T=turn("L0_gnn_W"), b0=row("L0_gnn_b"), w1=g["L1_gnn_W"], w1T=turn("L1_gnn_W"),
        a_l=g["L1_gnn_a_l"].reshape(-1, 1), a_r=g["L1_gnn_a_r"].reshape(-1, 1),
        gat_w=side(g["L2_gnn_gat_W"]), gat_wT=side(g["L2_gnn_gat_W"].transpose(0, 2, 1)),
        gat_a=np.ascontiguousarray(g["L2_gnn_gat_a"].reshape(L2_HEADS, 2, P).transpose(2, 0, 1).reshape(P, -1)),
        ewihT=turn("L2_gnn_edge_Wih"), ewhhT=turn("L2_gnn_edge_Whh"), nwihT=turn("L2_gnn_node_Wih"),
        nwhhT=turn("L2_gnn_node_Whh"), ebih=row("L2_gnn_edge_bih"), ebhh=row("L2_gnn_edge_bhh"),
        nbih=row("L2_gnn_node_bih"), nbhh=row("L2_gnn_node_bhh"), ln_g=row("L3_gnn_ln_g"), ln_b=row("L3_gnn_ln_b"),
        l3w1T=turn("L3_gnn_W1"), l3w2T=turn("L3_gnn_W2"), l3w3T=turn("L3_gnn_W3"),
        u1T=side(g["L3_gnn_U1"].transpose(0, 2, 1)), u2T=side(g["L3_gnn_U2"].transpose(0, 2, 1)))
    arrays = {n: np.ascontiguousarray(a) for n, a in arrays.items()}
    nc = bacc.Bacc("TRN2", target_bir_lowering=False, num_devices=1)
    d = {n: nc.dram_tensor(f"in_{n}", a.shape, mybir.dt.from_np(a.dtype), kind="ExternalInput").ap()
         for n, a in arrays.items()}
    out = nc.dram_tensor("out_x", (P, T, P), F32, kind="ExternalOutput").ap()
    build(nc, d, out)
    r = run_bass_kernel_spmd(nc, [{f"in_{n}": a for n, a in arrays.items()}], core_ids=[0])
    return np.ascontiguousarray(r.results[0]["out_x"].transpose(1, 0, 2).reshape(NP, P)[:NODES])
```

```python
import concourse.bass as bass
from concourse import mybir
from contextlib import ExitStack

F32 = mybir.dt.float32
BF16 = mybir.dt.bfloat16
ALU = mybir.AluOpType
ACT = mybir.ActivationFunctionType
X = mybir.AxisListType.X
ADD, SUB, MUL, MAX, MIN = ALU.add, ALU.subtract, ALU.mult, ALU.max, ALU.min
ds = bass.ds

P = 128
NODES = 3327
T = (NODES + P - 1) // P
NP = T * P
BANK = 512
NB = (NP + BANK - 1) // BANK
PER = BANK // P
BANKS = [(b, b * BANK, min(BANK, NP - b * BANK)) for b in range(NB)]
LN_EPS = 1e-5
L1_HEADS, L1_D = 4, 32
L1_SLOPE = 0.2
L2_HEADS = 3
L2_ALPHA = 0.2
CHUNKS = [(0, 7), (7, 7), (14, 6), (20, 6)]
WMAX = max(n for _, n in CHUNKS)
D_ATTN, STEPS, TOP_P = 64, 2, 0.9
SEARCH_SPAN = 10.42
SEARCH_ROUNDS = ((10, 9), (13, 12))
ALL_ROUNDS = 22


class Chain:

    def __init__(self, engine, sem):
        self.engine, self.sem, self.base, self.k, self.i, self.per = engine, sem, 0, 0, None, 0

    def count(self, ins):
        self.k += 1
        ins.then_inc(self.sem, 1)

    def __call__(self, ins):
        self.count(ins)
        at = self.base + self.k
        if self.i is not None:
            at = at + self.i * self.per
        self.engine.wait_ge(self.sem, at)
        return ins

    def enter(self, i, per):
        assert self.i is None
        self.base, self.k, self.i, self.per = self.base + self.k, 0, i, per

    def leave(self, rounds):
        assert self.k == self.per, (self.k, self.per)
        self.base, self.k, self.i = self.base + rounds * self.per, 0, None


def tiles(ap):
    return ap.rearrange("p (t c) -> p t c", t=T)


class Kernel:

    def __init__(self, nc, ctx, d, out):
        self.nc, self.ctx, self.d, self.out = nc, ctx, d, out
        self.names = {}
        self.counted = []
        sb = self.sb
        self.ps = ctx.enter_context(nc.psum_tensor("psum", [P, 8, BANK], F32))
        self.psf = self.ps[:, :, :].rearrange("p b c -> p (b c)")
        self.x = sb("x", [P, T, P])
        self.h = sb("h", [P, T, P])
        self.hT = sb("hT", [P, NP])
        self.ident = sb("ident", [P, P])
        self.deg = sb("deg", [P, T])
        self.diag = sb("diag", [P, T])
        self.signed = sb("signed", [P, 1], mybir.dt.int32)
        self.s1 = sb("s1", [P, T])
        self.s2 = sb("s2", [P, T])
        self.s3 = sb("s3", [P, T])
        self.s4 = sb("s4", [P, T])

    def sb(self, name, shape, dt=F32, ctx=None):
        return (ctx or self.ctx).enter_context(self.nc.sbuf_tensor(name, shape, dt))

    def sem(self, name, ctx):
        n = self.names[name] = self.names.get(name, 0) + 1
        handle = ctx.enter_context(self.nc.semaphore(f"{name}_{n}"))
        self.counted.append(handle)
        return handle


def clear_semaphores(k):
    with k.nc.Block() as block:
        @block.gpsimd
        def _(pool):
            for handle in k.counted:
                pool.sem_clear(handle)
    k.counted = []


def bcast(ap, n):
    return ap.unsqueeze(2).to_broadcast([ap.shape[0], ap.shape[1], n])


def layer_norm(k, who, source=None, affine=None):
    nc, ctx = k.nc, ExitStack()
    source = k.x if source is None else source
    with ctx:
        xc = k.sb(f"ln_centred_{who}", [P, T, P], ctx=ctx)
        sq = k.sb(f"ln_squares_{who}", [P, T, P], ctx=ctx)
        centred, squared, var_ready, root_ready, h_ready = (
            k.sem(n, ctx) for n in ("ln_centred", "ln_squared", "ln_var", "ln_root", "ln_h"))
        turned, taken_dve, taken_act = (k.sem(n, ctx) for n in ("ln_turned", "ln_taken_dve", "ln_taken_act"))
        own, own_act = k.sem("ln_dve", ctx), k.sem("ln_act", ctx)
        block = ctx.enter_context(nc.Block())

        @block.vector
        def _(dve):
            link = Chain(dve, own)
            link(nc.vector.reduce_sum(k.s1[:, :], source[:, :, :], X))
            link(nc.vector.tensor_scalar(k.s1[:, :], k.s1[:, :], 1.0 / P, None, MUL))
            nc.vector.tensor_tensor(xc[:, :, :], source[:, :, :], bcast(k.s1[:, :], P), SUB).then_inc(centred, 1)
            dve.wait_ge(squared, 1)
            link(nc.vector.reduce_sum(k.s2[:, :], sq[:, :, :], X))
            nc.vector.tensor_scalar(k.s2[:, :], k.s2[:, :], 1.0 / P, LN_EPS, MUL, ADD).then_inc(var_ready, 1)
            dve.wait_ge(var_ready, 1)
            dve.wait_ge(root_ready, 1)
            link(nc.vector.reciprocal(k.s4[:, :], k.s3[:, :]))
            link(nc.vector.tensor_tensor(k.s4[:, :], k.s4[:, :], k.s2[:, :], MUL))
            link(nc.vector.tensor_tensor(k.s4[:, :], k.s4[:, :], k.s3[:, :], ADD))
            link(nc.vector.tensor_scalar(k.s4[:, :], k.s4[:, :], 0.5, None, MUL))
            link(nc.vector.reciprocal(k.s4[:, :], k.s4[:, :]))
            if affine:
                gain, shift = (v[:, :].unsqueeze(1).to_broadcast([P, T, P]) for v in affine)
                link(nc.vector.tensor_tensor(xc[:, :, :], xc[:, :, :], bcast(k.s4[:, :], P), MUL))
                link(nc.vector.tensor_tensor(xc[:, :, :], xc[:, :, :], gain, MUL))
                link(nc.vector.tensor_tensor(xc[:, :, :], xc[:, :, :], shift, ADD))
                link(nc.vector.tensor_tensor(k.x[:, :, :], k.x[:, :, :], xc[:, :, :], ADD))
                return
            nc.vector.scalar_tensor_tensor(k.h[:, :, :], xc[:, :, :], 0.0, bcast(k.s4[:, :], P),
                                           MAX, MUL).then_inc(h_ready, 1)
            for b, c, w in BANKS[0::2]:
                dve.wait_ge(turned, b + 1)
                last = nc.vector.tensor_copy(k.hT[:, c:c + w], k.psf[:, c:c + w])
            last.then_inc(taken_dve, 1)

        @block.scalar
        def _(act):
            act.wait_ge(centred, 1)
            nc.scalar.activation(sq[:, :, :], xc[:, :, :], ACT.Square).then_inc(squared, 1)
            act.wait_ge(var_ready, 1)
            nc.scalar.activation(k.s3[:, :], k.s2[:, :], ACT.Sqrt).then_inc(root_ready, 1)
            if affine:
                return
            for b, c, w in BANKS[1::2]:
                act.wait_ge(turned, b + 1)
                last = nc.scalar.copy(k.hT[:, c:c + w], k.psf[:, c:c + w])
            last.then_inc(taken_act, 1)

        @block.tensor
        def _(pe):
            if affine:
                return
            pe.wait_ge(h_ready, 1)
            for b, c, w in BANKS:
                for t in range(c // P, (c + w) // P):
                    last = nc.tensor.transpose(k.psf[:, t * P:(t + 1) * P], k.h[:, t, :], k.ident[:, :])
                last.then_inc(turned, 1)


def propagate(k, source, who, ring=3):
    nc, ctx = k.nc, ExitStack()
    first = 2
    assert (T - first) % ring == 0
    rounds = (T - first) // ring
    with ctx:
        a = k.sb(f"pr_adj_{who}", [P, ring, NP], ctx=ctx)
        v = k.sb(f"pr_source_{who}", [P, ring, P], ctx=ctx)
        loaded = [k.sem(f"pr_loaded{u}", ctx) for u in range(ring)]
        picked, used = k.sem("pr_picked", ctx), k.sem("pr_used", ctx)
        block = ctx.enter_context(nc.Block())

        def steps(engine, body):
            for j in range(first):
                body(j, j % ring, 0)
            with engine.Fori(0, rounds) as r:
                for u in range(ring):
                    slot = (first + u) % ring
                    body(r * ring + (first + u), slot, r + (first + u) // ring)

        @block.sync
        def _(sp):
            def load(j, slot, before):
                if not isinstance(j, int) or j >= ring:
                    sp.wait_ge(used, j - (ring - 1))
                sp.dma_start(a[:, slot, :], k.d["adjT"][ds(j * P, P), :]).then_inc(loaded[slot], 16)
            for j in range(ring):
                load(j, j, 0)
            with sp.Fori(0, rounds - 1) as r:
                for u in range(ring):
                    load(r * ring + (ring + u), u, r + 1)
            for j in range(ring * rounds, T):
                load(j, j % ring, 0)

        @block.gpsimd
        def _(pool):
            def pick(j, slot, before):
                if not isinstance(j, int) or j >= ring:
                    pool.wait_ge(used, j - (ring - 1))
                nc.gpsimd.tensor_copy(v[:, slot, :], source[:, ds(j, 1), :].rearrange("p o c -> p (o c)")
                                      ).then_inc(picked, 1)
            for j in range(ring):
                pick(j, j, 0)
            with pool.Fori(0, rounds - 1) as r:
                for u in range(ring):
                    pick(r * ring + (ring + u), u, r + 1)
            for j in range(ring * rounds, T):
                pick(j, j % ring, 0)

        @block.tensor
        def _(pe):
            def tile(j, slot, before):
                pe.wait_ge(loaded[slot], (before + 1) * 16)
                pe.wait_ge(picked, j + 1)
                for b, c, w in BANKS:
                    last = nc.tensor.matmul(k.psf[:, c:c + w], v[:, slot, :], a[:, slot, c:c + w],
                                            start=isinstance(j, int) and j == 0, stop=False,
                                            skip_group_check=True)
                last.then_inc(used, 1)
            steps(pe, tile)


def load_constants(k, c):
    nc, ctx = k.nc, ExitStack()
    ring = 4
    with ctx:
        a = k.sb("degree_rows", [P, ring, NP], ctx=ctx)
        below = k.sb("degree_below", [P, T], ctx=ctx)
        below_junk = k.sb("degree_below_junk", [P, ring, NP], BF16, ctx=ctx)
        most = k.sb("degree_most", [P, 1], ctx=ctx)
        most_all = k.sb("degree_most_all", [P, 1], ctx=ctx)
        negatives, most_ready, most_spread = (k.sem(n, ctx) for n in ("negatives", "most_ready", "most_spread"))
        arrived = k.sem("constants_arrived", ctx)
        loaded = [k.sem(f"rows_loaded{u}", ctx) for u in range(ring)]
        zeroed, ident_ready, blocks_zero, summed, own = (
            k.sem(n, ctx) for n in ("ident_zeroed", "ident_ready", "blocks_zero", "summed", "deg_dve"))
        block = ctx.enter_context(nc.Block())
        d = k.d
        first, rest = T % ring, T // ring

        @block.scalar
        def _(act):
            pairs = [(k.x[:, :, :], d["x"]), (k.diag[:, :], d["diag"])]
            pairs += [(c[n][:], d[n]) for n in ("w0T", "w1", "w1T")]
            pairs += [(c["b0"][:], d["b0"].to_broadcast([P, P]))]
            for dst, src in pairs:
                act.dma_start(dst, src).then_inc(arrived, 16)
            act.wait_ge(blocks_zero, 1)
            for s, name in enumerate(("a_l", "a_r")):
                for h in range(L1_HEADS):
                    at = slice(h * L1_D, (h + 1) * L1_D)
                    act.dma_start(c["a_blocks"][at, s * L1_HEADS + h:s * L1_HEADS + h + 1],
                                  d[name][at, :]).then_inc(arrived, 16)
            def find_negatives(t, u, turn):
                act.wait_ge(loaded[u], (turn + 1) * 16)
                nc.scalar.activation(below_junk[:, u, :], a[:, u, :], ACT.Relu, scale=-1.0,
                                     accum_out=below[:, ds(t, 1)]).then_inc(negatives, 1)
            with act.Fori(0, rest) as r:
                for u in range(ring):
                    find_negatives(r * ring + u, u, r)
            for t in range(rest * ring, T):
                find_negatives(t, t % ring, t // ring)
            act.wait_ge(arrived, 16 * (len(pairs) + 2 * L1_HEADS))

        @block.gpsimd
        def _(pool):
            nc.gpsimd.memset(c["a_blocks"][:], 0.0).then_inc(blocks_zero, 1)
            nc.gpsimd.memset(k.ident[:], 0.0).then_inc(zeroed, 1)
            pool.wait_ge(zeroed, 1)
            nc.gpsimd.affine_select(out=k.ident[:], in_=k.ident[:], compare_op=ALU.not_equal, fill=1.0,
                                    base=0, pattern=[[-1, P]], channel_multiplier=1).then_inc(ident_ready, 1)
            pool.wait_ge(ident_ready, 1)
            pool.wait_ge(most_ready, 1)
            nc.gpsimd.partition_all_reduce(most_all[:, :], most[:, :], P, bass.bass_isa.ReduceOp.max
                                           ).then_inc(most_spread, 1)

        @block.sync
        def _(sp):
            for u in range(ring):
                sp.dma_start(a[:, u, :], d["adj"][u * P:(u + 1) * P, :]).then_inc(loaded[u], 16)
            with sp.Fori(1, rest) as r:
                for u in range(ring):
                    sp.wait_ge(summed, r * ring + (u - ring + 1))
                    sp.wait_ge(negatives, r * ring + (u - ring + 1))
                    sp.dma_start(a[:, u, :], d["adj"][ds((r * ring + u) * P, P), :]).then_inc(loaded[u], 16)
            for t in range(rest * ring, T):
                sp.wait_ge(summed, t - ring + 1)
                sp.wait_ge(negatives, t - ring + 1)
                sp.dma_start(a[:, t % ring, :], d["adj"][t * P:(t + 1) * P, :]).then_inc(loaded[t % ring], 16)

        @block.vector
        def _(dve):
            def add_up(t, u, turn):
                dve.wait_ge(loaded[u], (turn + 1) * 16)
                nc.vector.reduce_sum(k.deg[:, ds(t, 1)], a[:, u, :], X).then_inc(summed, 1)
            with dve.Fori(0, rest) as r:
                for u in range(ring):
                    add_up(r * ring + u, u, r)
            for t in range(rest * ring, T):
                add_up(t, t % ring, t // ring)
            dve.wait_ge(negatives, T)
            nc.vector.reduce_max(most[:, :], below[:, :], X).then_inc(most_ready, 1)
            dve.wait_ge(most_spread, 1)
            nc.vector.tensor_scalar(k.signed[:, :], most_all[:, :], 0.0, None, ALU.is_gt)


def late_weights(k, c):
    nc, d = k.nc, k.d
    rows = dict(ebih=3 * P, ebhh=3 * P, nbih=3 * P, nbhh=3 * P, ln_g=P, ln_b=P)
    shapes = dict(gat_w=(P, L2_HEADS * P), gat_wT=(P, L2_HEADS * P), gat_a=(P, 2 * L2_HEADS), ewihT=(P, 3 * P),
                  ewhhT=(P, 3 * P), nwihT=(P, 3 * P), nwhhT=(P, 3 * P), l3w1T=(P, D_ATTN), l3w2T=(D_ATTN, D_ATTN),
                  l3w3T=(P, D_ATTN), u1T=(P, STEPS * P), u2T=(P, STEPS * P), **{n: (P, w) for n, w in rows.items()})
    c.update((n, k.sb(n + "_sb", list(s))) for n, s in shapes.items())
    with ExitStack() as ctx:
        arrived = k.sem("late_weights", ctx)
        block = ctx.enter_context(nc.Block())

        @block.sync
        def _(sp):
            for n in shapes:
                source = d[n].to_broadcast([P, rows[n]]) if n in rows else d[n]
                sp.dma_start(c[n][:], source).then_inc(arrived, 16)
            sp.wait_ge(arrived, 16 * len(shapes))


def layer0(k, c):
    nc, ctx = k.nc, ExitStack()
    with ctx:
        y = k.sb("l0_source", [P, T, P], ctx=ctx)
        dinv = k.sb("dinv", [P, T], ctx=ctx)
        with ExitStack() as inner:
            dp, root, own = (k.sem(n, inner) for n in ("l0_deg", "l0_root", "l0_own"))
            block = inner.enter_context(nc.Block())

            @block.vector
            def _(dve):
                link = Chain(dve, own)
                nc.vector.tensor_scalar(k.s1[:, :], k.deg[:, :], 1e-9, None, ADD).then_inc(dp, 1)
                dve.wait_ge(dp, 1)
                dve.wait_ge(root, 1)
                link(nc.vector.reciprocal(k.s3[:, :], k.s2[:, :]))
                link(nc.vector.tensor_tensor(k.s3[:, :], k.s3[:, :], k.s1[:, :], MUL))
                link(nc.vector.tensor_tensor(k.s3[:, :], k.s3[:, :], k.s2[:, :], ADD))
                link(nc.vector.tensor_scalar(k.s3[:, :], k.s3[:, :], 0.5, None, MUL))
                link(nc.vector.reciprocal(dinv[:, :], k.s3[:, :]))
                link(nc.vector.tensor_tensor(y[:, :, :], k.h[:, :, :], bcast(dinv[:, :], P), MUL))

            @block.scalar
            def _(act):
                act.wait_ge(dp, 1)
                nc.scalar.activation(k.s2[:, :], k.s1[:, :], ACT.Sqrt).then_inc(root, 1)
        propagate(k, y, "l0")
        agg = k.sb("l0_agg", [P, NP], ctx=ctx)
        z = k.sb("l0_z", [P, T, P], ctx=ctx)
        with ExitStack() as inner:
            taken_dve, taken_act, made, own = (k.sem(n, inner) for n in ("l0_td", "l0_ta", "l0_made", "l0_dve"))
            block = inner.enter_context(nc.Block())

            @block.scalar
            def _(act):
                for b, col, w in BANKS[1::2]:
                    nc.scalar.copy(agg[:, col:col + w], k.psf[:, col:col + w]).then_inc(taken_act, 1)

            @block.tensor
            def _(pe):
                pe.wait_ge(taken_dve, len(BANKS[0::2]))
                pe.wait_ge(taken_act, len(BANKS[1::2]))
                for b, col, w in BANKS:
                    for t in range(col // P, (col + w) // P):
                        last = nc.tensor.matmul(k.psf[:, t * P:(t + 1) * P], agg[:, t * P:(t + 1) * P],
                                                c["w0T"][:, :], start=True, stop=True)
                    last.then_inc(made, 1)

            @block.vector
            def _(dve):
                link = Chain(dve, own)
                for b, col, w in BANKS[0::2]:
                    nc.vector.tensor_copy(agg[:, col:col + w], k.psf[:, col:col + w]).then_inc(taken_dve, 1)
                for b, col, w in BANKS:
                    dve.wait_ge(made, b + 1)
                    for t in range(col // P, (col + w) // P):
                        ins = nc.vector.scalar_tensor_tensor(z[:, t, :], k.psf[:, t * P:(t + 1) * P],
                                                             dinv[:, t:t + 1], c["b0"][:, :], MUL, ADD)
                        if t == T - 1:
                            link(ins)
                link(nc.vector.scalar_tensor_tensor(k.x[:, :, :], z[:, :, :], 0.0, k.x[:, :, :], MAX, ADD))


def diagonal_block(engine, j, i0, n, spare):
    if isinstance(j, int):
        return (j - i0 if i0 <= j < i0 + n else spare) * P
    inside = (j >= i0) * (j < i0 + n) if i0 else (j < n)
    return engine.snap((inside * (j - i0) + (1 - inside) * spare) * P).with_bounds(min_val=0, max_val=spare * P)


def split_bf16(link, nc, parts, rest):
    for n, part in enumerate(parts):
        link(nc.vector.tensor_copy(part, rest))
        if n < 2:
            link(nc.vector.tensor_tensor(rest, rest, part, SUB))


def layer1(k, c):
    nc, ctx = k.nc, ExitStack()
    H, D = L1_HEADS, L1_D
    GC, MC = 2 * (D + 1), D + 1
    VC = H * (GC + MC)
    with ctx:
        v = k.sb("l1_v", [P, T, 3, VC], BF16, ctx=ctx)
        r_of = k.sb("l1_r", [P, T * H], ctx=ctx)
        a_n = k.sb("l1_a", [P, T, H], ctx=ctx)
        c_n = k.sb("l1_c", [P, T, H], ctx=ctx)
        ub = k.sb("l1_ub", [P, H, P], ctx=ctx)
        with ExitStack() as inner:
            vf = k.sb("l1_vf", [P, T, VC], ctx=inner)
            wh = k.sb("l1_wh", [P, T, P], ctx=inner)
            sc = k.sb("l1_scores", [P, T, 2 * H], ctx=inner)
            u8 = k.sb("l1_u8", [P, 2 * H], ctx=inner)
            rmax = k.sb("l1_rmax", [P, H], ctx=inner)
            rall = k.sb("l1_rall", [P, H], ctx=inner)
            rs = k.sb("l1_rs", [P, T, H], ctx=inner)
            bt = k.sb("l1_bt", [P, T, H], ctx=inner)
            dt = k.sb("l1_dt", [P, T, H], ctx=inner)
            names = ("u_made", "u_taken", "wh_made", "rmax_ready", "rall_ready", "shifted", "tabled",
                     "wh_act", "own")
            u_made, u_taken, wh_made, rmax_ready, rall_ready, shifted, tabled, wh_act, own = (
                k.sem("l1_" + n, inner) for n in names)
            block = inner.enter_context(nc.Block())

            @block.tensor
            def _(pe):
                nc.tensor.matmul(k.ps[:, 7, 0:2 * H], c["w1"][:, :], c["a_blocks"][:, :], start=True,
                                 stop=True).then_inc(u_made, 1)
                for b, col, w in BANKS:
                    for t in range(col // P, (col + w) // P):
                        last = nc.tensor.matmul(k.psf[:, t * P:(t + 1) * P], k.hT[:, t * P:(t + 1) * P],
                                                c["w1T"][:, :], start=True, stop=True)
                    last.then_inc(wh_made, 1)
                pe.wait_ge(u_taken, 1)
                for t in range(T):
                    last = nc.tensor.matmul(k.ps[:, 7, t * 2 * H:(t + 1) * 2 * H], k.hT[:, t * P:(t + 1) * P],
                                            u8[:, :], start=True, stop=True)
                last.then_inc(wh_made, 1)

            @block.scalar
            def _(act):
                for b, col, w in BANKS[1::2]:
                    act.wait_ge(wh_made, b + 1)
                    last = nc.scalar.copy(wh[:, :, :].rearrange("p t c -> p (t c)")[:, col:col + w],
                                          k.psf[:, col:col + w])
                last.then_inc(wh_act, 1)
                act.wait_ge(shifted, 1)
                nc.scalar.activation(bt[:, :, :], rs[:, :, :], ACT.Exp)
                nc.scalar.activation(dt[:, :, :], rs[:, :, :], ACT.Exp, scale=L1_SLOPE).then_inc(tabled, 1)
                act.wait_ge(shifted, 2)
                nc.scalar.activation(a_n[:, :, :], a_n[:, :, :], ACT.Exp)
                nc.scalar.activation(c_n[:, :, :], c_n[:, :, :], ACT.Exp).then_inc(tabled, 1)
                act.wait_ge(tabled, 2)

            @block.gpsimd
            def _(pool):
                pool.wait_ge(rmax_ready, 1)
                nc.gpsimd.partition_all_reduce(rall[:, :], rmax[:, :], P, bass.bass_isa.ReduceOp.max).then_inc(rall_ready, 1)
                pool.wait_ge(rall_ready, 1)

            @block.vector
            def _(dve):
                link = Chain(dve, own)
                dve.wait_ge(u_made, 1)
                nc.vector.tensor_copy(u8[:, :], k.ps[:, 7, 0:2 * H]).then_inc(u_taken, 1)
                dve.wait_ge(u_taken, 1)
                link(nc.vector.tensor_copy(ub[:, :, :], bcast(u8[:, 0:H], P)))
                for b, col, w in BANKS[0::2]:
                    dve.wait_ge(wh_made, b + 1)
                    nc.vector.tensor_copy(wh[:, :, :].rearrange("p t c -> p (t c)")[:, col:col + w],
                                          k.psf[:, col:col + w])
                dve.wait_ge(wh_made, NB + 1)
                link(nc.vector.tensor_copy(sc[:, :, :], k.ps[:, 7, 0:T * 2 * H].rearrange("p (t e) -> p t e", t=T)))
                nc.vector.reduce_max(rmax[:, :], sc[:, :, H:2 * H].rearrange("p t e -> p e t"), X).then_inc(rmax_ready, 1)
                link(nc.vector.tensor_copy(r_of[:, :].rearrange("p (t e) -> p t e", t=T), sc[:, :, H:2 * H]))
                dve.wait_ge(rall_ready, 1)
                top = rall[:, :].unsqueeze(1).to_broadcast([P, T, H])
                nc.vector.tensor_tensor(rs[:, :, :], sc[:, :, H:2 * H], top, SUB).then_inc(shifted, 1)
                link(nc.vector.tensor_tensor(sc[:, :, 0:H], sc[:, :, 0:H], top, ADD))
                link(nc.vector.tensor_scalar(a_n[:, :, :], sc[:, :, 0:H], 1 - L1_SLOPE, 0.0, MUL, MIN))
                nc.vector.tensor_scalar(c_n[:, :, :], sc[:, :, 0:H], L1_SLOPE - 1, 0.0, MUL, MIN).then_inc(shifted, 1)
                dve.wait_ge(tabled, 1)
                dve.wait_ge(wh_act, 1)
                wh4 = wh[:, :, :].rearrange("p t (h d) -> p t h d", h=H)
                vg = vf[:, :, 0:H * GC].rearrange("p t (h d) -> p t h d", h=H)
                vm = vf[:, :, H * GC:VC].rearrange("p t (h d) -> p t h d", h=H)
                wide = lambda ap, n: ap.unsqueeze(3).to_broadcast([P, T, H, n])
                nc.vector.tensor_tensor(vg[:, :, :, 0:D], wh4, wide(bt[:, :, :], D), MUL)
                nc.vector.tensor_copy(vg[:, :, :, D:D + 1], wide(bt[:, :, :], 1))
                nc.vector.tensor_tensor(vm[:, :, :, 0:D], wh4, wide(dt[:, :, :], D), MUL)
                link(nc.vector.tensor_copy(vm[:, :, :, D:MC], wide(dt[:, :, :], 1)))
                link(nc.vector.tensor_scalar(vg[:, :, :, D + 1:GC], vm, -1.0, None, MUL))
                split_bf16(link, nc, [v[:, :, n, :] for n in range(3)], vf[:, :, :])

        lb = k.sb("l1_lb", [P, H, NP], ctx=ctx)
        with ExitStack() as inner:
            made, taken = k.sem("l1_lb_made", inner), k.sem("l1_lb_taken", inner)
            taken_dve = k.sem("l1_lb_taken_dve", inner)
            block = inner.enter_context(nc.Block())

            @block.tensor
            def _(pe):
                for h in range(H):
                    for b, col, w in BANKS:
                        if h:
                            pe.wait_ge(*((taken_dve, (h - 1) * 4 + b // 2 + 1) if b % 2 == 0 else
                                         (taken, (h - 1) * 3 + b // 2 + 1)))
                        nc.tensor.matmul(k.psf[:, col:col + w], ub[:, h, :], k.hT[:, col:col + w], start=True,
                                         stop=True).then_inc(made, 1)

            @block.scalar
            def _(act):
                for h in range(H):
                    for b, col, w in BANKS[1::2]:
                        act.wait_ge(made, h * NB + b + 1)
                        nc.scalar.copy(lb[:, h, col:col + w], k.psf[:, col:col + w]).then_inc(taken, 1)

            @block.vector
            def _(dve):
                for h in range(H):
                    for b, col, w in BANKS[0::2]:
                        dve.wait_ge(made, h * NB + b + 1)
                        nc.vector.tensor_copy(lb[:, h, col:col + w], k.psf[:, col:col + w]).then_inc(taken_dve, 1)

        ring = 2
        assert T % ring == 0
        a = k.sb("l1_adj", [P, ring, (WMAX + 1) * P], ctx=ctx)
        mask = k.sb("l1_mask", [P, ring, WMAX * P], BF16, ctx=ctx)
        unmasked = k.sb("l1_unmasked", [P, ring, WMAX * P], BF16, ctx=ctx)
        sign = k.sb("l1_sign", [P, ring, H, WMAX * P], BF16, ctx=ctx)
        g = k.sb("l1_g", [P, ring, H, WMAX * P], BF16, ctx=ctx)
        zeros = k.sb("l1_zeros", [P, P], BF16, ctx=ctx)
        e = k.h[:, :, :].rearrange("p t c -> p (t c)")[:, 0:WMAX * VC].rearrange("p (i c) -> p i c", i=WMAX)
        t1, t2 = (k.hT[:, n * WMAX * H * MC:(n + 1) * WMAX * H * MC].rearrange("p (i h d) -> p i h d", i=WMAX, h=H)
                  for n in range(2))
        loaded = [k.sem(f"l1_loaded{u}", ctx) for u in range(ring)]
        freed, signs_ready, g_ready, g_free, taken, sums_used, mins, exps, own, init = (
            k.sem("l1_" + n, ctx) for n in ("freed", "signs_ready", "g_ready", "g_free", "taken", "sums_used", "mins",
                                            "exps", "dve", "zeros"))
        block = ctx.enter_context(nc.Block())

        @block.sync
        def _(sp):
            for ic, (i0, n) in enumerate(CHUNKS):
                def load(j, u, g0):
                    if ic or not isinstance(j, int):
                        sp.wait_ge(freed, j + (ic * T - ring + 1))
                    sp.dma_start(a[:, u, 0:n * P], k.d["adjT"][ds(j * P, P), i0 * P:(i0 + n) * P]
                                 ).then_inc(loaded[u], 16)
                for u in range(ring):
                    load(u, u, 0)
                with sp.Fori(1, T // ring) as r:
                    for u in range(ring):
                        load(r * ring + u, u, 0)

        @block.vector
        def _(dve):
            link = Chain(dve, own)
            link(nc.vector.memset(a[:, :, WMAX * P:(WMAX + 1) * P], 0.0))
            nc.vector.memset(zeros[:, :], 0.0).then_inc(init, 1)
            for ic, (i0, n) in enumerate(CHUNKS):
                w = n * P
                with dve.Fori(0, T // ring) as r:
                    link.enter(r, ring)
                    for u in range(ring):
                        j = r * ring + u
                        dve.wait_ge(loaded[u], (r + (ic * (T // ring) + 1)) * 16)
                        own_block = a[:, u, ds(diagonal_block(dve, j, i0, n, WMAX), P)]
                        link(nc.vector.tensor_tensor(own_block, own_block, k.ident[:, :], ADD))
                        dve.wait_ge(g_free, j + (ic * T + 1))
                        nc.vector.tensor_scalar(mask[:, u, 0:w], a[:, u, 0:w], 0.0, None, ALU.is_gt)
                        nc.vector.tensor_scalar(unmasked[:, u, 0:w], a[:, u, 0:w], 0.0, None,
                                                ALU.is_le).then_inc(freed, 1)
                        dve.wait_ge(freed, j + (ic * T + 1))
                        dve.wait_ge(signs_ready, j + (ic * T + 1))
                        nc.vector.tensor_tensor(g[:, u, :, 0:w], sign[:, u, :, 0:w],
                                                unmasked[:, u, 0:w].unsqueeze(1).to_broadcast([P, H, w]), ALU.is_gt
                                                ).then_inc(g_ready, 1)
                link.leave(T // ring)
                dve.wait_ge(taken, ic + 1)
                eg = e[:, 0:n, 0:H * GC].rearrange("p i (h d) -> p i h d", h=H)
                em = e[:, 0:n, H * GC:VC].rearrange("p i (h d) -> p i h d", h=H)
                u1, u2 = t1[:, 0:n], t2[:, 0:n]
                wide = lambda ap, m: ap[:, i0:i0 + n, :].unsqueeze(3).to_broadcast([P, n, H, m])
                link(nc.vector.tensor_tensor(u1, eg[:, :, :, MC:GC], em, ADD))
                link(nc.vector.tensor_tensor(u1, u1, wide(c_n[:, :, :], MC), MUL))
                link(nc.vector.tensor_tensor(u2, eg[:, :, :, 0:MC], wide(a_n[:, :, :], MC), MUL))
                link(nc.vector.tensor_tensor(u1, u1, u2, ADD))
                link(nc.vector.reciprocal(u2[:, :, :, D:MC], u1[:, :, :, D:MC]))
                link(nc.vector.tensor_tensor(u1[:, :, :, 0:D], u1[:, :, :, 0:D],
                                             u2[:, :, :, D:MC].to_broadcast([P, n, H, D]), MUL))
                nc.vector.tensor_scalar(u2[:, :, :, 0:D], u1[:, :, :, 0:D], 0.0, None, MIN).then_inc(mins, 1)
                dve.wait_ge(exps, ic + 1)
                link(nc.vector.tensor_scalar(u1[:, :, :, 0:D], u1[:, :, :, 0:D], 0.0, -1.0, MAX, ADD))
                link(nc.vector.tensor_tensor(u1[:, :, :, 0:D], u1[:, :, :, 0:D], u2[:, :, :, 0:D], ADD))
                xs = k.x[:, i0:i0 + n, :].rearrange("p i (h d) -> p i h d", h=H)
                nc.vector.tensor_tensor(xs, xs, u1[:, :, :, 0:D], ADD).then_inc(sums_used, 1)

        @block.scalar
        def _(act):
            for ic, (i0, n) in enumerate(CHUNKS):
                def signs(j, u):
                    if ic or not isinstance(j, int):
                        act.wait_ge(g_ready, j + (ic * T - ring + 1))
                    for h in range(H):
                        last = nc.scalar.activation(sign[:, u, h, 0:n * P], lb[:, h, i0 * P:(i0 + n) * P], ACT.Sign,
                                                    bias=r_of[:, ds(j * H + h, 1)])
                    last.then_inc(signs_ready, 1)
                for u in range(ring):
                    signs(u, u)
                with act.Fori(1, T // ring) as r:
                    for u in range(ring):
                        signs(r * ring + u, u)
                act.wait_ge(g_free, (ic + 1) * T + ring)
                if ic:
                    act.wait_ge(sums_used, ic)
                for i in range(n):
                    last = nc.scalar.copy(e[:, i, :], k.ps[:, i, 0:VC])
                last.then_inc(taken, 1)
                act.wait_ge(mins, ic + 1)
                nc.scalar.activation(t2[:, 0:n, :, 0:D], t2[:, 0:n, :, 0:D], ACT.Exp).then_inc(exps, 1)

        @block.tensor
        def _(pe):
            pe.wait_ge(init, 1)
            for ic, (i0, n) in enumerate(CHUNKS):
                if ic:
                    pe.wait_ge(taken, ic)
                for i in range(n):
                    ins = nc.tensor.matmul(k.ps[:, i, 0:VC], zeros[:, :], v[:, 0, 0, :], start=True,
                                           stop=False, skip_group_check=True)
                    if ic == 0 and i < ring:
                        ins.then_inc(g_free, 1)
                with pe.Fori(0, T // ring) as r:
                    for u in range(ring):
                        j = r * ring + u
                        pe.wait_ge(g_ready, j + (ic * T + 1))
                        for i in range(n):
                            at = slice(i * P, (i + 1) * P)
                            for m in range(H + 1):
                                cols = slice(m * GC, (m + 1) * GC) if m < H else slice(H * GC, VC)
                                for s in range(3):
                                    last = nc.tensor.matmul(
                                        k.ps[:, i, cols], g[:, u, m, at] if m < H else mask[:, u, at],
                                        v[:, ds(j, 1), s, cols].rearrange("p o c -> p (o c)"),
                                        start=False, stop=False, skip_group_check=True)
                        last.then_inc(g_free, 1)


def halves(i0, n):
    w = n * P // 2
    return [(0, i0 * P, w), (w, i0 * P + w, w)]


def to_features(k, source, dest, who):
    nc = k.nc
    with ExitStack() as ctx:
        turned, taken_dve, taken_act = (k.sem(f"tf_{n}", ctx) for n in ("turned", "taken_dve", "taken_act"))
        block = ctx.enter_context(nc.Block())

        @block.tensor
        def _(pe):
            for b, c, w in BANKS:
                for t in range(c // P, (c + w) // P):
                    last = nc.tensor.transpose(k.psf[:, t * P:(t + 1) * P], source[:, t, :], k.ident[:, :])
                last.then_inc(turned, 1)

        @block.vector
        def _(dve):
            for b, c, w in BANKS[0::2]:
                dve.wait_ge(turned, b + 1)
                nc.vector.tensor_copy(dest[:, c:c + w], k.psf[:, c:c + w]).then_inc(taken_dve, 1)

        @block.scalar
        def _(act):
            for b, c, w in BANKS[1::2]:
                act.wait_ge(turned, b + 1)
                nc.scalar.copy(dest[:, c:c + w], k.psf[:, c:c + w]).then_inc(taken_act, 1)


def spread_rows(k, columns, dest, who):
    nc = k.nc
    heads = dest.shape[1]
    with ExitStack() as ctx:
        made, taken_dve, taken_act = (k.sem(f"sr_{n}", ctx) for n in ("made", "taken_dve", "taken_act"))
        block = ctx.enter_context(nc.Block())

        @block.tensor
        def _(pe):
            for h in range(heads):
                for b, c, w in BANKS:
                    if h and b % 2 == 0:
                        pe.wait_ge(taken_dve, (h - 1) * len(BANKS[0::2]) + b // 2 + 1)
                    elif h:
                        pe.wait_ge(taken_act, (h - 1) * len(BANKS[1::2]) + b // 2 + 1)
                    for t in range(c // P, (c + w) // P):
                        last = nc.tensor.matmul(k.psf[:, t * P:(t + 1) * P], columns(t, h).to_broadcast([P, P]),
                                                k.ident[:, :], start=True, stop=True)
                    last.then_inc(made, 1)

        @block.vector
        def _(dve):
            for h in range(heads):
                for b, c, w in BANKS[0::2]:
                    dve.wait_ge(made, h * NB + b + 1)
                    nc.vector.tensor_copy(dest[:, h, c:c + w], k.psf[:, c:c + w]).then_inc(taken_dve, 1)

        @block.scalar
        def _(act):
            for h in range(heads):
                for b, c, w in BANKS[1::2]:
                    act.wait_ge(made, h * NB + b + 1)
                    nc.scalar.copy(dest[:, h, c:c + w], k.psf[:, c:c + w]).then_inc(taken_act, 1)


def where_signed(k, engine, signed=True):
    flag = engine.value_load(k.signed[0:1, 0:1], min_val=0, max_val=1)
    return engine.If(flag > 0) if signed else engine.If(flag < 1)


def signed_sums(k, hs, not_ident, nsT, spT, smT):
    nc, ctx = k.nc, ExitStack()
    ring = 4
    with ctx:
        a = k.sb("ss_adj", [P, ring, (WMAX + 1) * P], ctx=ctx)
        pos = k.sb("ss_pos", [P, ring, WMAX * P], BF16, ctx=ctx)
        neg = k.sb("ss_neg", [P, ring, WMAX * P], BF16, ctx=ctx)
        hv = k.sb("ss_h", [P, ring, P], ctx=ctx)
        zeros = k.sb("ss_zeros", [P, BANK], BF16, ctx=ctx)
        loaded = [k.sem(f"ss_loaded{u}", ctx) for u in range(ring)]
        ready, free, picked, taken_act, taken_dve, init, cleared = (
            k.sem("ss_" + n, ctx) for n in ("ready", "free", "picked", "taken_act", "taken_dve", "zeros", "cleared"))
        block = ctx.enter_context(nc.Block())

        def tiles_of(engine, ic, body):
            with engine.Fori(0, T // ring) as r:
                for u in range(ring):
                    body(r * ring + u, (ic * T + u) % ring, r + (ic * T + u) // ring)
            for j in range(T // ring * ring, T):
                body(j, (ic * T + j) % ring, (ic * T + j) // ring)

        @block.sync
        def _(sp):
            for ic, (i0, n) in enumerate(CHUNKS):
                def load(j, u, turn):
                    sp.wait_ge(free, j + (ic * T + 1))
                    sp.dma_start(a[:, u, 0:n * P], k.d["adjT"][ds(j * P, P), i0 * P:(i0 + n) * P]
                                 ).then_inc(loaded[u], 16)
                tiles_of(sp, ic, load)

        @block.gpsimd
        def _(pool):
            for ic in range(len(CHUNKS)):
                def pick(j, u, turn):
                    pool.wait_ge(free, j + (ic * T + 1))
                    nc.gpsimd.tensor_copy(hv[:, u, :], k.h[:, ds(j, 1), :].rearrange("p o c -> p (o c)")
                                          ).then_inc(picked, 1)
                tiles_of(pool, ic, pick)

        @block.vector
        def _(dve):
            nc.vector.memset(a[:, :, WMAX * P:(WMAX + 1) * P], 0.0).then_inc(init, 1)
            nc.vector.memset(zeros[:, :], 0.0).then_inc(init, 1)
            dve.wait_ge(init, 2)
            for ic, (i0, n) in enumerate(CHUNKS):
                w = n * P
                def masks(j, u, turn, signed):
                    dve.wait_ge(loaded[u], (turn + 1) * 16)
                    nc.vector.tensor_tensor(
                        *[a[:, u, ds(diagonal_block(dve, j, i0, n, WMAX), P)]] * 2, not_ident[:, :], MUL
                        ).then_inc(cleared, 1)
                    dve.wait_ge(cleared, j + (ic * T + 1))
                    last = nc.vector.tensor_scalar(pos[:, u, 0:w], a[:, u, 0:w], 0.0, None, ALU.is_gt)
                    if signed:
                        last = nc.vector.tensor_scalar(neg[:, u, 0:w], a[:, u, 0:w], 0.0, None, ALU.is_lt)
                    last.then_inc(ready, 1)
                for signed in (True, False):
                    with where_signed(k, dve, signed):
                        tiles_of(dve, ic, lambda j, u, turn: masks(j, u, turn, signed))
                dve.wait_ge(free, (ic + 1) * T + ring)
                for b, (c0, col, hw) in zip((0, 1), halves(i0, n)):
                    nc.vector.tensor_copy(nsT[:, col:col + hw], k.ps[:, b, 0:hw])
                for b, (c0, col, hw) in zip((2,), halves(i0, n)):
                    nc.vector.tensor_copy(spT[:, col:col + hw], k.ps[:, b, 0:hw]).then_inc(taken_dve, 1)

        @block.scalar
        def _(act):
            for ic, (i0, n) in enumerate(CHUNKS):
                act.wait_ge(free, (ic + 1) * T + ring)
                (_, col, hw) = halves(i0, n)[1]
                nc.scalar.copy(spT[:, col:col + hw], k.ps[:, 3, 0:hw])
                for b, (c0, col, hw) in zip((4, 5), halves(i0, n)):
                    last = nc.scalar.copy(smT[:, col:col + hw], k.ps[:, b, 0:hw])
                last.then_inc(taken_act, 1)

        @block.tensor
        def _(pe):
            pe.wait_ge(init, 2)
            for ic, (i0, n) in enumerate(CHUNKS):
                if ic:
                    pe.wait_ge(taken_dve, ic)
                    pe.wait_ge(taken_act, ic)
                for b in range(6):
                    ins = nc.tensor.matmul(k.ps[:, b, :], zeros[:, 0:P], zeros[:, :], start=True, stop=False,
                                           skip_group_check=True)
                    if ic == 0 and b < ring:
                        ins.then_inc(free, 1)
                acc = dict(stop=False, start=False, skip_group_check=True)

                def add_up(j, u, turn, signed):
                    pe.wait_ge(ready, j + (ic * T + 1))
                    pe.wait_ge(picked, j + (ic * T + 1))
                    for b, (c0, _, hw) in enumerate(halves(i0, n)):
                        nc.tensor.matmul(k.ps[:, b, 0:hw], hv[:, u, :], a[:, u, c0:c0 + hw], **acc)
                    for s in range(3):
                        part = hs[:, ds(j, 1), s, :].rearrange("p o c -> p (o c)")
                        for m, mat in enumerate((pos, neg) if signed else (pos,)):
                            for b, (c0, _, hw) in enumerate(halves(i0, n)):
                                last = nc.tensor.matmul(k.ps[:, 2 + 2 * m + b, 0:hw], part,
                                                        mat[:, u, c0:c0 + hw], **acc)
                    last.then_inc(free, 1)
                for signed in (True, False):
                    with where_signed(k, pe, signed):
                        tiles_of(pe, ic, lambda j, u, turn: add_up(j, u, turn, signed))


LSE_HALF = 36.0


def attention_logits(k, c, spT, smT, et, tau, top, yt):
    nc, ctx = k.nc, ExitStack()
    H = L2_HEADS
    with ctx:
        r1 = k.sb("al_r1", [P, 2 * H], ctx=ctx)
        r2 = k.sb("al_r2", [P, 2 * H], ctx=ctx)
        ends = k.sb("al_ends", [P, 2], ctx=ctx)
        ends_all = k.sb("al_ends_all", [P, 2], ctx=ctx)
        rtau = k.sb("al_rtau", [P, 1], ctx=ctx)
        yf = k.sb("al_yf", [P, T, 2 * H], ctx=ctx)
        made, taken, logits, ends_ready, spread, scaled, exped, own = (
            k.sem("al_" + n, ctx) for n in ("made", "taken", "logits", "ends", "spread", "scaled", "exped", "dve"))
        block = ctx.enter_context(nc.Block())

        @block.tensor
        def _(pe):
            for h in range(H):
                last = nc.tensor.matmul(k.ps[:, 7, 2 * h:2 * h + 2], c["gat_wT"][:, h * P:(h + 1) * P],
                                        c["gat_a"][:, 2 * h:2 * h + 2], start=True, stop=True)
            last.then_inc(made, 1)
            pe.wait_ge(taken, 1)
            for t in range(T):
                at = slice(t * P, (t + 1) * P)
                out = k.ps[:, 6, t * 2 * H:(t + 1) * 2 * H]
                nc.tensor.matmul(out, spT[:, at], r1[:, :], start=True, stop=False)
                last = nc.tensor.matmul(out, smT[:, at], r2[:, :], start=False, stop=True)
            last.then_inc(logits, 1)

        @block.vector
        def _(dve):
            link = Chain(dve, own)
            dve.wait_ge(made, 1)
            uv = k.ps[:, 7, 0:2 * H].rearrange("p (h a) -> p a h", a=2)
            nc.vector.tensor_copy(r1[:, :].rearrange("p (a h) -> p a h", a=2), uv)
            nc.vector.tensor_copy(r2[:, 0:H], uv[:, 1, :])
            nc.vector.tensor_copy(r2[:, H:2 * H], uv[:, 0, :]).then_inc(taken, 1)
            dve.wait_ge(logits, 1)
            link(nc.vector.tensor_copy(et[:, :], k.ps[:, 6, 0:T * 2 * H]))
            link(nc.vector.scalar_tensor_tensor(et[:, :], et[:, :], L2_ALPHA, et[:, :], MUL, MAX))
            nc.vector.reduce_max(ends[:, 0:1], et[:, :], X)
            link(nc.vector.tensor_reduce(ends[:, 1:2], et[:, :], X, MIN))
            nc.vector.tensor_scalar(ends[:, 1:2], ends[:, 1:2], -1.0, None, MUL).then_inc(ends_ready, 1)
            dve.wait_ge(spread, 1)
            link(nc.vector.tensor_copy(top[:, :], ends_all[:, 0:1]))
            link(nc.vector.tensor_tensor(tau[:, :], ends_all[:, 0:1], ends_all[:, 1:2], ADD))
            link(nc.vector.tensor_scalar(tau[:, :], tau[:, :], 0.5 / LSE_HALF, 1e-20, MUL, ADD))
            link(nc.vector.reciprocal(rtau[:, :], tau[:, :]))
            link(nc.vector.tensor_scalar(yf[:, :, :].rearrange("p t c -> p (t c)"), et[:, :], top[:, 0:1],
                                         rtau[:, 0:1], SUB, MUL))
            nc.vector.tensor_scalar(yf[:, :, :], yf[:, :, :], LSE_HALF, None, ADD).then_inc(scaled, 1)
            link(nc.vector.tensor_scalar(et[:, :], et[:, :], -1.0, None, MUL))

        @block.gpsimd
        def _(pool):
            pool.wait_ge(ends_ready, 1)
            nc.gpsimd.partition_all_reduce(ends_all[:, :], ends[:, :], P, bass.bass_isa.ReduceOp.max
                                           ).then_inc(spread, 1)

        @block.scalar
        def _(act):
            act.wait_ge(scaled, 1)
            nc.scalar.activation(yt[:, :, :], yf[:, :, :], ACT.Exp).then_inc(exped, 1)


def row_guards(k, not_ident, yt, tau, top, guards):
    nc, ctx = k.nc, ExitStack()
    H, ring = L2_HEADS, 2
    R = T // ring
    with ctx:
        a = k.sb("rg_adj", [P, ring, NP], ctx=ctx)
        pos = k.sb("rg_pos", [P, ring, NP], BF16, ctx=ctx)
        neg = k.sb("rg_neg", [P, ring, NP], BF16, ctx=ctx)
        zeros = k.sb("rg_zeros", [P, P], BF16, ctx=ctx)
        sums = k.sb("rg_sums", [P, T * H], ctx=ctx)
        shift = k.sb("rg_shift", [P, 1], ctx=ctx)
        loaded = [k.sem(f"rg_loaded{u}", ctx) for u in range(ring)]
        ready, free, cleared, clipped, logged, init, own = (
            k.sem("rg_" + n, ctx) for n in ("ready", "free", "cleared", "clipped", "logged", "zeros", "dve"))
        block = ctx.enter_context(nc.Block())

        @block.sync
        def _(sp):
            for u in range(ring):
                sp.dma_start(a[:, u, :], k.d["adjT"][u * P:(u + 1) * P, :]).then_inc(loaded[u], 16)
            with sp.Fori(1, R) as r:
                for u in range(ring):
                    j = r * ring + u
                    sp.wait_ge(ready, j - (ring - 1))
                    sp.dma_start(a[:, u, :], k.d["adjT"][ds(j * P, P), :]).then_inc(loaded[u], 16)

        @block.vector
        def _(dve):
            link = Chain(dve, own)
            nc.vector.memset(zeros[:, :], 0.0).then_inc(init, 1)
            for signed in (True, False):
                with where_signed(k, dve, signed):
                    with dve.Fori(0, R) as r:
                        for u in range(ring):
                            j = r * ring + u
                            dve.wait_ge(loaded[u], (r + 1) * 16)
                            own_block = a[:, u, ds(j * P, P)]
                            nc.vector.tensor_tensor(own_block, own_block, not_ident[:, :], MUL).then_inc(cleared, 1)
                            dve.wait_ge(cleared, j + 1)
                            dve.wait_ge(free, j + 1)
                            last = nc.vector.tensor_scalar(pos[:, u, :], a[:, u, :], 0.0, None, ALU.is_gt)
                            if signed:
                                last = nc.vector.tensor_scalar(neg[:, u, :], a[:, u, :], 0.0, None, ALU.is_lt)
                            last.then_inc(ready, 1)
            dve.wait_ge(free, T + ring)
            nc.vector.tensor_scalar(sums[:, :], k.ps[:, 0, 0:T * H], 1e-19, None, MAX).then_inc(clipped, 1)
            link(nc.vector.scalar_tensor_tensor(shift[:, :], tau[:, :], 0.01 - LSE_HALF, top[:, :], MUL, ADD))
            dve.wait_ge(logged, 1)
            link(nc.vector.tensor_scalar(guards[:, :], sums[:, :], tau[:, 0:1], shift[:, 0:1], MUL, ADD))

        @block.scalar
        def _(act):
            act.wait_ge(clipped, 1)
            nc.scalar.activation(sums[:, :], sums[:, :], ACT.Ln).then_inc(logged, 1)

        @block.tensor
        def _(pe):
            pe.wait_ge(init, 1)
            acc = dict(start=False, stop=False, skip_group_check=True)
            for u in range(ring):
                nc.tensor.matmul(k.ps[:, 0, 0:P], zeros[:, :], zeros[:, :], start=True, stop=False,
                                 skip_group_check=True).then_inc(free, 1)
            for signed in (True, False):
                with where_signed(k, pe, signed):
                    with pe.Fori(0, R) as r:
                        for u in range(ring):
                            j = r * ring + u
                            pe.wait_ge(ready, j + 1)
                            for i in range(T):
                                at = slice(i * P, (i + 1) * P)
                                for m, mat in enumerate((pos, neg) if signed else (pos,)):
                                    last = nc.tensor.matmul(
                                        k.ps[:, 0, i * H:(i + 1) * H], mat[:, u, at],
                                        yt[:, ds(j, 1), m * H:(m + 1) * H].rearrange("p o c -> p (o c)"), **acc)
                            last.then_inc(free, 1)


def signed_attention(k, c, not_ident, neg_et, gb, es):
    nc, ctx = k.nc, ExitStack()
    H, ring = L2_HEADS, 2
    R = T // ring
    signs = ((ALU.is_gt, MAX), (ALU.is_lt, MIN))
    with ctx:
        a = k.sb("sa_adj", [P, ring, (WMAX + 1) * P], ctx=ctx)
        mask = k.sb("sa_mask", [P, ring, WMAX * P], BF16, ctx=ctx)
        q = k.sb("sa_q", [P, ring, H, WMAX * P], ctx=ctx)
        wa = k.sb("sa_wa", [P, ring, H, WMAX * P], ctx=ctx)
        added_up = k.sb("sa_added_up", [P, H, WMAX * P], ctx=ctx)
        hv = k.sb("sa_h", [P, ring, P], ctx=ctx)
        zeros = k.sb("sa_zeros", [P, BANK], BF16, ctx=ctx)
        ones = k.sb("sa_ones", [P, 1], ctx=ctx)
        rden = k.sb("sa_rden", [P, H * WMAX], ctx=ctx)
        numT = k.sb("sa_numT", [P, H, WMAX * P], ctx=ctx)

        class Sems:
            def __init__(self, sign):
                self.loaded = [k.sem(f"sa_loaded{u}_{sign}", ctx) for u in range(ring)]
                self.exped, self.ready, self.free, self.weighed, self.distanced, self.picked, self.added, self.own = (
                    k.sem(f"sa_{n}_{sign}", ctx)
                    for n in ("exped", "ready", "free", "weighed", "distanced", "picked", "added", "dve"))
        sems = [Sems("positive"), Sems("negative")]
        taken_act, taken_dve, projected, summed, init, cleared, reduced = (
            k.sem("sa_" + n, ctx)
            for n in ("taken_act", "taken_dve", "projected", "summed", "zeros", "cleared", "reduced"))
        block = ctx.enter_context(nc.Block())

        def chunk_passes(engine, ic, one_pass):
            one_pass(0, sems[0])
            with where_signed(k, engine):
                for m in sems:
                    engine.wait_ge(m.free, ((ic + 1) * T + ring) * H)
                    engine.wait_ge(m.added, ((ic + 1) * T + ring) * H)
                    if m is sems[0]:
                        one_pass(1, sems[1])

        @block.sync
        def _(sp):
            for ic, (i0, n) in enumerate(CHUNKS):
                def load(s, m):
                    with sp.Fori(0, R) as r:
                        for u in range(ring):
                            j = r * ring + u
                            sp.wait_ge(m.weighed, j + (ic * T + 1))
                            sp.dma_start(a[:, u, 0:n * P], k.d["adjT"][ds(j * P, P), i0 * P:(i0 + n) * P]
                                         ).then_inc(m.loaded[u], 16)
                chunk_passes(sp, ic, load)

        @block.gpsimd
        def _(pool):
            for m in sems:
                nc.gpsimd.memset(hv[:, 0, 0:1], 0.0).then_inc(m.added, ring * H)
                pool.wait_ge(m.added, ring * H)
            for ic, (i0, n) in enumerate(CHUNKS):
                w = n * P
                if ic:
                    pool.wait_ge(taken_dve, ic)
                nc.gpsimd.memset(added_up[:, :, :], 0.0).then_inc(cleared, 1)
                pool.wait_ge(cleared, ic + 1)

                def pick_and_add(s, m):
                    with pool.Fori(0, R) as r:
                        for u in range(ring):
                            j = r * ring + u
                            pool.wait_ge(m.free, j * H + (ic * T + 1) * H)
                            nc.gpsimd.tensor_copy(hv[:, u, :], k.h[:, ds(j, 1), :].rearrange("p o c -> p (o c)")
                                                  ).then_inc(m.picked, 1)
                            for h in range(H):
                                pool.wait_ge(m.added, j * H + (ic * T * H + ring * H + h - 2))
                                pool.wait_ge(m.ready, j * H + (ic * T * H + h + 1))
                                nc.gpsimd.tensor_tensor(added_up[:, h, 0:w], added_up[:, h, 0:w], q[:, u, h, 0:w], ADD
                                                        ).then_inc(m.added, 1)
                chunk_passes(pool, ic, pick_and_add)

        @block.scalar
        def _(act):
            for ic, (i0, n) in enumerate(CHUNKS):
                w = n * P

                def exponentials(s, m):
                    with act.Fori(0, R) as r:
                        for u in range(ring):
                            j = r * ring + u
                            for h in range(H):
                                act.wait_ge(m.added, j * H + (ic * T * H + h + 1))
                                nc.scalar.activation(q[:, u, h, 0:w], gb[:, h, i0 * P:i0 * P + w], ACT.Relu,
                                                     bias=neg_et[:, ds(j * (2 * H) + (s * H + h), 1)]
                                                     ).then_inc(m.distanced, 1)
                            for h in range(H):
                                act.wait_ge(m.distanced, j * H + (ic * T * H + h + 1))
                                nc.scalar.activation(q[:, u, h, 0:w], q[:, u, h, 0:w], ACT.Exp, scale=-1.0
                                                     ).then_inc(m.exped, 1)
                chunk_passes(act, ic, exponentials)
                act.wait_ge(sems[0].free, ((ic + 1) * T + ring) * H)
                if ic:
                    act.wait_ge(projected, ic)
                for h in range(H):
                    for b, (c0, _, hw) in enumerate(halves(i0, n)):
                        last = nc.scalar.copy(numT[:, h, c0:c0 + hw], k.ps[:, 2 * h + b, 0:hw])
                last.then_inc(taken_act, 1)

        @block.vector
        def _(dve):
            nc.vector.memset(ones[:, :], 1.0)
            nc.vector.memset(zeros[:, :], 0.0).then_inc(init, 1)
            nc.vector.memset(a[:, :, WMAX * P:(WMAX + 1) * P], 0.0).then_inc(init, 1)
            dve.wait_ge(init, 2)
            chains = [Chain(dve, m.own) for m in sems]
            epilogue = Chain(dve, k.sem("sa_epilogue", ctx))
            for ic, (i0, n) in enumerate(CHUNKS):
                w = n * P

                def weigh(s, m):
                    compare, keep = signs[s]
                    link = chains[s]
                    with dve.Fori(0, R) as r:
                        link.enter(r, 2 * ring)
                        for u in range(ring):
                            j = r * ring + u
                            dve.wait_ge(m.loaded[u], (r + (ic * R + 1)) * 16)
                            own_block = a[:, u, ds(diagonal_block(dve, j, i0, n, WMAX), P)]
                            link(nc.vector.tensor_tensor(own_block, own_block, not_ident[:, :], MUL))
                            nc.vector.tensor_scalar(mask[:, u, 0:w], a[:, u, 0:w], 0.0, None, compare)
                            link(nc.vector.tensor_scalar(a[:, u, 0:w], a[:, u, 0:w], 0.0, None, keep))
                            for h in range(H):
                                dve.wait_ge(m.exped, j * H + (ic * T * H + h + 1))
                                dve.wait_ge(m.free, j * H + (ic * T * H + h + 1))
                                product = nc.vector.tensor_tensor(wa[:, u, h, 0:w], q[:, u, h, 0:w], a[:, u, 0:w], MUL)
                                if h == H - 1:
                                    product.then_inc(m.weighed, 1)
                                nc.vector.tensor_tensor(q[:, u, h, 0:w], q[:, u, h, 0:w], mask[:, u, 0:w], MUL
                                                        ).then_inc(m.ready, 1)
                    link.leave(R)
                chunk_passes(dve, ic, weigh)
                dve.wait_ge(reduced, ic + 1)
                sums = lambda ap: ap.rearrange("p (h i) -> p h i", h=H)[:, :, 0:n]
                epilogue(nc.vector.tensor_scalar(sums(rden[:, :]), sums(k.ps[:, 6, 0:H * WMAX]), 1e-37, float(H), MAX,
                                                 MUL))
                nc.vector.reciprocal(sums(rden[:, :]), sums(rden[:, :])).then_inc(taken_dve, 1)
                dve.wait_ge(taken_dve, ic + 1)
                dve.wait_ge(projected, ic + 1)
                for h in range(H):
                    for i in range(n):
                        out, term = es[:, i0 + i, :], k.ps[:, i, h * P:(h + 1) * P]
                        scale = rden[:, h * WMAX + i:h * WMAX + i + 1]
                        if h == 0:
                            last = nc.vector.tensor_scalar(out, term, scale, None, MUL)
                        else:
                            last = nc.vector.scalar_tensor_tensor(out, term, scale, out, MUL, ADD)
                    if h < H - 1:
                        epilogue(last)
                last.then_inc(summed, 1)

        @block.tensor
        def _(pe):
            pe.wait_ge(init, 1)
            acc = dict(start=False, stop=False, skip_group_check=True)
            for ic, (i0, n) in enumerate(CHUNKS):
                if ic:
                    pe.wait_ge(summed, ic)
                for b in range(6):
                    ins = nc.tensor.matmul(k.ps[:, b, :], zeros[:, 0:P], zeros[:, :], start=True, stop=False,
                                           skip_group_check=True)
                    if ic == 0 and b < 2 * ring:
                        ins.then_inc(sems[b // ring].free, H)
                    elif ic == 0 and b < 2 * ring + 2:
                        ins.then_inc(sems[b - 2 * ring].weighed, ring)

                def add_up(s, m):
                    with pe.Fori(0, R) as r:
                        for u in range(ring):
                            j = r * ring + u
                            pe.wait_ge(m.picked, j + (ic * T + 1))
                            for h in range(H):
                                pe.wait_ge(m.ready, j * H + (ic * T * H + h + 1))
                                for b, (c0, _, hw) in enumerate(halves(i0, n)):
                                    last = nc.tensor.matmul(k.ps[:, 2 * h + b, 0:hw], hv[:, u, :], wa[:, u, h, c0:c0 + hw],
                                                     **acc)
                                last.then_inc(m.free, 1)
                chunk_passes(pe, ic, add_up)
                pe.wait_ge(sems[0].added, ((ic + 1) * T + ring) * H)
                for h in range(H):
                    for i in range(n):
                        last = nc.tensor.matmul(k.ps[:, 6, h * WMAX + i:h * WMAX + i + 1],
                                                added_up[:, h, i * P:(i + 1) * P], ones[:, :], start=True, stop=True)
                last.then_inc(reduced, 1)
                pe.wait_ge(taken_act, ic + 1)
                pe.wait_ge(taken_dve, ic + 1)
                for i in range(n):
                    for h in range(H):
                        last = nc.tensor.matmul(k.ps[:, i, h * P:(h + 1) * P], numT[:, h, i * P:(i + 1) * P],
                                                c["gat_w"][:, h * P:(h + 1) * P], start=True, stop=True)
                last.then_inc(projected, 1)


def gru(k, inT, wih, whh, bih, bhh, who):
    nc, ctx = k.nc, ExitStack()
    groups = [(t, min(PER, T - t)) for t in range(0, T, PER)]
    RZ, IN, HN = slice(0, 2 * P), slice(2 * P, 3 * P), slice(3 * P, 4 * P)
    with ctx:
        bias = k.sb(f"gru_bias_{who}", [P, 4 * P], ctx=ctx)
        gate = k.sb(f"gru_gate_{who}", [P, PER, 4 * P], ctx=ctx)
        n_t = k.sb(f"gru_n_{who}", [P, PER, P], ctx=ctx)
        made, added, sig, mixed, tanh, own = (
            k.sem("gru_" + n, ctx) for n in ("made", "added", "sig", "mixed", "tanh", "dve"))
        block = ctx.enter_context(nc.Block())

        @block.tensor
        def _(pe):
            for g, (t0, n) in enumerate(groups):
                if g >= 2:
                    pe.wait_ge(added, g - 1)
                for i in range(n):
                    at, bank = slice((t0 + i) * P, (t0 + i + 1) * P), k.ps[:, (g % 2) * PER + i, :]
                    nc.tensor.matmul(bank[:, RZ], inT[:, at], wih[:, RZ], start=True, stop=False)
                    nc.tensor.matmul(bank[:, RZ], k.hT[:, at], whh[:, RZ], start=False, stop=True)
                    nc.tensor.matmul(bank[:, IN], inT[:, at], wih[:, IN], start=True, stop=True)
                    last = nc.tensor.matmul(bank[:, HN], k.hT[:, at], whh[:, IN], start=True, stop=True)
                last.then_inc(made, 1)

        @block.scalar
        def _(act):
            for g, (t0, n) in enumerate(groups):
                act.wait_ge(added, g + 1)
                nc.scalar.activation(gate[:, 0:n, RZ], gate[:, 0:n, RZ], ACT.Sigmoid).then_inc(sig, 1)
                act.wait_ge(mixed, g + 1)
                nc.scalar.activation(n_t[:, 0:n, :], n_t[:, 0:n, :], ACT.Tanh).then_inc(tanh, 1)

        @block.vector
        def _(dve):
            link = Chain(dve, own)
            nc.vector.tensor_tensor(bias[:, RZ], bih[:, RZ], bhh[:, RZ], ADD)
            nc.vector.tensor_copy(bias[:, IN], bih[:, IN])
            link(nc.vector.tensor_copy(bias[:, HN], bhh[:, IN]))
            for g, (t0, n) in enumerate(groups):
                dve.wait_ge(made, g + 1)
                b0 = (g % 2) * PER
                nc.vector.tensor_tensor(gate[:, 0:n, :], k.ps[:, b0:b0 + n, :],
                                        bias[:, :].unsqueeze(1).to_broadcast([P, n, 4 * P]), ADD).then_inc(added, 1)
                dve.wait_ge(added, g + 1)
                dve.wait_ge(sig, g + 1)
                link(nc.vector.tensor_tensor(n_t[:, 0:n, :], gate[:, 0:n, 0:P], gate[:, 0:n, HN], MUL))
                nc.vector.tensor_tensor(n_t[:, 0:n, :], n_t[:, 0:n, :], gate[:, 0:n, IN], ADD).then_inc(mixed, 1)
                dve.wait_ge(tanh, g + 1)
                link(nc.vector.tensor_tensor(gate[:, 0:n, IN], k.h[:, t0:t0 + n, :], n_t[:, 0:n, :], SUB))
                link(nc.vector.tensor_tensor(gate[:, 0:n, IN], gate[:, 0:n, IN], gate[:, 0:n, P:2 * P], MUL))
                link(nc.vector.tensor_tensor(gate[:, 0:n, IN], gate[:, 0:n, IN], n_t[:, 0:n, :], ADD))
                link(nc.vector.tensor_tensor(gate[:, 0:n, IN], gate[:, 0:n, IN], bcast(k.diag[:, t0:t0 + n], P), MUL))
                link(nc.vector.tensor_tensor(k.x[:, t0:t0 + n, :], k.x[:, t0:t0 + n, :], gate[:, 0:n, IN], ADD))


def layer2(k, c):
    nc = k.nc
    H = L2_HEADS
    with ExitStack() as ctx:
        not_ident = k.sb("not_ident", [P, P], ctx=ctx)
        nsT = k.sb("l2_nsT", [P, NP], ctx=ctx)
        et = k.sb("l2_et", [P, T * 2 * H], ctx=ctx)
        tau = k.sb("l2_tau", [P, 1], ctx=ctx)
        top = k.sb("l2_top", [P, 1], ctx=ctx)
        yt = k.sb("l2_yt", [P, T, 2 * H], BF16, ctx=ctx)
        guards = k.sb("l2_guards", [P, T * H], ctx=ctx)
        with ExitStack() as inner:
            spT = k.sb("l2_spT", [P, NP], ctx=inner)
            smT = k.sb("l2_smT", [P, NP], ctx=inner)
            hs = k.sb("l2_hs", [P, T, 3, P], BF16, ctx=inner)
            with ExitStack() as first:
                rest = k.sb("l2_rest", [P, T, P], ctx=first)
                own = k.sem("l2_dve", first)
                block = first.enter_context(nc.Block())

                @block.vector
                def _(dve):
                    link = Chain(dve, own)
                    link(nc.vector.tensor_scalar(not_ident[:, :], k.ident[:, :], -1.0, 1.0, MUL, ADD))
                    link(nc.vector.tensor_copy(rest[:, :, :], k.h[:, :, :]))
                    split_bf16(link, nc, [hs[:, :, n, :] for n in range(3)], rest[:, :, :])
            signed_sums(k, hs, not_ident, nsT, spT, smT)
            attention_logits(k, c, spT, smT, et, tau, top, yt)
        row_guards(k, not_ident, yt, tau, top, guards)
        es = k.sb("l2_es", [P, T, P], ctx=ctx)
        with ExitStack() as inner:
            gb = k.sb("l2_gb", [P, H, NP], ctx=inner)
            spread_rows(k, lambda t, h: guards[:, t * H + h:t * H + h + 1], gb, "l2")
            signed_attention(k, c, not_ident, et, gb, es)
        gru(k, nsT, c["ewihT"], c["ewhhT"], c["ebih"], c["ebhh"], "edge")
        to_features(k, es, nsT, "l2")
        gru(k, nsT, c["nwihT"], c["nwhhT"], c["nbih"], c["nbhh"], "node")


def queries_and_keys(k, c, xaT, q1T, qT, kT, who):
    nc = k.nc
    with ExitStack() as ctx:
        made, taken_dve, taken_act = (k.sem("qk_" + n, ctx) for n in ("made", "taken_dve", "taken_act"))
        block = ctx.enter_context(nc.Block())
        jobs = [(c["l3w1T"], xaT, q1T), (c["l3w3T"], xaT, kT), (c["l3w2T"], q1T, qT)]
        EVEN, ODD = len(BANKS[0::2]), len(BANKS[1::2])

        @block.tensor
        def _(pe):
            for n, (w, source, _) in enumerate(jobs):
                if n == 2:
                    pe.wait_ge(taken_dve, EVEN)
                    pe.wait_ge(taken_act, ODD)
                for b, col, wd in BANKS:
                    if n and b % 2 == 0:
                        pe.wait_ge(taken_dve, (n - 1) * EVEN + b // 2 + 1)
                    elif n:
                        pe.wait_ge(taken_act, (n - 1) * ODD + b // 2 + 1)
                    nc.tensor.matmul(k.psf[0:D_ATTN, col:col + wd], w[:], source[:, col:col + wd], start=True,
                                     stop=True).then_inc(made, 1)

        @block.vector
        def _(dve):
            for n, (_, _, dest) in enumerate(jobs):
                for b, col, wd in BANKS[0::2]:
                    dve.wait_ge(made, n * NB + b + 1)
                    nc.vector.tensor_copy(dest[:, col:col + wd], k.psf[0:D_ATTN, col:col + wd]).then_inc(taken_dve, 1)

        @block.scalar
        def _(act):
            for n, (_, _, dest) in enumerate(jobs):
                for b, col, wd in BANKS[1::2]:
                    act.wait_ge(made, n * NB + b + 1)
                    nc.scalar.copy(dest[:, col:col + wd], k.psf[0:D_ATTN, col:col + wd]).then_inc(taken_act, 1)


def attend_and_walk(k, qT, kT, xa, out, xf, xf_out, rdeg, u1T, z, rounds, who):
    nc, ctx = k.nc, ExitStack()
    from math import exp
    half_range = [SEARCH_SPAN / 2 ** (n + 1) for n in range(ALL_ROUNDS + 1)]
    groups = [(g, g * PER, min(PER, T - g * PER)) for g in range(NB)]
    LB, WB, TB, OB = 0, 3, 4, 6
    AGG, BY_U1, TURNED_BACK = (slice(n * P, (n + 1) * P) for n in range(3))
    SLOTS, PAIRS = 4, T // 2
    ROUNDS, SHARED = rounds
    FILL = 1
    MIDWAY = ROUNDS // 2
    TURNED_B, WALKED_A, LOGITS_B, TURNED_A, WALKED_B, LOGITS_A = 0, 6, 6, 9, 15, 15
    with ctx:
        p = k.sb(f"ta_p_{who}", [P, SLOTS, NP], ctx=ctx)
        chosen = k.sb(f"ta_chosen_{who}", [P, NODES], ctx=ctx)
        junk = k.sb(f"ta_junk_{who}", [P, NODES], BF16, ctx=ctx)
        pT = k.sb(f"ta_pT_{who}", [P, T, P], ctx=ctx)
        sumsT = k.sb(f"ta_sumsT_{who}", [P, P], ctx=ctx)
        rows_of_adj = k.hT
        qs = k.sb(f"ta_q_{who}", [D_ATTN, 2, P], ctx=ctx)
        small = lambda name, n, dt=F32: k.sb(f"ta_{name}_{who}", [P, n], dt, ctx=ctx)
        top, total, goal, thr, rden = (small(n, SLOTS) for n in ("top", "total", "goal", "thr", "rden"))
        reach, step, least, high, below, need, cut, flag = (
            small(n, 1) for n in ("reach", "step", "least", "high", "below", "need", "cut", "flag"))
        best, sums, sums2 = (small(n, 12) for n in ("best", "sums", "sums2"))
        hits = small("hits", 8)
        flag_row, open_rows = small("flag_row", P), small("open_rows", 1, mybir.dt.int32)
        neg_thr, neg_goal = small("neg_thr", SLOTS), small("neg_goal", SLOTS)
        signs, excess, count, product, neg_reach, pstep, neg_share, halves = (small(n, 1) for n in (
            "signs", "excess", "count", "product", "neg_reach", "pstep", "neg_share", "halves"))
        names = ("padded", "q_ready", "logits", "copied", "topped", "exped", "masked", "turned", "taken", "multiplied",
                 "out_read", "adj_loaded", "looped", "walked", "sums_taken", "walk_made", "walk_read", "own", "own_pool",
                 "passed", "decided", "flagged", "flag_moved", "further")
        (padded, q_ready, logits, copied, topped, exped, masked, turned, taken, multiplied, out_read, adj_loaded,
         looped, walked, sums_taken, walk_made, walk_read, own, own_pool, passed, decided, flagged, flag_moved,
         further) = (k.sem("ta_" + n, ctx) for n in names)
        block = ctx.enter_context(nc.Block())
        LOOPED = (PAIRS - 3) // 2
        assert PAIRS == 3 + 2 * LOOPED

        def pairs(engine, body, chain=None, links=0):
            body(0, 0, 0)
            with engine.Fori(0, LOOPED) as n:
                if chain:
                    chain.enter(n, links)
                body(n * 2 + 1, n * 4 + 2, 2)
                body(n * 2 + 2, n * 4 + 4, 0)
            if chain:
                chain.leave(LOOPED)
            body(PAIRS - 2, T - 4, (T - 4) % SLOTS)
            body(PAIRS - 1, T - 2, (T - 2) % SLOTS)

        def has(i):
            return not isinstance(i, int) or 0 <= i < T

        def late(i, first):
            return not isinstance(i, int) or i >= first

        @block.sync
        def _(sp):
            def move_flags(i):
                sp.wait_ge(flagged, i + 1)
                sp.dma_start(flag_row[0:1, :], flag[:, 0:1]).then_inc(flag_moved, 16)

            def load_adj(i):
                sp.dma_start(rows_of_adj[:, :], k.d["adj_tiles"][ds(i * P, P), :]).then_inc(adj_loaded, 16)
            load_adj(0)
            with sp.Fori(0, T - 1) as i:
                move_flags(i)
                sp.wait_ge(walked, i + 1)
                load_adj(i + 1)
            move_flags(T - 1)

        @block.gpsimd
        def _(pool):
            def decide(r, i, s):
                at = slice(s, s + 1)
                pool.sem_clear(own_pool)
                link = Chain(pool, own_pool)
                pool.wait_ge(exped, i + 1)
                link(nc.gpsimd.tensor_tensor(neg_goal[:, at], total[:, at], neg_share[:, :], MUL))
                nc.gpsimd.memset(neg_thr[:, at], -exp(-half_range[0])).then_inc(decided, 1)
                for n in range(SHARED):
                    before = r * (2 * SHARED) - 2 * SHARED + 2 * n
                    pool.wait_ge(passed, before + 1)
                    link(nc.gpsimd.tensor_tensor(count[:, :], signs[:, :], halves[:, :], MUL))
                    link(nc.gpsimd.tensor_scalar(product[:, :], count[:, :], NODES / 2, neg_thr[:, at], ADD, MUL))
                    pool.wait_ge(passed, before + 2)
                    link(nc.gpsimd.tensor_tensor(neg_reach[:, :], product[:, :], excess[:, :], SUB))
                    up, down = exp(half_range[n + 1]), exp(-half_range[n + 1])
                    link(nc.gpsimd.tensor_scalar(pstep[:, :], neg_reach[:, :], neg_goal[:, at], up - down, ALU.is_le,
                                                 MUL))
                    nc.gpsimd.tensor_scalar(neg_thr[:, at], pstep[:, :], down, neg_thr[:, at], ADD, MUL
                                            ).then_inc(decided, 1)

            link = Chain(pool, own_pool)
            link(nc.gpsimd.memset(neg_share[:, :], -TOP_P))
            link(nc.gpsimd.memset(halves[:, :], 0.5))

            def pair(r, a, s):
                if has(a + 2):
                    decide(r + 1, a + 2, (s + 2) % SLOTS)
            pairs(pool, pair)

        @block.tensor
        def _(pe):
            def make_logits(i, slot):
                pe.wait_ge(q_ready, i + 1)
                for b, col, w in BANKS:
                    if b >= 3:
                        pe.wait_ge(copied, i * NB + (b - 2))
                    elif b == 0 and late(i, 1):
                        pe.wait_ge(copied, i * NB)
                    nc.tensor.matmul(k.ps[:, LB + b % 3, 0:w], qs[:, slot % 2, :], kT[:, col:col + w],
                                     start=True, stop=True).then_inc(logits, 1)

            def turn_and_multiply(i, slot):
                pe.wait_ge(masked, i + 1)
                for g, t0, n in groups:
                    if late(i, 1) or g >= 2:
                        pe.wait_ge(taken, i * NB + (g - 1))
                    for t in range(n):
                        last = nc.tensor.transpose(k.ps[:, TB + (slot * NB + g) % 2, t * P:(t + 1) * P],
                                                   p[:, slot, (t0 + t) * P:(t0 + t + 1) * P], k.ident[:, :])
                    last.then_inc(turned, 1)
                if late(i, 2):
                    pe.wait_ge(out_read, i - 1)
                for g, t0, n in groups:
                    pe.wait_ge(taken, i * NB + (g + 1))
                    for j in range(t0, t0 + n):
                        last = nc.tensor.matmul(k.ps[:, OB + slot % 2, 0:P], pT[:, j, :], xa[:, j, :], start=j == 0,
                                                stop=j == T - 1)
                last.then_inc(multiplied, 1)

            def walk(i):
                pe.wait_ge(looped, i + 1)
                if late(i, 1):
                    pe.wait_ge(walk_read, i)
                for j in range(T):
                    last = nc.tensor.matmul(k.ps[:, WB, AGG], xf[:, j, :], rows_of_adj[:, j * P:(j + 1) * P],
                                            start=j == 0, stop=j == T - 1)
                last.then_inc(walked, 1)

            def end_walk(i):
                pe.wait_ge(sums_taken, i + 1)
                last = nc.tensor.matmul(k.ps[:, WB, BY_U1], sumsT[:, :], u1T, start=True, stop=True)
                if xf_out is not None:
                    last = nc.tensor.matmul(k.ps[:, WB, TURNED_BACK], sumsT[:, :], k.ident[:, :], start=True, stop=True)
                last.then_inc(walk_made, 1)

            for i in range(3):
                make_logits(i, i)

            def pair(r, a, s):
                if late(a, 1):
                    turn_and_multiply(a - 1, (s - 1) % SLOTS)
                walk(a)
                if has(a + 3):
                    make_logits(a + 3, (s + 3) % SLOTS)
                end_walk(a)
                turn_and_multiply(a, s)
                walk(a + 1)
                if has(a + 4):
                    make_logits(a + 4, s)
                end_walk(a + 1)
            pairs(pe, pair)
            turn_and_multiply(T - 1, (T - 1) % SLOTS)

        @block.scalar
        def _(act):
            def copy_logits(i, slot, banks=BANKS):
                for b, col, w in banks:
                    act.wait_ge(logits, i * NB + (b + 1))
                    if b == 0 and late(i, SLOTS):
                        act.wait_ge(turned, i * NB - (SLOTS - 1) * NB)
                    w = min(w, NODES - col)
                    nc.scalar.copy(p[:, slot, col:col + w], k.ps[:, LB + b % 3, 0:w]).then_inc(copied, 1)

            def copy_turned(i, slot, some=groups):
                for g, t0, n in some:
                    act.wait_ge(turned, i * NB + (g + 1))
                    if g == 0 and late(i, 1):
                        act.wait_ge(multiplied, i)
                    nc.scalar.copy(pT[:, t0:t0 + n, :].rearrange("p t c -> p (t c)"),
                                   k.ps[:, TB + (slot * NB + g) % 2, 0:n * P]).then_inc(taken, 1)

            def exponentials(i, slot):
                act.wait_ge(topped, i + 1)
                nc.scalar.activation(p[:, slot, 0:NODES], p[:, slot, 0:NODES], ACT.Exp, bias=top[:, slot:slot + 1],
                                     accum_out=total[:, slot:slot + 1]).then_inc(exped, 1)

            def take_sums(i):
                act.wait_ge(walked, i + 1)
                if late(i, 1):
                    act.wait_ge(walk_made, i)
                nc.scalar.copy(sumsT[:, :], k.ps[:, WB, AGG]).then_inc(sums_taken, 1)

            def pick(i, slot):
                nc.scalar.copy(qs[:, slot % 2, :], qT[:, ds(i * P, P)]).then_inc(q_ready, 1)

            pick(0, 0)
            pick(1, 1)
            act.wait_ge(padded, 1)
            copy_logits(0, 0)
            pick(2, 2)
            copy_logits(1, 1)
            exponentials(0, 0)
            copy_logits(2, 2)

            def pair(r, a, s):
                def take_over(step):
                    if 0 <= step - TURNED_B < 4 and late(a, 1):
                        n = 2 * (step - TURNED_B)
                        copy_turned(a - 1, (s - 1) % SLOTS, groups[n:n + 2])
                    if step == WALKED_A:
                        take_sums(a)
                    if 0 <= step - LOGITS_B < 3 and has(a + 3):
                        n = 2 * (step - LOGITS_B) + 1
                        copy_logits(a + 3, (s + 3) % SLOTS, BANKS[n if n > 1 else 0:n + 2])
                    if 0 <= step - TURNED_A < 4:
                        n = 2 * (step - TURNED_A)
                        copy_turned(a, s, groups[n:n + 2])
                    if step == WALKED_B:
                        take_sums(a + 1)
                    if 0 <= step - LOGITS_A < 3 and has(a + 4):
                        n = 2 * (step - LOGITS_A) + 1
                        copy_logits(a + 4, s, BANKS[n if n > 1 else 0:n + 2])

                for o in (3, 4):
                    if has(a + o):
                        pick(a + o, s + o)
                exponentials(a + 1, (s + 1) % SLOTS)
                if has(a + 2):
                    exponentials(a + 2, (s + 2) % SLOTS)
                slot = (s + 2) % SLOTS
                at = slice(slot, slot + 1)
                for n in range(SHARED):
                    if has(a + 2):
                        act.wait_ge(exped, a + 3)
                        if late(r, 1) or n > 0:
                            act.wait_ge(passed, r * (2 * SHARED) + 2 * n)
                        act.wait_ge(decided, r * (SHARED + 1) + (n + 1))
                        nc.scalar.activation(junk[:, :], p[:, slot, 0:NODES], ACT.Sign, bias=neg_thr[:, at],
                                             accum_out=signs[:, 0:1]).then_inc(passed, 1)
                    take_over(2 * n)
                    if has(a + 2):
                        act.wait_ge(passed, r * (2 * SHARED) + (2 * n + 1))
                        nc.scalar.activation(junk[:, :], p[:, slot, 0:NODES], ACT.Relu, bias=neg_thr[:, at],
                                             accum_out=excess[:, 0:1]).then_inc(passed, 1)
                    take_over(2 * n + 1)
            pairs(act, pair)
            copy_turned(T - 1, (T - 1) % SLOTS)

        @block.vector
        def _(dve):
            link = Chain(dve, own)
            nc.vector.memset(p[:, :, NODES:NP], 0.0).then_inc(padded, 1)
            for buffer in (best, sums, sums2):
                link(nc.vector.memset(buffer[:, 0:4], 0.0))

            def largest(i, slot):
                dve.wait_ge(copied, i * NB + NB)
                link(nc.vector.reduce_max(top[:, slot:slot + 1], p[:, slot, 0:NODES], X))
                nc.vector.tensor_scalar(top[:, slot:slot + 1], top[:, slot:slot + 1], -1.0, None, MUL
                                        ).then_inc(topped, 1)

            def search(link, slot, rounds):
                at = slice(slot, slot + 1)
                for n in rounds:
                    link(nc.vector.scalar_tensor_tensor(chosen[:, :], p[:, slot, 0:NODES], thr[:, at],
                                                        p[:, slot, 0:NODES], ALU.is_ge, MUL, accum_out=reach[:, 0:1]))
                    up, down = exp(half_range[n + 1]), exp(-half_range[n + 1])
                    link(nc.vector.tensor_scalar(step[:, :], reach[:, :], goal[:, at], up - down, ALU.is_ge, MUL))
                    link(nc.vector.scalar_tensor_tensor(thr[:, at], step[:, :], down, thr[:, at], ADD, MUL))

            def begin(slot):
                at = slice(slot, slot + 1)
                link(nc.vector.tensor_scalar(goal[:, at], total[:, at], TOP_P, None, MUL))

            def pick_cut(i, slot):
                at = slice(slot, slot + 1)
                link(nc.vector.tensor_scalar(high[:, :], thr[:, at], exp(half_range[ROUNDS]) * (1 + 1e-5), None,
                                             MUL))
                link(nc.vector.scalar_tensor_tensor(chosen[:, :], p[:, slot, 0:NODES], high[:, 0:1],
                                                    p[:, slot, 0:NODES], ALU.is_lt, MUL, accum_out=below[:, 0:1]))
                link.count(nc.vector.scalar_tensor_tensor(need[:, :], below[:, :], total[:, at], goal[:, at], SUB, ADD))
                link(nc.vector.max(out=best[:, 4:12], in_=chosen[:, :]))
                link(nc.vector.tensor_tensor(sums[:, 4:12], best[:, 4:12], best[:, 3:11], ADD))
                link(nc.vector.tensor_tensor(sums2[:, 4:12], sums[:, 4:12], sums[:, 2:10], ADD))
                link(nc.vector.tensor_tensor(sums[:, 4:12], sums2[:, 4:12], sums2[:, 0:8], ADD))
                link(nc.vector.scalar_tensor_tensor(hits[:, :], sums[:, 4:12], need[:, 0:1], best[:, 4:12],
                                                    ALU.is_ge, MUL))
                link(nc.vector.reduce_max(cut[:, :], hits[:, :], X))
                link(nc.vector.tensor_tensor(need[:, :], need[:, :], cut[:, :], MIN))
                nc.vector.tensor_scalar(flag[:, :], need[:, :], 0.0, None, ALU.is_le).then_inc(flagged, 1)

            def go_further(i, slot):
                at = slice(slot, slot + 1)
                dve.wait_ge(flag_moved, i * 16 + 16)
                link(nc.vector.reduce_max(open_rows[0:1, :], flag_row[0:1, :], X))
                nc.vector.tensor_scalar(least[:, :], total[:, at], 1e-12, None, MUL)
                some = dve.value_load(open_rows[0:1, 0:1], min_val=0, max_val=1)
                with dve.If(some > 0):
                    dve.sem_clear(further)
                    chain = Chain(dve, further)
                    search(chain, slot, range(ROUNDS, ALL_ROUNDS))
                    chain(nc.vector.tensor_scalar(cut[:, :], thr[:, at], exp(-half_range[ALL_ROUNDS]), None, MUL))

            def mask(i, slot):
                at = slice(slot, slot + 1)
                nc.vector.scalar_tensor_tensor(p[:, slot, 0:NODES], p[:, slot, 0:NODES], cut[:, 0:1],
                                               p[:, slot, 0:NODES], ALU.is_ge, MUL, accum_out=rden[:, at]
                                               ).then_inc(masked, 1)
                dve.wait_ge(masked, i + 1)
                link(nc.vector.tensor_tensor(rden[:, at], rden[:, at], least[:, :], MAX))
                link(nc.vector.reciprocal(rden[:, at], rden[:, at]))

            def read_out(i, slot):
                dve.wait_ge(multiplied, i + 1)
                nc.vector.tensor_scalar(out[:, ds(i, 1), :].rearrange("p o c -> p (o c)"), k.ps[:, OB + slot % 2, 0:P],
                                        rden[:, slot:slot + 1], None, MUL).then_inc(out_read, 1)

            def add_loops(i):
                dve.wait_ge(adj_loaded, i * 16 + 16)
                own_block = rows_of_adj[:, ds(i * P, P)]
                nc.vector.tensor_tensor(own_block, own_block, k.ident[:, :], ADD).then_inc(looped, 1)

            def read_walk(i):
                dve.wait_ge(walk_made, i + 1)
                flat = lambda buffer: buffer[:, ds(i, 1), :].rearrange("p o c -> p (o c)")
                scale = rdeg[:, ds(i, 1)]
                last = nc.vector.scalar_tensor_tensor(flat(z), k.ps[:, WB, BY_U1], scale, flat(z), MUL, ADD)
                if xf_out is not None:
                    last = nc.vector.tensor_scalar(flat(xf_out), k.ps[:, WB, TURNED_BACK], scale, None, MUL)
                last.then_inc(walk_read, 1)

            largest(0, 0)

            def pair(r, a, s):
                b, sb = a + 1, (s + 1) % SLOTS
                add_loops(a)
                if late(a, 1):
                    dve.wait_ge(decided, r * (SHARED + 1))
                    begin(s)
                    link(nc.vector.tensor_scalar(thr[:, s:s + 1], neg_thr[:, s:s + 1], -1.0, None, MUL))
                    search(link, s, range(SHARED, ROUNDS))
                    read_walk(a - 1)
                else:
                    dve.wait_ge(exped, 1)
                    begin(s)
                    link(nc.vector.memset(thr[:, s:s + 1], exp(-half_range[0])))
                    search(link, s, range(3))
                    largest(1, 1)
                    search(link, s, range(3, 6))
                    largest(2, 2)
                    search(link, s, range(6, ROUNDS))
                pick_cut(a, s)
                dve.wait_ge(exped, b + 1)
                begin(sb)
                link(nc.vector.memset(thr[:, sb:sb + 1], exp(-half_range[0])))
                search(link, sb, range(FILL))
                go_further(a, s)
                mask(a, s)
                if late(a, 1):
                    read_out(a - 1, (s - 1) % SLOTS)
                search(link, sb, range(FILL, MIDWAY))
                read_walk(a)
                add_loops(b)
                if has(a + 3):
                    largest(a + 3, (s + 3) % SLOTS)
                search(link, sb, range(MIDWAY, ROUNDS))
                pick_cut(b, sb)
                read_out(a, s)
                if has(a + 4):
                    largest(a + 4, s)
                go_further(b, sb)
                mask(b, sb)
            A_LINKS = 2 + 3 * (ROUNDS - SHARED)
            BOTH = 10 + 1 + 2
            B_LINKS = 2 + 3 * ROUNDS + 2
            pairs(dve, pair, link, 2 * (A_LINKS + B_LINKS + 2 * BOTH))
            read_walk(T - 1)
            read_out(T - 1, (T - 1) % SLOTS)


def add_product(k, sourceT, w, z, who):
    nc = k.nc
    with ExitStack() as ctx:
        made = k.sem("ap_made", ctx)
        block = ctx.enter_context(nc.Block())

        @block.tensor
        def _(pe):
            for b, col, wd in BANKS:
                for t in range(col // P, (col + wd) // P):
                    last = nc.tensor.matmul(k.psf[:, t * P:(t + 1) * P], sourceT[:, t * P:(t + 1) * P], w, start=True,
                                            stop=True)
                last.then_inc(made, 1)

        @block.vector
        def _(dve):
            for b, col, wd in BANKS:
                dve.wait_ge(made, b + 1)
                zs = z[:, col // P:(col + wd) // P, :]
                nc.vector.tensor_tensor(zs, zs, k.psf[:, col:col + wd].rearrange("p (t c) -> p t c", c=P), ADD)


def layer3(k, c):
    nc = k.nc
    with ExitStack() as ctx:
        z = k.sb("l3_z", [P, T, P], ctx=ctx)
        rdeg = k.sb("l3_rdeg", [P, T], ctx=ctx)
        xf = k.sb("l3_xf", [P, T, P], ctx=ctx)
        xa = k.sb("l3_xa", [P, T, P], ctx=ctx)
        with ExitStack() as inner:
            own = k.sem("l3_own", inner)
            block = inner.enter_context(nc.Block())

            @block.vector
            def _(dve):
                link = Chain(dve, own)
                nc.vector.tensor_copy(z[:, :, :], k.h[:, :, :])
                link(nc.vector.tensor_scalar(rdeg[:, :], k.deg[:, :], 1.0, None, ADD))
                link(nc.vector.reciprocal(rdeg[:, :], rdeg[:, :]))
        assert STEPS == 2
        for n, (old, new, walked, walked_on) in enumerate(((k.h, xa, k.h, xf), (xa, k.h, xf, None))):
            with ExitStack() as inner:
                keys_queries = k.sb(f"l3_keys_queries{n}", [2 * D_ATTN, NP], ctx=inner)
                kT, qT = keys_queries[0:D_ATTN, :], keys_queries[D_ATTN:2 * D_ATTN, :]
                with ExitStack() as first:
                    q1T = k.sb(f"l3_q1T{n}", [D_ATTN, NP], ctx=first)
                    queries_and_keys(k, c, k.hT, q1T, qT, kT, n)
                at = slice(n * P, (n + 1) * P)
                attend_and_walk(k, qT, kT, old, new, walked, walked_on, rdeg, c["u1T"][:, at], z, SEARCH_ROUNDS[n], n)
            to_features(k, new, k.hT, f"l3{n}")
            add_product(k, k.hT, c["u2T"][:, at], z, n)
        layer_norm(k, "l3_out", source=z, affine=(c["ln_g"], c["ln_b"]))


def build(nc, d, out):
    ctx = ExitStack()
    with ctx:
        k = Kernel(nc, ctx, d, out)
        c = {n: k.sb(n + "_sb", list(s)) for n, s in dict(
            w0T=(P, P), w1=(P, P), w1T=(P, P), b0=(P, P), a_blocks=(P, 2 * L1_HEADS)).items()}
        load_constants(k, c)
        layer_norm(k, "l0")
        layer0(k, c)
        layer_norm(k, "l1")
        layer1(k, c)
        clear_semaphores(k)
        late_weights(k, c)
        layer_norm(k, "l2")
        layer2(k, c)
        clear_semaphores(k)
        layer_norm(k, "l3")
        layer3(k, c)
        store(k)


def store(k):
    nc = k.nc
    with ExitStack() as ctx:
        stored = k.sem("stored", ctx)
        block = ctx.enter_context(nc.Block())

        @block.sync
        def _(sp):
            sp.dma_start(k.out, k.x[:, :, :]).then_inc(stored, 16)
            sp.wait_ge(stored, 16)


def kernel(**inputs):
    import numpy as np
    import concourse.bacc as bacc
    from concourse.bass_utils import run_bass_kernel_spmd

    def packed(a):
        return np.ascontiguousarray(a.reshape(T, P, -1).transpose(1, 0, 2))

    g = {n: np.asarray(a) for n, a in inputs.items()}
    pad = NP - NODES
    adj = np.pad(g["adj"], ((0, pad), (0, pad)))
    row = lambda n: np.ascontiguousarray(g[n].reshape(1, -1))
    turn = lambda n: np.ascontiguousarray(g[n].T)
    side = lambda a: np.ascontiguousarray(np.concatenate(list(a), axis=1))
    arrays = dict(
        x=packed(np.pad(g["x"], ((0, pad), (0, 0)))), adj=adj, adjT=np.ascontiguousarray(adj.T),
        adj_tiles=adj.reshape(T, P, T, P).transpose(0, 3, 2, 1).reshape(NP, NP),
        diag=packed(np.diagonal(adj)).reshape(P, T),
        w0T=turn("L0_gnn_W"), b0=row("L0_gnn_b"), w1=g["L1_gnn_W"], w1T=turn("L1_gnn_W"),
        a_l=g["L1_gnn_a_l"].reshape(-1, 1), a_r=g["L1_gnn_a_r"].reshape(-1, 1),
        gat_w=side(g["L2_gnn_gat_W"]), gat_wT=side(g["L2_gnn_gat_W"].transpose(0, 2, 1)),
        gat_a=np.ascontiguousarray(g["L2_gnn_gat_a"].reshape(L2_HEADS, 2, P).transpose(2, 0, 1).reshape(P, -1)),
        ewihT=turn("L2_gnn_edge_Wih"), ewhhT=turn("L2_gnn_edge_Whh"), nwihT=turn("L2_gnn_node_Wih"),
        nwhhT=turn("L2_gnn_node_Whh"), ebih=row("L2_gnn_edge_bih"), ebhh=row("L2_gnn_edge_bhh"),
        nbih=row("L2_gnn_node_bih"), nbhh=row("L2_gnn_node_bhh"), ln_g=row("L3_gnn_ln_g"), ln_b=row("L3_gnn_ln_b"),
        l3w1T=turn("L3_gnn_W1"), l3w2T=turn("L3_gnn_W2"), l3w3T=turn("L3_gnn_W3"),
        u1T=side(g["L3_gnn_U1"].transpose(0, 2, 1)), u2T=side(g["L3_gnn_U2"].transpose(0, 2, 1)))
    arrays = {n: np.ascontiguousarray(a) for n, a in arrays.items()}
    nc = bacc.Bacc("TRN2", target_bir_lowering=False, num_devices=1)
    d = {n: nc.dram_tensor(f"in_{n}", a.shape, mybir.dt.from_np(a.dtype), kind="ExternalInput").ap()
         for n, a in arrays.items()}
    out = nc.dram_tensor("out_x", (P, T, P), F32, kind="ExternalOutput").ap()
    build(nc, d, out)
    r = run_bass_kernel_spmd(nc, [{f"in_{n}": a for n, a in arrays.items()}], core_ids=[0])
    return np.ascontiguousarray(r.results[0]["out_x"].transpose(1, 0, 2).reshape(NP, P)[:NODES])
```
